# Optimizing a Trainium2 kernel written in Bass

```python
import numpy as np
import jax
import jax.numpy as jnp

def _softmax(x, axis=-1):
    return jax.nn.softmax(x, axis=axis)

def _gelu(x):
    return jax.nn.gelu(x, approximate=True)

def _silu(x):
    return jax.nn.silu(x)

def _sigmoid(x):
    return jax.nn.sigmoid(x)

def _layernorm(x, axis=-1, eps=1e-05):
    m = jnp.mean(x, axis=axis, keepdims=True)
    v = jnp.var(x, axis=axis, keepdims=True)
    return (x - m) / jnp.sqrt(v + eps)

def _scatter_add(tgt, idx, src, axis=0):
    return tgt.at[idx].add(src)

def _segment_sum(src, seg, n):
    return jax.ops.segment_sum(src, seg, n)
kernel_name = 'mk_vit_tower_cls_d4_tok_img768_r4_af86bf'

def setup_inputs(seed: int=0):
    np.random.seed(seed)
    _w = jnp.asarray

    def _rec_inputs():
        import jax
        import jax.numpy as jnp
        _rk = jax.random.key(seed)
        x = -0.00040386 + 0.999972 * jax.random.normal(jax.random.fold_in(_rk, 1), (64, 64, 64, 3), jnp.float32)
        cls_tok = 0.02 * jax.random.normal(jax.random.fold_in(_rk, 5), (1, 1, 192), jnp.float32)
        return (x, cls_tok)
    x, cls_tok = _rec_inputs()

    def _L0_tok_setup():
        import jax, jax.numpy as jnp
        import numpy as np
        IMG = 64
        PATCH = 16
        C = 3
        D = 192
        NP_ = (IMG // PATCH) ** 2
        B = 64

        def _patchify(x):
            Bn, H, Wd, Cn = x.shape
            hp, wp = (H // PATCH, Wd // PATCH)
            x = x.reshape(Bn, hp, PATCH, wp, PATCH, Cn)
            x = x.transpose(0, 1, 3, 2, 4, 5)
            return x.reshape(Bn, hp * wp, PATCH * PATCH * Cn)
        key = jax.random.key(seed)
        k1, k2, k3 = jax.random.split(key, 3)
        x = jax.random.normal(k1, (B, IMG, IMG, C), dtype=jnp.float32)
        patch_dim = C * PATCH * PATCH
        W = jax.random.normal(k2, (patch_dim, D), dtype=jnp.float32) / np.sqrt(patch_dim)
        b = jnp.zeros((D,), dtype=jnp.float32)
        pos_emb = jax.random.normal(k3, (NP_, D), dtype=jnp.float32) * 0.02
        return {'x': x, 'W': W, 'b': b, 'pos_emb': pos_emb}
    _L0_tok_all = _L0_tok_setup()
    _L0_tok_in = {k: v for k, v in _L0_tok_all.items() if k in ('W', 'b', 'pos_emb')}
    del _L0_tok_all

    def _L0_attn_setup():
        import jax, jax.numpy as jnp
        import numpy as np
        import math
        DIM = 192
        NUM_HEADS = 12
        HEAD_DIM = DIM // NUM_HEADS
        EPS = 1e-06

        def rms_norm(x, w):
            xf = x.astype(jnp.float32)
            var = jnp.mean(xf * xf, axis=-1, keepdims=True)
            return (xf * jax.lax.rsqrt(var + EPS) * w).astype(x.dtype)
        key = jax.random.key(seed)
        ks = jax.random.split(key, 6)
        B, N, C = (4, 512, DIM)
        return {'x': jax.random.normal(ks[0], (B, N, C), dtype=jnp.float32), 'qkv_w': jax.random.normal(ks[1], (3 * C, C), dtype=jnp.float32) * C ** (-0.5), 'qkv_b': jax.random.normal(ks[2], (3 * C,), dtype=jnp.float32) * 0.02, 'proj_w': jax.random.normal(ks[3], (C, C), dtype=jnp.float32) * C ** (-0.5), 'proj_b': jax.random.normal(ks[4], (C,), dtype=jnp.float32) * 0.02, 'q_norm_w': jnp.ones((HEAD_DIM,), dtype=jnp.float32), 'k_norm_w': jnp.ones((HEAD_DIM,), dtype=jnp.float32)}
    _L0_attn_all = _L0_attn_setup()
    _L0_attn_in = {k: v for k, v in _L0_attn_all.items() if k in ('qkv_w', 'qkv_b', 'proj_w', 'proj_b', 'q_norm_w', 'k_norm_w')}
    del _L0_attn_all

    def _L0_ffn_setup():
        import jax, jax.numpy as jnp
        import numpy as np
        HID = 192
        NQ = 12
        NKV = 3
        HD = 64
        REP = NQ // NKV
        E = 16
        TOPK = 2
        FF = 384
        EPS = 1e-06
        THETA = 10000.0

        def rms_norm(x, w):
            return x / jnp.sqrt(jnp.mean(x * x, axis=-1, keepdims=True) + EPS) * w

        def rope_tables(seq_len):
            inv = 1.0 / THETA ** (jnp.arange(0, HD, 2, dtype=jnp.float32) / HD)
            f = jnp.arange(seq_len, dtype=jnp.float32)[:, None] * inv[None, :]
            return (jnp.cos(f), jnp.sin(f))

        def apply_rope(t, cos, sin):
            B, S, H, _ = t.shape
            tr = t.reshape(B, S, H, HD // 2, 2)
            c = cos[None, :, None, :]
            s = sin[None, :, None, :]
            r0 = tr[..., 0] * c - tr[..., 1] * s
            r1 = tr[..., 0] * s + tr[..., 1] * c
            return jnp.stack([r0, r1], axis=-1).reshape(B, S, H, HD)

        def attention(x, w_qkv, w_out):
            B, S, _ = x.shape
            qkv = x @ w_qkv
            q, k, v = jnp.split(qkv, [NQ * HD, (NQ + NKV) * HD], axis=-1)
            q = q.reshape(B, S, NQ, HD)
            k = k.reshape(B, S, NKV, HD)
            v = v.reshape(B, S, NKV, HD)
            cos, sin = rope_tables(S)
            q = apply_rope(q, cos, sin)
            k = apply_rope(k, cos, sin)
            k = jnp.repeat(k, REP, axis=2)
            v = jnp.repeat(v, REP, axis=2)
            q = q.transpose(0, 2, 1, 3)
            k = k.transpose(0, 2, 1, 3)
            v = v.transpose(0, 2, 1, 3)
            scores = jnp.einsum('bhqd,bhkd->bhqk', q, k) / jnp.sqrt(jnp.float32(HD))
            causal = jnp.tril(jnp.ones((S, S), dtype=bool))
            scores = jnp.where(causal[None, None], scores, jnp.finfo(scores.dtype).min)
            attn = jax.nn.softmax(scores, axis=-1)
            out = jnp.einsum('bhqk,bhkd->bhqd', attn, v)
            out = out.transpose(0, 2, 1, 3).reshape(B, S, NQ * HD)
            return out @ w_out

        def moe_ffn(x2d, w_router, w_gate_up, w_down):
            logits = x2d @ w_router
            probs = jax.nn.softmax(logits, axis=-1)
            vals, idx = jax.lax.top_k(probs, TOPK)
            vals = vals / jnp.sum(vals, axis=-1, keepdims=True)
            combine = jnp.sum(jax.nn.one_hot(idx, E, dtype=x2d.dtype) * vals[..., None], axis=1)
            out = jnp.zeros_like(x2d)
            for e in range(E):
                gu = x2d @ w_gate_up[e]
                gate, up = jnp.split(gu, 2, axis=-1)
                h = jax.nn.silu(gate) * up
                out = out + combine[:, e:e + 1] * (h @ w_down[e])
            return out
        key = jax.random.key(seed)
        ks = jax.random.split(key, 6)
        B, S = (1, 512)
        return {'x': jax.random.normal(ks[0], (B, S, HID), dtype=jnp.float32), 'norm1_w': jnp.ones((HID,), dtype=jnp.float32), 'w_qkv': jax.random.normal(ks[1], (HID, (NQ + 2 * NKV) * HD), dtype=jnp.float32) * 0.02, 'w_out': jax.random.normal(ks[2], (NQ * HD, HID), dtype=jnp.float32) * 0.02, 'norm2_w': jnp.ones((HID,), dtype=jnp.float32), 'w_router': jax.random.normal(ks[3], (HID, E), dtype=jnp.float32) * 0.02, 'w_gate_up': jax.random.normal(ks[4], (E, HID, 2 * FF), dtype=jnp.float32) * 0.02, 'w_down': jax.random.normal(ks[5], (E, FF, HID), dtype=jnp.float32) * 0.02}
    _L0_ffn_all = _L0_ffn_setup()
    _L0_ffn_in = {k: v for k, v in _L0_ffn_all.items() if k in ('norm1_w', 'w_qkv', 'w_out', 'norm2_w', 'w_router', 'w_gate_up', 'w_down')}
    del _L0_ffn_all

    def _L1_attn_setup():
        import jax, jax.numpy as jnp
        import numpy as np
        key = jax.random.key(seed)
        k0, k1, k2, k3, k4 = jax.random.split(key, 5)
        B, L, D, N = (4, 512, 192, 64)
        u = jax.random.normal(k0, (B, L, D), dtype=jnp.float32)
        A_real = -0.5 - 0.5 * jax.random.uniform(k1, (D, N), dtype=jnp.float32)
        A_imag = jax.random.normal(k2, (D, N), dtype=jnp.float32)
        B_mat = jax.random.normal(k3, (D, N), dtype=jnp.float32)
        C_mat = jax.random.normal(k4, (D, N), dtype=jnp.float32)
        log_delta = jnp.full((D,), np.log(0.1), dtype=jnp.float32)
        return {'u': u, 'A_real': A_real, 'A_imag': A_imag, 'B_mat': B_mat, 'C_mat': C_mat, 'log_delta': log_delta}
    _L1_attn_all = _L1_attn_setup()
    _L1_attn_in = {k: v for k, v in _L1_attn_all.items() if k in ('A_real', 'A_imag', 'B_mat', 'C_mat', 'log_delta')}
    del _L1_attn_all

    def _L1_ffn_setup():
        import jax, jax.numpy as jnp
        import numpy as np
        QN, QP = (-8, 7)

        def round_pass(x):
            return x + jax.lax.stop_gradient(jnp.round(x) - x)

        def _quant_act(x, alpha_a):
            a = alpha_a.mean()
            return round_pass(jnp.clip(x / a, QN, QP))

        def _quant_w(w, alpha_w):
            return round_pass(jnp.clip(w / alpha_w[:, None], QN, QP))
        key = jax.random.key(seed)
        ks = jax.random.split(key, 9)
        B, S, D, H = (16, 256, 192, 768)

        def unif(k, shape):
            return jax.random.uniform(k, shape, jnp.float32, 0.02, 0.1)
        return {'x0': jax.random.normal(ks[0], (B, S, D), jnp.float32), 'w1': jax.random.normal(ks[1], (H, D), jnp.float32) * 0.02, 'b1': jax.random.normal(ks[2], (H,), jnp.float32) * 0.02, 'alpha_w1': unif(ks[3], (H,)), 'alpha_a1': unif(ks[4], (D,)), 'w2': jax.random.normal(ks[5], (D, H), jnp.float32) * 0.02, 'b2': jax.random.normal(ks[6], (D,), jnp.float32) * 0.02, 'alpha_w2': unif(ks[7], (D,)), 'alpha_a2': unif(ks[8], (H,))}
    _L1_ffn_all = _L1_ffn_setup()
    _L1_ffn_in = {k: v for k, v in _L1_ffn_all.items() if k in ('w1', 'b1', 'alpha_w1', 'alpha_a1', 'w2', 'b2', 'alpha_w2', 'alpha_a2')}
    del _L1_ffn_all

    def _L2_attn_setup():
        import jax, jax.numpy as jnp
        import numpy as np
        import math
        DIM = 192
        NUM_HEADS = 12

        def _xavier_uniform(key, out_f, in_f):
            a = math.sqrt(6.0 / (in_f + out_f))
            return jax.random.uniform(key, (out_f, in_f), jnp.float32, -a, a)
        key = jax.random.key(seed)
        k_x, k_qw, k_qB, k_pw, k_pB = jax.random.split(key, 5)
        B, N = (16, 256)
        x = jax.random.normal(k_x, (B, N, DIM), jnp.float32)
        qkv_w = _xavier_uniform(k_qw, 3 * DIM, DIM)
        qkv_b = jnp.zeros((3 * DIM,), jnp.float32)
        qkv_B = jax.random.normal(k_qB, (3 * DIM, DIM), jnp.float32) * math.sqrt(1.0 / DIM)
        proj_w = _xavier_uniform(k_pw, DIM, DIM)
        proj_b = jnp.zeros((DIM,), jnp.float32)
        proj_B = jax.random.normal(k_pB, (DIM, DIM), jnp.float32) * math.sqrt(1.0 / DIM)
        return {'x': x, 'qkv_w': qkv_w, 'qkv_b': qkv_b, 'qkv_B': qkv_B, 'proj_w': proj_w, 'proj_b': proj_b, 'proj_B': proj_B}
    _L2_attn_all = _L2_attn_setup()
    _L2_attn_in = {k: v for k, v in _L2_attn_all.items() if k in ('qkv_w', 'qkv_b', 'qkv_B', 'proj_w', 'proj_b', 'proj_B')}
    del _L2_attn_all

    def _L2_ffn_setup():
        import jax, jax.numpy as jnp
        import numpy as np
        GT0 = [[0, 1, 0, 0, 1, 0], [0, 1, 0, 0, 0, 1], [0, 0, 1, 0, 1, 0], [0, 0, 1, 0, 0, 1], [0, 0, 0, 1, 1, 0], [0, 0, 0, 1, 0, 1]]
        NCLS = 6
        K = 1

        def _expert_pairs():
            pairs = []
            for i in range(NCLS):
                p = [(j - 1, k - 1) for j in range(1, 6) for k in range(1, 6) if j != k and GT0[i][j] == 1 and (GT0[i][k] == 1)]
                pairs.append(p)
            return pairs
        PAIRS = _expert_pairs()
        B, P, D, H = (64, 64, 192, 768)

        def _gelu(t):
            return jax.nn.gelu(t, approximate=False)
        key = jax.random.key(seed)
        ks = jax.random.split(key, 8)
        s = 0.02
        x = jax.random.normal(ks[0], (B, NCLS + P, D), dtype=jnp.float32)
        mids = jax.random.randint(ks[1], (B,), 0, 6)
        moe0_W1 = jax.random.normal(ks[2], (D, H), dtype=jnp.float32) * s
        moe0_b1 = jnp.zeros((H,), jnp.float32)
        moe0_W2 = jax.random.normal(ks[3], (H, D), dtype=jnp.float32) * s
        moe0_b2 = jnp.zeros((D,), jnp.float32)
        A1_W = jax.random.normal(ks[4], (5, D, H), dtype=jnp.float32) * s
        A1_b = jnp.zeros((5, H), jnp.float32)
        A2_W = jax.random.normal(ks[5], (5, H, D), dtype=jnp.float32) * s
        A2_b = jnp.zeros((5, D), jnp.float32)
        G_W = jax.random.normal(ks[6], (NCLS, D, 2), dtype=jnp.float32) * s
        return {'x': x, 'moe0_W1': moe0_W1, 'moe0_b1': moe0_b1, 'moe0_W2': moe0_W2, 'moe0_b2': moe0_b2, 'A1_W': A1_W, 'A1_b': A1_b, 'A2_W': A2_W, 'A2_b': A2_b, 'G_W': G_W, 'mids': mids}
    _L2_ffn_all = _L2_ffn_setup()
    _L2_ffn_in = {k: v for k, v in _L2_ffn_all.items() if k in ('moe0_W1', 'moe0_b1', 'moe0_W2', 'moe0_b2', 'A1_W', 'A1_b', 'A2_W', 'A2_b', 'G_W', 'mids')}
    del _L2_ffn_all

    def _L3_attn_setup():
        import jax, jax.numpy as jnp
        import numpy as np
        N_QUBITS = 8
        N_HEADS = 12
        EPS = 1e-08
        key = jax.random.key(seed)
        ks = jax.random.split(key, 8)
        B, S, D = (4, 512, 192)
        scale = 0.02
        return {'x': jax.random.normal(ks[0], (B, S, D), jnp.float32), 'sp_w': jax.random.normal(ks[1], (2 * N_QUBITS, D), jnp.float32) * scale, 'sp_b': jax.random.normal(ks[2], (2 * N_QUBITS,), jnp.float32) * scale, 'in_w': jax.random.normal(ks[3], (3 * D, D), jnp.float32) * scale, 'in_b': jax.random.normal(ks[4], (3 * D,), jnp.float32) * scale, 'out_w': jax.random.normal(ks[5], (D, D), jnp.float32) * scale, 'out_b': jax.random.normal(ks[6], (D,), jnp.float32) * scale, 'qw': jnp.array(0.5, jnp.float32)}
    _L3_attn_all = _L3_attn_setup()
    _L3_attn_in = {k: v for k, v in _L3_attn_all.items() if k in ('sp_w', 'sp_b', 'in_w', 'in_b', 'out_w', 'out_b', 'qw')}
    del _L3_attn_all

    def _L3_ffn_setup():
        import jax, jax.numpy as jnp
        import numpy as np
        B, T, E = (2, 256, 192)
        H = 768
        N_EXP = 4
        key = jax.random.key(seed)
        ks = jax.random.split(key, 8)
        s_e = 1.0 / np.sqrt(E)
        s_h = 1.0 / np.sqrt(H)
        return {'x': jax.random.normal(ks[0], (B, T, E), dtype=jnp.float32), 'Wg': jax.random.uniform(ks[1], (E, N_EXP), minval=-s_e, maxval=s_e, dtype=jnp.float32), 'bg': jax.random.uniform(ks[2], (N_EXP,), minval=-s_e, maxval=s_e, dtype=jnp.float32), 'W1': jax.random.uniform(ks[3], (N_EXP, E, H), minval=-s_e, maxval=s_e, dtype=jnp.float32), 'b1': jax.random.uniform(ks[4], (N_EXP, H), minval=-s_e, maxval=s_e, dtype=jnp.float32), 'W2': jax.random.uniform(ks[5], (N_EXP, H, E), minval=-s_h, maxval=s_h, dtype=jnp.float32), 'b2': jax.random.uniform(ks[6], (N_EXP, E), minval=-s_h, maxval=s_h, dtype=jnp.float32)}
    _L3_ffn_all = _L3_ffn_setup()
    _L3_ffn_in = {k: v for k, v in _L3_ffn_all.items() if k in ('Wg', 'bg', 'W1', 'b1', 'W2', 'b2')}
    del _L3_ffn_all
    return {'x': x, 'cls_tok': cls_tok, 'L0_tok_W': _L0_tok_in['W'], 'L0_tok_b': _L0_tok_in['b'], 'L0_tok_pos_emb': _L0_tok_in['pos_emb'], 'L0_attn_qkv_w': _L0_attn_in['qkv_w'], 'L0_attn_qkv_b': _L0_attn_in['qkv_b'], 'L0_attn_proj_w': _L0_attn_in['proj_w'], 'L0_attn_proj_b': _L0_attn_in['proj_b'], 'L0_attn_q_norm_w': _L0_attn_in['q_norm_w'], 'L0_attn_k_norm_w': _L0_attn_in['k_norm_w'], 'L0_ffn_norm1_w': _L0_ffn_in['norm1_w'], 'L0_ffn_w_qkv': _L0_ffn_in['w_qkv'], 'L0_ffn_w_out': _L0_ffn_in['w_out'], 'L0_ffn_norm2_w': _L0_ffn_in['norm2_w'], 'L0_ffn_w_router': _L0_ffn_in['w_router'], 'L0_ffn_w_gate_up': _L0_ffn_in['w_gate_up'], 'L0_ffn_w_down': _L0_ffn_in['w_down'], 'L1_attn_A_real': _L1_attn_in['A_real'], 'L1_attn_A_imag': _L1_attn_in['A_imag'], 'L1_attn_B_mat': _L1_attn_in['B_mat'], 'L1_attn_C_mat': _L1_attn_in['C_mat'], 'L1_attn_log_delta': _L1_attn_in['log_delta'], 'L1_ffn_w1': _L1_ffn_in['w1'], 'L1_ffn_b1': _L1_ffn_in['b1'], 'L1_ffn_alpha_w1': _L1_ffn_in['alpha_w1'], 'L1_ffn_alpha_a1': _L1_ffn_in['alpha_a1'], 'L1_ffn_w2': _L1_ffn_in['w2'], 'L1_ffn_b2': _L1_ffn_in['b2'], 'L1_ffn_alpha_w2': _L1_ffn_in['alpha_w2'], 'L1_ffn_alpha_a2': _L1_ffn_in['alpha_a2'], 'L2_attn_qkv_w': _L2_attn_in['qkv_w'], 'L2_attn_qkv_b': _L2_attn_in['qkv_b'], 'L2_attn_qkv_B': _L2_attn_in['qkv_B'], 'L2_attn_proj_w': _L2_attn_in['proj_w'], 'L2_attn_proj_b': _L2_attn_in['proj_b'], 'L2_attn_proj_B': _L2_attn_in['proj_B'], 'L2_ffn_moe0_W1': _L2_ffn_in['moe0_W1'], 'L2_ffn_moe0_b1': _L2_ffn_in['moe0_b1'], 'L2_ffn_moe0_W2': _L2_ffn_in['moe0_W2'], 'L2_ffn_moe0_b2': _L2_ffn_in['moe0_b2'], 'L2_ffn_A1_W': _L2_ffn_in['A1_W'], 'L2_ffn_A1_b': _L2_ffn_in['A1_b'], 'L2_ffn_A2_W': _L2_ffn_in['A2_W'], 'L2_ffn_A2_b': _L2_ffn_in['A2_b'], 'L2_ffn_G_W': _L2_ffn_in['G_W'], 'L2_ffn_mids': _L2_ffn_in['mids'], 'L3_attn_sp_w': _L3_attn_in['sp_w'], 'L3_attn_sp_b': _L3_attn_in['sp_b'], 'L3_attn_in_w': _L3_attn_in['in_w'], 'L3_attn_in_b': _L3_attn_in['in_b'], 'L3_attn_out_w': _L3_attn_in['out_w'], 'L3_attn_out_b': _L3_attn_in['out_b'], 'L3_attn_qw': _L3_attn_in['qw'], 'L3_ffn_Wg': _L3_ffn_in['Wg'], 'L3_ffn_bg': _L3_ffn_in['bg'], 'L3_ffn_W1': _L3_ffn_in['W1'], 'L3_ffn_b1': _L3_ffn_in['b1'], 'L3_ffn_W2': _L3_ffn_in['W2'], 'L3_ffn_b2': _L3_ffn_in['b2']}

def reference(x, cls_tok, L0_tok_W, L0_tok_b, L0_tok_pos_emb, L0_attn_qkv_w, L0_attn_qkv_b, L0_attn_proj_w, L0_attn_proj_b, L0_attn_q_norm_w, L0_attn_k_norm_w, L0_ffn_norm1_w, L0_ffn_w_qkv, L0_ffn_w_out, L0_ffn_norm2_w, L0_ffn_w_router, L0_ffn_w_gate_up, L0_ffn_w_down, L1_attn_A_real, L1_attn_A_imag, L1_attn_B_mat, L1_attn_C_mat, L1_attn_log_delta, L1_ffn_w1, L1_ffn_b1, L1_ffn_alpha_w1, L1_ffn_alpha_a1, L1_ffn_w2, L1_ffn_b2, L1_ffn_alpha_w2, L1_ffn_alpha_a2, L2_attn_qkv_w, L2_attn_qkv_b, L2_attn_qkv_B, L2_attn_proj_w, L2_attn_proj_b, L2_attn_proj_B, L2_ffn_moe0_W1, L2_ffn_moe0_b1, L2_ffn_moe0_W2, L2_ffn_moe0_b2, L2_ffn_A1_W, L2_ffn_A1_b, L2_ffn_A2_W, L2_ffn_A2_b, L2_ffn_G_W, L2_ffn_mids, L3_attn_sp_w, L3_attn_sp_b, L3_attn_in_w, L3_attn_in_b, L3_attn_out_w, L3_attn_out_b, L3_attn_qw, L3_ffn_Wg, L3_ffn_bg, L3_ffn_W1, L3_ffn_b1, L3_ffn_W2, L3_ffn_b2):
    import jax
    import jax.numpy as jnp

    def _L0_tok_ref(x, W, b, pos_emb):
        import jax, jax.numpy as jnp
        import numpy as np
        IMG = 64
        PATCH = 16
        C = 3
        D = 192
        NP_ = (IMG // PATCH) ** 2
        B = 64

        def _patchify(x):
            Bn, H, Wd, Cn = x.shape
            hp, wp = (H // PATCH, Wd // PATCH)
            x = x.reshape(Bn, hp, PATCH, wp, PATCH, Cn)
            x = x.transpose(0, 1, 3, 2, 4, 5)
            return x.reshape(Bn, hp * wp, PATCH * PATCH * Cn)
        patches = _patchify(x)
        proj = jnp.einsum('bnd,de->bne', patches, W) + b
        return proj + pos_emb[None, :, :]

    def _L0_attn_ref(x, qkv_w, qkv_b, proj_w, proj_b, q_norm_w, k_norm_w):
        import jax, jax.numpy as jnp
        import numpy as np
        import math
        DIM = 192
        NUM_HEADS = 12
        HEAD_DIM = DIM // NUM_HEADS
        EPS = 1e-06

        def rms_norm(x, w):
            xf = x.astype(jnp.float32)
            var = jnp.mean(xf * xf, axis=-1, keepdims=True)
            return (xf * jax.lax.rsqrt(var + EPS) * w).astype(x.dtype)
        B, N, C = x.shape
        H, D = (NUM_HEADS, C // NUM_HEADS)
        qkv = x @ qkv_w.T + qkv_b
        qkv = qkv.reshape(B, N, 3, H, D).transpose(2, 0, 3, 1, 4)
        q, k, v = (qkv[0], qkv[1], qkv[2])
        q = rms_norm(q, q_norm_w)
        k = rms_norm(k, k_norm_w)
        scale = 1.0 / math.sqrt(D)
        w = jnp.einsum('bhnd,bhmd->bhnm', q.astype(jnp.float32), k.astype(jnp.float32)) * scale
        w = jax.nn.softmax(w, axis=-1).astype(v.dtype)
        out = jnp.einsum('bhnm,bhmd->bhnd', w, v)
        out = out.transpose(0, 2, 1, 3).reshape(B, N, C)
        return out @ proj_w.T + proj_b

    def _L0_ffn_ref(x, norm1_w, w_qkv, w_out, norm2_w, w_router, w_gate_up, w_down):
        import jax, jax.numpy as jnp
        import numpy as np
        HID = 192
        NQ = 12
        NKV = 3
        HD = 64
        REP = NQ // NKV
        E = 16
        TOPK = 2
        FF = 384
        EPS = 1e-06
        THETA = 10000.0

        def rms_norm(x, w):
            return x / jnp.sqrt(jnp.mean(x * x, axis=-1, keepdims=True) + EPS) * w

        def rope_tables(seq_len):
            inv = 1.0 / THETA ** (jnp.arange(0, HD, 2, dtype=jnp.float32) / HD)
            f = jnp.arange(seq_len, dtype=jnp.float32)[:, None] * inv[None, :]
            return (jnp.cos(f), jnp.sin(f))

        def apply_rope(t, cos, sin):
            B, S, H, _ = t.shape
            tr = t.reshape(B, S, H, HD // 2, 2)
            c = cos[None, :, None, :]
            s = sin[None, :, None, :]
            r0 = tr[..., 0] * c - tr[..., 1] * s
            r1 = tr[..., 0] * s + tr[..., 1] * c
            return jnp.stack([r0, r1], axis=-1).reshape(B, S, H, HD)

        def attention(x, w_qkv, w_out):
            B, S, _ = x.shape
            qkv = x @ w_qkv
            q, k, v = jnp.split(qkv, [NQ * HD, (NQ + NKV) * HD], axis=-1)
            q = q.reshape(B, S, NQ, HD)
            k = k.reshape(B, S, NKV, HD)
            v = v.reshape(B, S, NKV, HD)
            cos, sin = rope_tables(S)
            q = apply_rope(q, cos, sin)
            k = apply_rope(k, cos, sin)
            k = jnp.repeat(k, REP, axis=2)
            v = jnp.repeat(v, REP, axis=2)
            q = q.transpose(0, 2, 1, 3)
            k = k.transpose(0, 2, 1, 3)
            v = v.transpose(0, 2, 1, 3)
            scores = jnp.einsum('bhqd,bhkd->bhqk', q, k) / jnp.sqrt(jnp.float32(HD))
            causal = jnp.tril(jnp.ones((S, S), dtype=bool))
            scores = jnp.where(causal[None, None], scores, jnp.finfo(scores.dtype).min)
            attn = jax.nn.softmax(scores, axis=-1)
            out = jnp.einsum('bhqk,bhkd->bhqd', attn, v)
            out = out.transpose(0, 2, 1, 3).reshape(B, S, NQ * HD)
            return out @ w_out

        def moe_ffn(x2d, w_router, w_gate_up, w_down):
            logits = x2d @ w_router
            probs = jax.nn.softmax(logits, axis=-1)
            vals, idx = jax.lax.top_k(probs, TOPK)
            vals = vals / jnp.sum(vals, axis=-1, keepdims=True)
            combine = jnp.sum(jax.nn.one_hot(idx, E, dtype=x2d.dtype) * vals[..., None], axis=1)
            out = jnp.zeros_like(x2d)
            for e in range(E):
                gu = x2d @ w_gate_up[e]
                gate, up = jnp.split(gu, 2, axis=-1)
                h = jax.nn.silu(gate) * up
                out = out + combine[:, e:e + 1] * (h @ w_down[e])
            return out
        B, S, _ = x.shape
        h = x + attention(rms_norm(x, norm1_w), w_qkv, w_out)
        moe_in = rms_norm(h, norm2_w).reshape(B * S, HID)
        out = h + moe_ffn(moe_in, w_router, w_gate_up, w_down).reshape(B, S, HID)
        return out

    def _L1_attn_ref(u, A_real, A_imag, B_mat, C_mat, log_delta):
        import jax, jax.numpy as jnp
        import numpy as np
        Bsz, L, D = u.shape
        delta = jax.nn.softplus(log_delta)
        A = A_real + 1j * A_imag
        dA = delta[:, None] * A
        A_bar = jnp.exp(dA)
        B_bar = (A_bar - 1.0) / A * B_mat
        CB = C_mat.astype(B_bar.dtype) * B_bar
        ell = jnp.arange(L, dtype=jnp.float32)
        P = jnp.exp(dA[:, :, None] * ell[None, None, :])
        K = jnp.einsum('dn,dnl->dl', CB, P).real
        n_fft = 2 * L
        Uf = jnp.fft.rfft(u, n=n_fft, axis=1)
        Kf = jnp.fft.rfft(K, n=n_fft, axis=1)
        y = jnp.fft.irfft(Uf * Kf.T[None, :, :], n=n_fft, axis=1)[:, :L, :]
        return y.astype(u.dtype)

    def _L1_ffn_ref(x0, w1, b1, alpha_w1, alpha_a1, w2, b2, alpha_w2, alpha_a2):
        import jax, jax.numpy as jnp
        import numpy as np
        QN, QP = (-8, 7)

        def round_pass(x):
            return x + jax.lax.stop_gradient(jnp.round(x) - x)

        def _quant_act(x, alpha_a):
            a = alpha_a.mean()
            return round_pass(jnp.clip(x / a, QN, QP))

        def _quant_w(w, alpha_w):
            return round_pass(jnp.clip(w / alpha_w[:, None], QN, QP))
        xq = _quant_act(x0, alpha_a1)
        wq1 = _quant_w(w1, alpha_w1)
        x1 = jnp.einsum('bsd,hd->bsh', xq, wq1)
        x1 = x1 * alpha_w1 * alpha_a1.mean() + b1
        x1 = jax.nn.gelu(x1, approximate=False)
        x1 = jnp.clip(x1, -10.0, 10.0)
        hq = _quant_act(x1, alpha_a2)
        wq2 = _quant_w(w2, alpha_w2)
        x2 = jnp.einsum('bsh,dh->bsd', hq, wq2)
        x2 = x2 * alpha_w2 * alpha_a2.mean() + b2
        return x2

    def _L2_attn_ref(x, qkv_w, qkv_b, qkv_B, proj_w, proj_b, proj_B):
        import jax, jax.numpy as jnp
        import numpy as np
        import math
        DIM = 192
        NUM_HEADS = 12

        def _xavier_uniform(key, out_f, in_f):
            a = math.sqrt(6.0 / (in_f + out_f))
            return jax.random.uniform(key, (out_f, in_f), jnp.float32, -a, a)
        B, N, C = x.shape
        hd = C // NUM_HEADS
        scale = hd ** (-0.5)
        qkv = x @ qkv_w.T + qkv_b
        qkv = qkv.reshape(B, N, 3, NUM_HEADS, hd).transpose(2, 0, 3, 1, 4)
        q, k, v = (qkv[0], qkv[1], qkv[2])
        attn = jnp.einsum('bhnd,bhmd->bhnm', q, k) * scale
        attn = jax.nn.softmax(attn, axis=-1)
        out = jnp.einsum('bhnm,bhmd->bhnd', attn, v)
        out = out.transpose(0, 2, 1, 3).reshape(B, N, C)
        return out @ proj_w.T + proj_b

    def _L2_ffn_ref(x, moe0_W1, moe0_b1, moe0_W2, moe0_b2, A1_W, A1_b, A2_W, A2_b, G_W, mids):
        import jax, jax.numpy as jnp
        import numpy as np
        GT0 = [[0, 1, 0, 0, 1, 0], [0, 1, 0, 0, 0, 1], [0, 0, 1, 0, 1, 0], [0, 0, 1, 0, 0, 1], [0, 0, 0, 1, 1, 0], [0, 0, 0, 1, 0, 1]]
        NCLS = 6
        K = 1

        def _expert_pairs():
            pairs = []
            for i in range(NCLS):
                p = [(j - 1, k - 1) for j in range(1, 6) for k in range(1, 6) if j != k and GT0[i][j] == 1 and (GT0[i][k] == 1)]
                pairs.append(p)
            return pairs
        PAIRS = _expert_pairs()
        B, P, D, H = (64, 64, 192, 768)

        def _gelu(t):
            return jax.nn.gelu(t, approximate=False)
        cls_tokens = x[:, :NCLS]
        patch_tokens = x[:, NCLS:]
        patch_out = _gelu(patch_tokens @ moe0_W1 + moe0_b1) @ moe0_W2 + moe0_b2
        cls_outs = []
        for i in range(NCLS):
            tok = cls_tokens[:, i]
            eouts = [_gelu(tok @ A1_W[a] + A1_b[a]) @ A2_W[c] + A2_b[c] for a, c in PAIRS[i]]
            out = jnp.stack(eouts, axis=-1)
            gate = jax.nn.softmax(tok @ G_W[i], axis=-1)
            thr = jnp.sort(gate, axis=-1)[..., -(K + 1)]
            mask = (gate > thr[..., None]).astype(gate.dtype)
            g = gate * mask
            g = g / jnp.clip(jnp.sum(g, axis=-1, keepdims=True), 1e-06)
            cls_outs.append(jnp.sum(out * g[:, None, :], axis=-1))
        cls_out = jnp.stack(cls_outs, axis=1)
        return jnp.concatenate([cls_out, patch_out], axis=1)

    def _L3_attn_ref(x, sp_w, sp_b, in_w, in_b, out_w, out_b, qw):
        import jax, jax.numpy as jnp
        import numpy as np
        N_QUBITS = 8
        N_HEADS = 12
        EPS = 1e-08
        B, S, D = x.shape
        Q = N_QUBITS
        sp = x @ sp_w.T + sp_b
        re, im = (sp[..., :Q], sp[..., Q:])
        norm = jnp.sqrt(jnp.sum(re * re + im * im, axis=-1, keepdims=True))
        re = re / (norm + EPS)
        im = im / (norm + EPS)
        ov_re = jnp.einsum('bid,bjd->bij', re, re) + jnp.einsum('bid,bjd->bij', im, im)
        ov_im = jnp.einsum('bid,bjd->bij', re, im) - jnp.einsum('bid,bjd->bij', im, re)
        fid = ov_re * ov_re + ov_im * ov_im
        qa = jax.nn.softmax(fid, axis=-1)
        quantum_out = jnp.einsum('bij,bjd->bid', qa, x)
        H, Dh = (N_HEADS, D // N_HEADS)
        qkv = x @ in_w.T + in_b
        q, k, v = jnp.split(qkv, 3, axis=-1)
        q = q.reshape(B, S, H, Dh).transpose(0, 2, 1, 3)
        k = k.reshape(B, S, H, Dh).transpose(0, 2, 1, 3)
        v = v.reshape(B, S, H, Dh).transpose(0, 2, 1, 3)
        scores = jnp.einsum('bhid,bhjd->bhij', q, k) / jnp.sqrt(jnp.asarray(Dh, x.dtype))
        attn = jax.nn.softmax(scores, axis=-1)
        ctx = jnp.einsum('bhij,bhjd->bhid', attn, v)
        ctx = ctx.transpose(0, 2, 1, 3).reshape(B, S, D)
        classical_out = ctx @ out_w.T + out_b
        w = jax.nn.sigmoid(qw)
        return w * quantum_out + (1.0 - w) * classical_out

    def _L3_ffn_ref(x, Wg, bg, W1, b1, W2, b2):
        import jax, jax.numpy as jnp
        import numpy as np
        B, T, E = (2, 256, 192)
        H = 768
        N_EXP = 4
        gate_logits = jnp.einsum('bte,en->btn', x, Wg) + bg
        top = jnp.argmax(gate_logits, axis=-1)
        h = jax.nn.gelu(jnp.einsum('bte,neh->nbth', x, W1) + b1[:, None, None, :], approximate=False)
        y = jnp.einsum('nbth,nhe->nbte', h, W2) + b2[:, None, None, :]
        onehot = jax.nn.one_hot(top, N_EXP, dtype=x.dtype)
        out = jnp.einsum('nbte,btn->bte', y, onehot)
        return out
    h = _L0_tok_ref(x, L0_tok_W, L0_tok_b, L0_tok_pos_emb)
    h = jnp.concatenate([jnp.broadcast_to(cls_tok, (h.shape[0], 1, h.shape[2])), h], axis=1)
    h = h + _L0_attn_ref(_layernorm(h, axis=-1), L0_attn_qkv_w, L0_attn_qkv_b, L0_attn_proj_w, L0_attn_proj_b, L0_attn_q_norm_w, L0_attn_k_norm_w)
    h = h + _L0_ffn_ref(_layernorm(h, axis=-1), L0_ffn_norm1_w, L0_ffn_w_qkv, L0_ffn_w_out, L0_ffn_norm2_w, L0_ffn_w_router, L0_ffn_w_gate_up, L0_ffn_w_down)
    h = h + _L1_attn_ref(_layernorm(h, axis=-1), L1_attn_A_real, L1_attn_A_imag, L1_attn_B_mat, L1_attn_C_mat, L1_attn_log_delta)
    h = h + _L1_ffn_ref(_layernorm(h, axis=-1), L1_ffn_w1, L1_ffn_b1, L1_ffn_alpha_w1, L1_ffn_alpha_a1, L1_ffn_w2, L1_ffn_b2, L1_ffn_alpha_w2, L1_ffn_alpha_a2)
    h = h + _L2_attn_ref(_layernorm(h, axis=-1), L2_attn_qkv_w, L2_attn_qkv_b, L2_attn_qkv_B, L2_attn_proj_w, L2_attn_proj_b, L2_attn_proj_B)
    h = h + _L2_ffn_ref(_layernorm(h, axis=-1), L2_ffn_moe0_W1, L2_ffn_moe0_b1, L2_ffn_moe0_W2, L2_ffn_moe0_b2, L2_ffn_A1_W, L2_ffn_A1_b, L2_ffn_A2_W, L2_ffn_A2_b, L2_ffn_G_W, L2_ffn_mids)
    h = h + _L3_attn_ref(_layernorm(h, axis=-1), L3_attn_sp_w, L3_attn_sp_b, L3_attn_in_w, L3_attn_in_b, L3_attn_out_w, L3_attn_out_b, L3_attn_qw)
    h = h + _L3_ffn_ref(_layernorm(h, axis=-1), L3_ffn_Wg, L3_ffn_bg, L3_ffn_W1, L3_ffn_b1, L3_ffn_W2, L3_ffn_b2)
    return h

_drawn_inputs = setup_inputs


def setup_inputs(seed=0):
    import zlib

    import numpy as np

    out = dict(_drawn_inputs(seed))
    spreads = {'L0_tok_b': (0.0, 0.1),
     'L0_attn_q_norm_w': (1.0, 0.2),
     'L0_attn_k_norm_w': (1.0, 0.2),
     'L0_ffn_norm1_w': (1.0, 0.6),
     'L0_ffn_norm2_w': (1.0, 0.6),
     'L1_attn_log_delta': (-2.3025851249694824, 0.572),
     'L2_attn_qkv_b': (0.0, 0.8),
     'L2_attn_proj_b': (0.0, 0.8),
     'L2_ffn_moe0_b1': (0.0, 2.0),
     'L2_ffn_moe0_b2': (0.0, 0.8),
     'L2_ffn_A1_b': (0.0, 2.0),
     'L2_ffn_A2_b': (0.0, 2.0)}
    factors = {'L0_ffn_w_router': 8.0,
     'L0_ffn_w_gate_up': 8.0,
     'L0_ffn_w_down': 8.0,
     'L1_ffn_w1': 4.338,
     'L1_ffn_b1': 36.116,
     'L1_ffn_alpha_w1': 58.426,
     'L1_ffn_w2': 4.32,
     'L1_ffn_b2': 48.444,
     'L1_ffn_alpha_w2': 18.853,
     'L1_ffn_alpha_a2': 200.0,
     'L2_ffn_A1_W': 3.258,
     'L2_ffn_A2_W': 2.94,
     'L2_ffn_G_W': 2.852,
     'L3_attn_sp_w': 200.0,
     'L3_attn_sp_b': 200.0,
     'L3_attn_in_w': 7.504,
     'L3_attn_in_b': 41.928,
     'L3_attn_out_w': 8.0,
     'L3_attn_out_b': 64.0,
     'L3_ffn_b1': 64.0,
     'L3_ffn_b2': 49.004,
     'L1_attn_A_real': 8.0,
     'L1_attn_A_imag': 2.723,
     'L2_attn_qkv_w': 4.646,
     'L2_attn_proj_w': 4.361,
     'L2_ffn_moe0_W1': 8.0,
     'L2_ffn_moe0_W2': 4.828,
     'L3_ffn_Wg': 4.348,
     'L3_ffn_bg': 8.0,
     'L3_ffn_W1': 5.472,
     'L3_ffn_W2': 4.586}
    for name, (base, spread) in spreads.items():
        noise = np.random.default_rng([zlib.crc32(name.encode()), seed]).standard_normal(out[name].shape)
        drawn = base * np.exp(spread * noise) if base else spread * noise
        out[name] = jnp.asarray(drawn.astype(out[name].dtype))
    for name, factor in factors.items():
        out[name] = (out[name] * factor).astype(out[name].dtype)
    return out
```

```python
from contextlib import ExitStack

import numpy as np

import concourse.bass as bass
from concourse import mybir
from concourse.alu_op_type import AluOpType as ALU

F32 = mybir.dt.float32
BF16 = mybir.dt.bfloat16
ACT = mybir.ActivationFunctionType
AX_X = mybir.AxisListType.X

B = 64
NP = 16
N = NP + 1
T = B * N
D = 192
HD = 96
HN = 12
HW = 16
HH = HN // 2
NC = 4
IC = B // NC
CW = IC * N
GI = 8
GPC = IC // GI
NG = B // GI
GW = GI * N
SLOT = 32
PD = 768
KP = PD // 128
LN_EPS = 1e-5
RMS_EPS = 1e-6
FF = 768
QH = 12
KVH = 3
WD = 64
THETA = 10000.0
QB = 8
QR = 3 * SLOT + N
NE = 16
EF = 384
MASKED = -1e30


class Env:

    def __init__(self, nc, ctx):
        self.nc, self.ctx, self.of_stage = nc, ctx, []

    def sb(self, name, shape, dt=F32):
        return self.ctx.enter_context(self.nc.sbuf_tensor(name, shape, dt))

    def keep_sem(self, name):
        return self.ctx.enter_context(self.nc.semaphore(name))

    def sem(self, name):
        self.of_stage.append(self.nc.alloc_semaphore(name))
        return self.of_stage[-1]

    def end_stage(self):
        self.nc.clear_and_free_semaphores(self.of_stage)
        self.of_stage = []
        self.nc.all_engine_barrier()


def cols(env, name):
    a, n = COLS[name]
    return env.vec[:, a:a + n]


def chunk(ap3, c):
    return ap3[:, :, c * CW:(c + 1) * CW]


class Norm:

    def __init__(self, env, name, x):
        self.env, self.x = env, x
        self.mean_ready = env.sem(name + "_mean_ready")
        self.centred = env.sem(name + "_centred")
        self.squared = env.sem(name + "_squared")
        self.var_ready = env.sem(name + "_var_ready")
        self.log_var = env.sem(name + "_log_var")
        self.rstd_ready = env.sem(name + "_rstd_ready")
        self.ready = env.sem(name + "_x_ready")

    def mean(self, pe, c):
        if c > 0:
            pe.wait_ge(self.log_var, c)
        nc, env = self.env.nc, self.env
        for a in range(2):
            last = nc.tensor.matmul(env.ps[0][0:HD, 0:CW], env.mean_w, chunk(env.h, c)[:, a], start=a == 0, stop=a == 1)
        last.then_inc(self.mean_ready, 1)

    def var(self, pe, c):
        nc, env = self.env.nc, self.env
        pe.wait_ge(self.centred, c + 1)
        pe.wait_ge(self.squared, c + 1)
        for a in range(2):
            last = nc.tensor.matmul(env.ps[0][0:HD, 0:CW], env.mean_w, env.sq[:, c % 2, a], start=a == 0, stop=a == 1)
        last.then_inc(self.var_ready, 1)

    def centre(self, dve, c):
        nc, env = self.env.nc, self.env
        dve.wait_ge(self.mean_ready, c + 1)
        nc.vector.tensor_tensor(chunk(self.x, c), chunk(env.h, c), env.ps[0][0:HD, None, 0:CW].broadcast_to([HD, 2, CW]),
                                ALU.subtract).then_inc(self.centred, 1)

    def square(self, act, c):
        nc, env = self.env.nc, self.env
        act.wait_ge(self.centred, c + 1)
        if c >= 2:
            act.wait_ge(self.var_ready, c - 1)
        nc.scalar.activation(env.sq[:, c % 2], chunk(self.x, c), ACT.Square).then_inc(self.squared, 1)

    def rstd(self, act, c):
        nc, env = self.env.nc, self.env
        act.wait_ge(self.var_ready, c + 1)
        if c >= 2:
            act.wait_ge(self.ready, c - 1)
        nc.scalar.activation(env.rs[:, c % 2], env.ps[0][0:HD, 0:CW], ACT.Ln, bias=env.ln_eps[0:HD, :]).then_inc(self.log_var, 1)
        act.wait_ge(self.log_var, c + 1)
        nc.scalar.activation(env.rs[:, c % 2], env.rs[:, c % 2], ACT.Exp, scale=-0.5).then_inc(self.rstd_ready, 1)

    def scale(self, dve, c):
        nc, env = self.env.nc, self.env
        dve.wait_ge(self.rstd_ready, c + 1)
        nc.vector.tensor_tensor(chunk(self.x, c), chunk(self.x, c), env.rs[:, c % 2, None, :].broadcast_to([HD, 2, CW]),
                                ALU.mult).then_inc(self.ready, 1)


def stage_tokens(env, patches, w, pos):
    nc = env.nc
    with ExitStack() as ctx:
        px = ctx.enter_context(nc.sbuf_tensor("patch_px", [128, NC, KP, IC * NP], F32))
        ws = ctx.enter_context(nc.sbuf_tensor("patch_w", [128, KP, D], F32))
        posb = ctx.enter_context(nc.sbuf_tensor("patch_pos", [HD, 2, NP], F32))
        w_in, pos_in = env.sem("tok_w_in"), env.sem("tok_pos_in")
        px_in = [env.sem(f"tok_px{c}_in") for c in range(NC)]
        posb_ready, embedded, cls_in, placed = (env.sem("tok_" + n) for n in ("posb_ready", "embedded", "cls_placed", "placed"))
        block = ctx.enter_context(nc.Block())

        @block.sync
        def _(sp):
            sp.dma_start(ws[:], w).then_inc(w_in, 16)
            for c in range(NC):
                sp.dma_start(px[:, c], patches[c]).then_inc(px_in[c], 16)

        @block.scalar
        def _(act):
            act.preload_act_table_set("natural_log_exp_and_others")
            act.dma_start(env.vec[:], env.vec_dram).then_inc(env.vec_in, 16)
            act.dma_start(posb[:], pos).then_inc(pos_in, 16)
            act.dma_start(env.con[:], env.con_dram).then_inc(env.con_in, 16)
            act.wait_ge(env.vec_in, 16)
            c3 = cols(env, "cls")[0:HD, :]
            nc.scalar.activation(env.h4[:, :, :, 0], c3[:, :, None].broadcast_to([HD, 2, B]), ACT.Copy).then_inc(cls_in, 1)
            act.wait_ge(cls_in, 1)

        @block.gpsimd
        def _(pool):
            pool.memset(env.ln_eps[:], LN_EPS)
            pool.memset(env.rms_eps[:], RMS_EPS)

        @block.tensor
        def _(pe):
            pe.wait_ge(w_in, 16)
            for c in range(NC):
                pe.wait_ge(px_in[c], 16)
                for m in range(2):
                    for k in range(KP):
                        last = nc.tensor.matmul(env.ps[2 * c + m][0:HD, 0:IC * NP], ws[:, k, m * HD:(m + 1) * HD],
                                                px[:, c, k], start=k == 0, stop=k == KP - 1)
                    last.then_inc(embedded, 1)

        @block.vector
        def _(dve):
            dve.wait_ge(env.vec_in, 16)
            dve.wait_ge(pos_in, 16)
            tb = cols(env, "tok_b")[0:HD, :]
            nc.vector.tensor_tensor(posb[:], posb[:], tb[:, :, None].broadcast_to([HD, 2, NP]), ALU.add).then_inc(posb_ready, 1)
            dve.wait_ge(posb_ready, 1)
            for c in range(NC):
                for m in range(2):
                    dve.wait_ge(embedded, 2 * c + m + 1)
                    src = env.ps[2 * c + m][0:HD, 0:IC * NP].rearrange("p (i n) -> p i n", n=NP)
                    nc.vector.tensor_tensor(env.h4[:, m, c * IC:(c + 1) * IC, 1:N], src,
                                            posb[:, m, None, :].broadcast_to([HD, IC, NP]), ALU.add).then_inc(placed, 1)
            dve.wait_ge(placed, 2 * NC)


def stage_narrow_attention(env, name, dram, rms=False, quantum=False):
    nc = env.nc
    x, ps = env.x, env.ps
    HP = HN + 1 if quantum else HN
    with ExitStack() as ctx:
        def sb(n, shape, dt=F32):
            return ctx.enter_context(nc.sbuf_tensor(name + "_" + n, shape, dt))

        def sem(n):
            return env.sem(name + "_" + n)

        wqkv = sb("wqkv", [HD, 2, 3 * D])
        wo = sb("wo", [HD, 2, D])
        q = sb("q", [HD, 2, 2, CW + SLOT - N])
        k = sb("k", [HD, 2, 2, CW])
        kx = sb("kx", [HD, 2, 2, IC, HH * N])
        vx = sb("vx", [HD, 2, 2, IC, HH * N])
        vt = sb("vt", [HH * N, 2, GI, 2, HD])
        p = sb("p", [128, 2, 2, HP * N])
        pt = sb("pt", [HH * N, 2, 4, 128])
        mx = sb("mx", [128, 2, 2, HP])
        sm = sb("sm", [128, 2, 2, HP])
        cx = sb("cx", [HD, 2, 2, CW])
        w_in, gate_in = sem("w_in"), sem("gate_in")
        ln = Norm(env, name + "_ln", x)
        pad_zero = sem("pad_zero")
        proj = [sem(f"{n}_proj") for n in "qkvo"]
        qk_evicted, k_spread, v_spread = sem("qk_evicted"), sem("k_spread"), sem("v_spread")
        if rms:
            rsq = sb("rsq", [HD, 2, CW])
            rrs = sb("rrs", [HD, 2, CW])
            raw_evicted, head_sq, head_ms, head_log, head_rstd, head_scaled = (
                sem(n) for n in ("raw_evicted", "head_squared", "head_ms", "head_log", "head_rstd", "head_scaled"))
        if quantum:
            wsp = sb("wsp", [HD, 2, 4 * QB])
            st = sb("st", [2 * QB, 2, 2, CW + SLOT - N])
            ssq, srs = sb("ssq", [2 * QB, CW]), sb("srs", [2 * QB, CW])
            osq = sb("osq", [128, 2, 2, 2, N])
            px = sb("px", [128, 2, 2, 4, N])
            xt = sb("xt", [4 * N, 2, 2, 2, HD])
            qt = sb("qt", [4 * N, 2, 2, 128])
            gate = sb("gate", [128, 2])
            gated_b = sb("gated_b", [HD, 2, 2])
            tiny = sb("tiny", [128, 2])
            (s_proj, s_taken, s_squared, s_norm, s_factor, s_scaled, ov_squared, fid_ready, spread, qt_ready, qt_moved, gate_step,
             weighted) = (sem(n) for n in (
                 "s_proj", "s_taken", "s_squared", "s_norm", "s_factor", "s_scaled", "overlap_squared", "fidelity_ready",
                 "q_spread", "qt_ready", "qt_moved", "gate_step", "sm_weighted"))
        FV = GI // 2 + (1 if quantum else 0)
        scored, vt_ready, vt_evicted = sem("scored"), sem("vt_ready"), sem("vt_evicted")
        maxed, shifted, expd, summed, inverted, normed = (sem(n) for n in ("maxed", "shifted", "expd", "summed", "inverted", "normed"))
        pt_ready, pt_evicted, ctx_ready, ctx_evicted, added = (sem(n) for n in ("pt_ready", "pt_evicted", "ctx_ready", "ctx_evicted", "added"))
        block = ctx.enter_context(nc.Block())
        NT = 4

        @block.sync
        def _(sp):
            sp.dma_start(wqkv[:], dram["wqkv"]).then_inc(w_in, 16)
            sp.dma_start(wo[:], dram["wo"]).then_inc(w_in, 16)
            if quantum:
                sp.dma_start(wsp[:], dram["wsp"]).then_inc(w_in, 16)
                sp.dma_start(gate[:, 0:1], dram["qw"].broadcast_to([128, 1])).then_inc(gate_in, 16)

        @block.tensor
        def _(pe):
            if name == "a0":
                pe.wait_ge(env.con_in, 16)

            def project(c):
                pe.wait_ge(ln.ready, c + 1)
                raw = raw_evicted if rms else qk_evicted
                for j in range(3):
                    for m in range(2):
                        if j == 0 and c == 1:
                            pe.wait_ge(s_taken if quantum else v_spread, m + 1)
                        if j == 0 and c >= 2:
                            pe.wait_ge(added, 2 * (c - 2) + m + 1)
                        if j >= 1:
                            pe.wait_ge(raw, NT * c + 2 * (j - 1) + m + 1)
                        for a in range(2):
                            last = nc.tensor.matmul(ps[2 + m][0:HD, 0:CW], wqkv[:, a, j * D + m * HD:j * D + (m + 1) * HD],
                                                    chunk(x, c)[:, a], start=a == 0, stop=a == 1)
                        last.then_inc(proj[j], 1)
                        if rms and j >= 1:
                            head_mean_square(NT * c + 2 * (j - 1) + m)
                if quantum:
                    states(c)

            def states(c):
                for m in range(2):
                    pe.wait_ge(v_spread, 2 * c + m + 1)
                    for a in range(2):
                        last = nc.tensor.matmul(ps[2 + m][0:2 * QB, 0:CW], wsp[:, a, m * 2 * QB:(m + 1) * 2 * QB],
                                                chunk(x, c)[:, a], start=a == 0, stop=a == 1)
                    last.then_inc(s_proj, 1)
                pe.wait_ge(s_squared, c + 1)
                pe.wait_ge(ln.log_var, min(NC, c + 2))
                if c >= 1:
                    pe.wait_ge(s_factor, 4 * c - 3)
                if c >= 2:
                    pe.wait_ge(qt_moved, GPC * (c - 1))
                nc.tensor.matmul(ps[0][0:2 * QB, 0:CW], env.ones, ssq[:], start=True, stop=True).then_inc(s_norm, 1)

            def head_mean_square(t):
                pe.wait_ge(head_sq, t + 1)
                if t % NT == 0:
                    pe.wait_ge(ln.log_var, min(NC, t // NT + 2))
                if t > 0:
                    pe.wait_ge(head_log, t)
                nc.tensor.matmul(ps[0][0:HD, 0:CW], env.head_mean, rsq[:, t % 2], start=True, stop=True).then_inc(head_ms, 1)

            def scores(g):
                c = g // GPC
                pe.wait_ge(head_scaled if rms else qk_evicted, NT * c + NT)
                pe.wait_ge(k_spread, 2 * c + 2)
                if quantum:
                    pe.wait_ge(s_scaled, 2 * c + 2)
                if g >= 1:
                    pe.wait_ge(shifted, g)
                for i in range(GI):
                    i16 = (g % GPC) * GI + i
                    for a in range(2):
                        o = (i // 4) * HN * N + a * HH * N
                        last = nc.tensor.matmul(ps[4][SLOT * (i % 4):SLOT * (i % 4 + 1), o:o + HH * N],
                                                q[:, c % 2, a, i16 * N:i16 * N + SLOT], kx[:, c % 2, a, i16, :],
                                                start=True, stop=True)
                    if quantum:
                        o = 2 * HN * N + (i // 4) * 2 * N
                        last = nc.tensor.matmul(ps[4][SLOT * (i % 4):SLOT * (i % 4 + 1), o:o + 2 * N],
                                                st[:, c % 2, 0, i16 * N:i16 * N + SLOT], st[:, c % 2, :, i16 * N:(i16 + 1) * N],
                                                start=True, stop=True)
                last.then_inc(scored, 1)

            def turn_values(g):
                c = g // GPC
                pe.wait_ge(v_spread, 2 * c + 2)
                for f in range(GI // 2):
                    n = g * FV + f
                    if n >= 2:
                        pe.wait_ge(vt_evicted, n - 1)
                    for i in range(2):
                        for a in range(2):
                            o = (2 * i + a) * HD
                            last = nc.tensor.transpose(ps[5 + n % 2][0:HH * N, o:o + HD],
                                                       vx[:, c % 2, a, (g % GPC) * GI + 2 * f + i, :], env.ident[0:HD, 0:HD])
                    last.then_inc(vt_ready, 1)
                if quantum:
                    n = g * FV + FV - 1
                    pe.wait_ge(vt_evicted, n - 1)
                    for f in range(2):
                        for a in range(2):
                            o = (g * GI + 4 * f) * N
                            last = nc.tensor.transpose(ps[5 + n % 2][0:4 * N, (2 * f + a) * HD:(2 * f + a + 1) * HD],
                                                       x[:, a, o:o + 4 * N], env.ident[0:HD, 0:HD])
                    last.then_inc(vt_ready, 1)

            def weigh(g):
                c = g // GPC
                pe.wait_ge(normed, g + 1)
                if g >= 1:
                    pe.wait_ge(pt_evicted, g)
                for f in range(2):
                    for a in range(2):
                        j = 2 * f + a
                        last = nc.tensor.transpose(ps[7][0:HH * N, j * 128:(j + 1) * 128],
                                                   p[:, g % 2, f, a * HH * N:(a + 1) * HH * N], env.ident)
                last.then_inc(pt_ready, 1)
                if quantum:
                    pe.wait_ge(spread, g + 1)
                    pe.wait_ge(s_factor, 4 * min(NC, c + 2) - 3)
                    pe.wait_ge(ln.log_var, min(NC, c + 3))
                    if g >= 1:
                        pe.wait_ge(qt_moved, g)
                    for f in range(2):
                        last = nc.tensor.transpose(ps[0][0:4 * N, f * 128:f * 128 + QR],
                                                   px[0:QR, g % 2, f].rearrange("p i k -> p (i k)"), env.ident[0:QR, 0:QR])
                    last.then_inc(qt_ready, 1)
                pe.wait_ge(pt_evicted, g + 1)
                pe.wait_ge(vt_evicted, (g + 1) * FV)
                if g >= 1:
                    pe.wait_ge(ctx_evicted, 2 * g)
                for i in range(GI):
                    for a in range(2):
                        o = a * GW + i * N
                        last = nc.tensor.matmul(ps[1][0:HD, o:o + N], vt[:, g % 2, i, a, :],
                                                pt[:, g % 2, 2 * (i // 4) + a, SLOT * (i % 4):SLOT * (i % 4) + N],
                                                start=True, stop=True)
                last.then_inc(ctx_ready, 1)

            def project_out(c):
                pe.wait_ge(ctx_evicted, 2 * GPC * (c + 1))
                for m in range(2):
                    pe.wait_ge(s_taken if quantum else v_spread, 2 * min(c + 1, NC - 1) + m + 1)
                    if quantum:
                        pe.wait_ge(qt_moved, GPC * (c + 1))
                    if c == NC - 1:
                        pe.wait_ge(added, 2 * (c - 1) + m + 1)
                    for a in range(2):
                        last = nc.tensor.matmul(ps[2 + m][0:HD, 0:CW], wo[:, a, m * HD:(m + 1) * HD], cx[:, c % 2, a],
                                                start=a == 0, stop=a == 1 and not quantum)
                    for f in range(2 * GPC if quantum else 0):
                        last = nc.tensor.matmul(ps[2 + m][0:HD, f * 4 * N:(f + 1) * 4 * N], xt[:, f // 2, f % 2, m],
                                                qt[:, f // 2, f % 2].rearrange("p (i n) -> p i n", n=SLOT)[:, :, 0:N],
                                                start=False, stop=f == 2 * GPC - 1)
                    last.then_inc(proj[3], 1)

            for c in range(2):
                ln.mean(pe, c)
                ln.var(pe, c)
            pe.wait_ge(w_in, 48 if quantum else 32)
            project(0)
            for c in range(NC):
                if c + 2 < NC:
                    if rms:
                        pe.wait_ge(head_log, NT * (c + 1))
                    if quantum:
                        pe.wait_ge(s_factor, 4 * c + 1)
                        if c >= 1:
                            pe.wait_ge(qt_moved, GPC * c)
                    ln.mean(pe, c + 2)
                for g in (2 * c, 2 * c + 1):
                    scores(g)
                    turn_values(g)
                if c + 2 < NC:
                    ln.var(pe, c + 2)
                if c + 1 < NC:
                    project(c + 1)
                for g in (2 * c, 2 * c + 1):
                    weigh(g)
                project_out(c)

        @block.scalar
        def _(act):
            pre = name

            def take_qk(c):
                for j in range(2):
                    for m in range(2):
                        t = NT * c + 2 * j + m
                        act.wait_ge(proj[j], 2 * c + m + 1)
                        if c >= 2 and j == 0:
                            act.wait_ge(scored, GPC * (c - 1))
                        if c >= 2 and j == 1:
                            act.wait_ge(k_spread, 2 * (c - 1))
                        dst = (q if j == 0 else k)[:, c % 2, m, 0:CW]
                        bias = cols(env, pre + ("_qb" if j == 0 else "_kb"))[0:HD, m:m + 1]
                        nc.scalar.activation(dst, ps[2 + m][0:HD, 0:CW], ACT.Identity, bias=bias)\
                            .then_inc(raw_evicted if rms else qk_evicted, 1)
                        if rms:
                            act.wait_ge(raw_evicted, t + 1)
                            if t >= 2:
                                act.wait_ge(head_ms, t - 1)
                            nc.scalar.activation(rsq[:, t % 2], dst, ACT.Square).then_inc(head_sq, 1)
                            if t % NT:
                                head_rms(t - 1)
                if rms:
                    head_rms(NT * c + NT - 1)
                if quantum:
                    take_states(c)

            def take_states(c):
                for m in range(2):
                    act.wait_ge(s_proj, 2 * c + m + 1)
                    if c >= 2:
                        act.wait_ge(scored, GPC * (c - 1))
                    nc.scalar.activation(st[:, c % 2, m, 0:CW], ps[2 + m][0:2 * QB, 0:CW], ACT.Identity,
                                         bias=cols(env, name + ("_spb", "_spbx")[m])[0:2 * QB, :]).then_inc(s_taken, 1)
                act.wait_ge(s_taken, 2 * c + 1)
                if c >= 1:
                    act.wait_ge(s_norm, c)
                nc.scalar.activation(ssq[:], st[:, c % 2, 0, 0:CW], ACT.Square).then_inc(s_squared, 1)
                act.wait_ge(s_norm, c + 1)
                if c >= 1:
                    act.wait_ge(s_scaled, 2 * c)
                nc.scalar.activation(srs[:], ps[0][0:2 * QB, 0:CW], ACT.Ln, bias=tiny[0:2 * QB, 0:1]).then_inc(s_factor, 1)
                act.wait_ge(s_factor, 4 * c + 1)
                nc.scalar.activation(srs[:], srs[:], ACT.Exp, scale=0.5).then_inc(s_factor, 1)
                act.wait_ge(s_factor, 4 * c + 2)
                nc.scalar.activation(srs[:], srs[:], ACT.Ln, bias=tiny[0:2 * QB, 1:2]).then_inc(s_factor, 1)
                act.wait_ge(s_factor, 4 * c + 3)
                nc.scalar.activation(srs[:], srs[:], ACT.Exp, scale=-1.0).then_inc(s_factor, 1)

            def square_overlaps(g):
                act.wait_ge(scored, g + 1)
                if g >= 2:
                    act.wait_ge(fid_ready, g - 1)
                nc.scalar.activation(osq[:, g % 2].rearrange("p f e k -> p (f e k)"), ps[4][:, 2 * HN * N:2 * HN * N + 4 * N],
                                     ACT.Square, scale=HW ** 0.25).then_inc(ov_squared, 1)

            def head_rms(t):
                act.wait_ge(head_ms, t + 1)
                if t >= 2:
                    act.wait_ge(head_scaled, t - 1)
                nc.scalar.activation(rrs[:, t % 2], ps[0][0:HD, 0:CW], ACT.Ln, bias=env.rms_eps[0:HD, :]).then_inc(head_log, 1)
                act.wait_ge(head_log, t + 1)
                nc.scalar.activation(rrs[:, t % 2], rrs[:, t % 2], ACT.Exp, scale=-0.5).then_inc(head_rstd, 1)

            def take_values(g):
                for f in range(GI // 2):
                    n = g * FV + f
                    act.wait_ge(vt_ready, n + 1)
                    if g >= 2 and f == 0:
                        act.wait_ge(ctx_ready, g - 1)
                    nc.scalar.activation(vt[:, g % 2, 2 * f:2 * f + 2].rearrange("p i a f -> p (i a f)"),
                                         ps[5 + n % 2][0:HH * N, 0:4 * HD], ACT.Copy).then_inc(vt_evicted, 1)
                if quantum:
                    n = g * FV + FV - 1
                    act.wait_ge(vt_ready, n + 1)
                    if g >= 2:
                        act.wait_ge(proj[3], 2 * (g // GPC))
                    nc.scalar.activation(xt[:, g % 2].rearrange("p f a d -> p (f a d)"), ps[5 + n % 2][0:4 * N, 0:4 * HD],
                                         ACT.Copy).then_inc(vt_evicted, 1)

            def exponent(g):
                act.wait_ge(shifted, g + 1)
                nc.scalar.activation(p[:, g % 2], p[:, g % 2], ACT.Exp, scale=HW ** -0.5).then_inc(expd, 1)

            def take_context(g):
                c = g // GPC
                act.wait_ge(pt_ready, g + 1)
                if g >= 2:
                    act.wait_ge(ctx_ready, g - 1)
                nc.scalar.activation(pt[:, g % 2].rearrange("p a b -> p (a b)"), ps[7][0:HH * N, 0:512], ACT.Copy).then_inc(pt_evicted, 1)
                if quantum:
                    act.wait_ge(qt_ready, g + 1)
                    if g >= 2:
                        act.wait_ge(proj[3], 2 * c)
                    nc.scalar.activation(qt[:, g % 2, :, 0:QR], ps[0][0:4 * N, 0:256].rearrange("p (f q) -> p f q", f=2)[:, :, 0:QR],
                                         ACT.Copy).then_inc(qt_moved, 1)
                act.wait_ge(ctx_ready, g + 1)
                if c >= 2:
                    act.wait_ge(proj[3], 2 * (c - 1))
                for a in range(2):
                    o = (g % GPC) * GW
                    bias, scale = (gated_b[:, 0, a:a + 1], gate[0:HD, 1:2]) if quantum else (cols(env, pre + "_vb")[0:HD, a:a + 1], 1.0)
                    nc.scalar.activation(cx[:, c % 2, a, o:o + GW], ps[1][0:HD, a * GW:(a + 1) * GW], ACT.Identity,
                                         bias=bias, scale=scale).then_inc(ctx_evicted, 1)

            act.preload_act_table_set("natural_log_exp_and_others")
            if quantum:
                act.wait_ge(gate_in, 16)
                nc.scalar.activation(gate[:, 0:1], gate[:, 0:1], ACT.Exp, scale=-1.0).then_inc(gate_step, 1)
            for c in range(2):
                ln.square(act, c)
                ln.rstd(act, c)
            act.wait_ge(pad_zero, 3 if quantum else 1)
            if quantum:
                act.wait_ge(gate_step, 5)
            take_qk(0)
            for c in range(NC):
                if c + 2 < NC:
                    ln.square(act, c + 2)
                for g in (2 * c, 2 * c + 1):
                    if quantum:
                        square_overlaps(g)
                    take_values(g)
                    exponent(g)
                if c + 2 < NC:
                    ln.rstd(act, c + 2)
                if c + 1 < NC:
                    take_qk(c + 1)
                for g in (2 * c, 2 * c + 1):
                    take_context(g)

        @block.gpsimd
        def _(pool):
            pool.memset(q[:, :, :, CW:], 0.0).then_inc(pad_zero, 1)
            if quantum:
                pool.memset(st[:, :, :, CW:], 0.0).then_inc(pad_zero, 1)
                pool.memset(tiny[:, 0:1], 1e-19)
                pool.memset(tiny[:, 1:2], 1e-8).then_inc(pad_zero, 1)

            def spread_fidelities(g):
                pool.wait_ge(normed, g + 1)
                if g >= 2:
                    pool.wait_ge(qt_ready, g - 1)
                nc.gpsimd.tensor_tensor(px[:, g % 2], p[:, g % 2, :, None, HN * N:HP * N].broadcast_to([128, 2, 4, N]),
                                        env.image_mask[:, None, :, None].broadcast_to([128, 2, 4, N]), ALU.mult).then_inc(spread, 1)

            for c in range(NC):
                for a in range(2):
                    pool.wait_ge(head_scaled if rms else qk_evicted, NT * c + 2 + a + 1)
                    if c >= 2:
                        pool.wait_ge(scored, GPC * (c - 1))
                    nc.gpsimd.tensor_tensor(kx[:, c % 2, a].rearrange("p i (h k) -> p i h k", h=HH),
                                            k[:, c % 2, a].rearrange("p (i k) -> p i k", k=N)[:, :, None, :].broadcast_to([HD, IC, HH, N]),
                                            env.head_mask[:, None, :, None].broadcast_to([HD, IC, HH, N]), ALU.mult).then_inc(k_spread, 1)
                if quantum and c >= 1:
                    spread_fidelities(2 * c - 2)
                    spread_fidelities(2 * c - 1)
            if quantum:
                spread_fidelities(NG - 2)
                spread_fidelities(NG - 1)
                pool.wait_ge(spread, NG)

        @block.vector
        def _(dve):
            def head_scale(c):
                for t in range(NT * c, NT * c + NT):
                    j, m = (t % NT) // 2, t % 2
                    dst = (q if j == 0 else k)[:, c % 2, m, 0:CW]
                    dve.wait_ge(head_rstd, t + 1)
                    wcol = cols(env, name + ("_qn" if j == 0 else "_kn"))[0:HD, 0:1]
                    nc.vector.scalar_tensor_tensor(dst, dst, wcol, rrs[:, t % 2], ALU.mult, ALU.mult).then_inc(head_scaled, 1)

            def spread_values(c):
                for a in range(2):
                    dve.wait_ge(proj[2], 2 * c + a + 1)
                    if c >= 2:
                        dve.wait_ge(vt_ready, FV * GPC * (c - 1))
                    nc.vector.tensor_tensor(vx[:, c % 2, a].rearrange("p i (h k) -> p i h k", h=HH),
                                            ps[2 + a][0:HD, 0:CW].rearrange("p (i k) -> p i k", k=N)[:, :, None, :].broadcast_to([HD, IC, HH, N]),
                                            env.head_mask[:, None, :, None].broadcast_to([HD, IC, HH, N]), ALU.mult).then_inc(v_spread, 1)

            def softmax(g):
                s = ps[4][:, 0:2 * HN * N].rearrange("p (f h k) -> p f h k", f=2, k=N)
                pg = p[:, g % 2].rearrange("p f (h k) -> p f h k", k=N)
                dve.wait_ge(scored, g + 1)
                if g >= 2:
                    dve.wait_ge(pt_ready, g - 1)
                if quantum:
                    dve.wait_ge(ov_squared, g + 1)
                    if g >= 2:
                        dve.wait_ge(spread, g - 1)
                    nc.vector.tensor_tensor(pg[:, :, HN], osq[:, g % 2, :, 0], osq[:, g % 2, :, 1], ALU.add).then_inc(fid_ready, 1)
                nc.vector.reduce_max(mx[:, g % 2, :, 0:HN], s, AX_X).then_inc(maxed, 1)
                if quantum:
                    dve.wait_ge(fid_ready, g + 1)
                    nc.vector.reduce_max(mx[:, g % 2, :, HN], pg[:, :, HN], AX_X).then_inc(maxed, 1)
                    dve.wait_ge(maxed, 2 * g + 2)
                    nc.vector.tensor_tensor(pg[:, :, HN], pg[:, :, HN], mx[:, g % 2, :, HN, None].broadcast_to([128, 2, N]), ALU.subtract)
                else:
                    dve.wait_ge(maxed, g + 1)
                nc.vector.tensor_tensor(pg[:, :, 0:HN], s, mx[:, g % 2, :, 0:HN, None].broadcast_to([128, 2, HN, N]), ALU.subtract)\
                    .then_inc(shifted, 1)
                dve.wait_ge(expd, g + 1)
                nc.vector.reduce_sum(sm[:, g % 2], pg, AX_X).then_inc(summed, 1)
                dve.wait_ge(summed, g + 1)
                nc.vector.reciprocal(sm[:, g % 2], sm[:, g % 2]).then_inc(inverted, 1)
                dve.wait_ge(inverted, g + 1)
                if quantum:
                    nc.vector.tensor_scalar(sm[:, g % 2, :, HN], sm[:, g % 2, :, HN], gate[:, 0:1], None, ALU.mult).then_inc(weighted, 1)
                    dve.wait_ge(weighted, g + 1)
                nc.vector.tensor_tensor(pg, pg, sm[:, g % 2, :, :, None].broadcast_to([128, 2, HP, N]), ALU.mult).then_inc(normed, 1)

            def scale_states(c):
                dve.wait_ge(s_factor, 4 * c + 4)
                nc.vector.tensor_tensor(st[:, c % 2, 0, 0:CW], st[:, c % 2, 0, 0:CW], srs[:], ALU.mult).then_inc(s_scaled, 1)
                dve.wait_ge(s_taken, 2 * c + 2)
                nc.vector.scalar_tensor_tensor(st[:, c % 2, 1, 0:CW], st[:, c % 2, 1, 0:CW], env.conj[:, 0:1], srs[:], ALU.mult, ALU.mult)\
                    .then_inc(s_scaled, 1)

            if quantum:
                dve.wait_ge(gate_step, 1)
                nc.vector.tensor_scalar(gate[:, 0:1], gate[:, 0:1], 1.0, None, ALU.add).then_inc(gate_step, 1)
                dve.wait_ge(gate_step, 2)
                nc.vector.reciprocal(gate[:, 0:1], gate[:, 0:1]).then_inc(gate_step, 1)
                dve.wait_ge(gate_step, 3)
                nc.vector.tensor_scalar(gate[:, 1:2], gate[:, 0:1], -1.0, 1.0, ALU.mult, ALU.add).then_inc(gate_step, 1)
                dve.wait_ge(gate_step, 4)
                nc.vector.tensor_scalar(gated_b[:, 1], cols(env, name + "_ob")[0:HD, :], gate[0:HD, 1:2], None, ALU.mult)
                nc.vector.tensor_scalar(gated_b[:, 0], cols(env, name + "_vb")[0:HD, :], gate[0:HD, 1:2], None, ALU.mult).then_inc(gate_step, 1)
                dve.wait_ge(gate_step, 5)
            for c in range(2):
                ln.centre(dve, c)
                ln.scale(dve, c)
            if rms:
                head_scale(0)
            spread_values(0)
            if quantum:
                scale_states(0)
            for c in range(NC):
                if c + 2 < NC:
                    ln.centre(dve, c + 2)
                softmax(2 * c)
                softmax(2 * c + 1)
                if c + 2 < NC:
                    ln.scale(dve, c + 2)
                if c + 1 < NC:
                    if rms:
                        head_scale(c + 1)
                    spread_values(c + 1)
                    if quantum:
                        scale_states(c + 1)
                ob = gated_b[:, 1] if quantum else cols(env, name + "_ob")[0:HD, :]
                for m in range(2):
                    dve.wait_ge(proj[3], 2 * c + m + 1)
                    hc = chunk(env.h, c)[:, m]
                    nc.vector.scalar_tensor_tensor(hc, ps[2 + m][0:HD, 0:CW], ob[:, m:m + 1], hc,
                                                   ALU.add, ALU.add).then_inc(added, 1)
            dve.wait_ge(added, 2 * NC)


class Rms:

    def __init__(self, env, name, src, dst, w, ready_src, per_chunk):
        self.env, self.src, self.dst, self.w, self.ready_src, self.per_chunk = env, src, dst, w, ready_src, per_chunk
        self.squared = env.sem(name + "_squared")
        self.mean_ready = env.sem(name + "_mean_ready")
        self.log_mean = env.sem(name + "_log_mean")
        self.factor_ready = env.sem(name + "_factor_ready")
        self.ready = env.sem(name + "_ready")

    def square(self, act, c):
        nc, env = self.env.nc, self.env
        act.wait_ge(self.ready_src, self.per_chunk * (c + 1))
        if c >= 2:
            act.wait_ge(self.mean_ready, c - 1)
        nc.scalar.activation(self.sq[:, c % 2], chunk(self.src, c), ACT.Square).then_inc(self.squared, 1)

    def mean(self, pe, c):
        nc, env = self.env.nc, self.env
        pe.wait_ge(self.squared, c + 1)
        if c > 0:
            pe.wait_ge(self.log_mean, c)
        for a in range(2):
            last = nc.tensor.matmul(env.ps[1][0:HD, 0:CW], env.mean_w, self.sq[:, c % 2, a], start=a == 0, stop=a == 1)
        last.then_inc(self.mean_ready, 1)

    def factor(self, act, c):
        nc, env = self.env.nc, self.env
        act.wait_ge(self.mean_ready, c + 1)
        if c >= 2:
            act.wait_ge(self.ready, 2 * (c - 1))
        nc.scalar.activation(self.rs[:, c % 2], env.ps[1][0:HD, 0:CW], ACT.Ln, bias=env.rms_eps[0:HD, :]).then_inc(self.log_mean, 1)
        act.wait_ge(self.log_mean, c + 1)
        nc.scalar.activation(self.rs[:, c % 2], self.rs[:, c % 2], ACT.Exp, scale=-0.5).then_inc(self.factor_ready, 1)

    def scale(self, dve, c):
        nc = self.env.nc
        dve.wait_ge(self.factor_ready, c + 1)
        for a in range(2):
            nc.vector.scalar_tensor_tensor(chunk(self.dst, c)[:, a], chunk(self.src, c)[:, a], self.w[0:HD, a:a + 1],
                                           self.rs[:, c % 2], ALU.mult, ALU.mult).then_inc(self.ready, 1)


def stage_wide_attention(env, name, dram):
    nc = env.nc
    x, x2, ps = env.x, env.x2, env.ps
    JQ = QH // 2
    R = JQ * N
    KC = KVH * N
    KS = KVH * SLOT
    TQK, TV = JQ + KVH, KVH
    NT = TQK + TV
    with ExitStack() as ctx:
        def sb(n, shape, dt=F32):
            return ctx.enter_context(nc.sbuf_tensor(name + "_" + n, shape, dt))

        def sem(n):
            return env.sem(name + "_" + n)

        wq = sb("wq", [HD, 2, QH * WD])
        wk = sb("wk", [HD, 2, KVH * 2 * WD])
        wv = sb("wv", [HD, 2, KVH * WD])
        wo = sb("wo", [128, JQ, D])
        raw = sb("raw", [128, 2, CW])
        swp = sb("swapped", [128, 2, CW])
        q = sb("q", [128, 2, IC, R])
        k = sb("k", [128, 2, KVH, CW])
        vs = sb("vs", [WD, 2, IC, KVH, SLOT])
        vt = sb("vt", [KS, 2, GI, WD])
        s = sb("s", [R, 2, GI, KC])
        mx = sb("mx", [R, 2, GI])
        sm = sb("sm", [R, 2, GI])
        p = sb("p", [R, 2, 2, GI, KVH, SLOT])
        pt = sb("pt", [KS, 2, 2, GI, R])
        cx = sb("cx", [128, 2, JQ, CW])
        rsq1, rrs1, rsq2, rrs2 = sb("rsq1", [HD, 2, 2, CW]), sb("rrs1", [HD, 2, CW]), sb("rsq2", [HD, 2, 2, CW]), sb("rrs2", [HD, 2, CW])
        w_in = sem("w_in")
        ln = Norm(env, name + "_ln", x)
        added = sem("added")
        n1 = Rms(env, name + "_n1", x, x2, cols(env, "n1w"), ln.ready, 1)
        n2 = Rms(env, name + "_n2", x, x2, cols(env, "n2w"), added, 2)
        n1.sq, n1.rs, n2.sq, n2.rs = rsq1, rrs1, rsq2, rrs2
        zeroed, projected, taken, swapped, sin_done, cos_done, turned = (
            sem(n) for n in ("zeroed", "projected", "taken", "swapped", "sin_done", "cos_done", "turned"))
        scored, masked, maxed, shifted, expd, summed, inverted, normed = (
            sem(n) for n in ("scored", "masked", "maxed", "shifted", "expd", "summed", "inverted", "normed"))
        filled, moved, out_ready, h_added = (sem(n) for n in ("filled", "moved", "out_ready", "h_added"))
        FG = 1 + 6
        FC = GPC * FG

        def fill_of(g, j):
            base = FC * (g // GPC)
            return base + g % GPC if j == 0 else base + GPC + (FG - 1) * (g % GPC) + j - 1

        block = ctx.enter_context(nc.Block())

        @block.sync
        def _(sp):
            sp.dma_start(wq[:], dram["wq"]).then_inc(w_in, 16)
            sp.dma_start(wk[:], dram["wk"]).then_inc(w_in, 16)
            sp.dma_start(wv[:], dram["wv"]).then_inc(w_in, 16)
            sp.dma_start(wo[:], dram["wo"]).then_inc(w_in, 16)

        @block.tensor
        def _(pe):
            def project(c):
                pe.wait_ge(n1.ready, 2 * (c + 1))
                for t in range(NT):
                    if t >= 2:
                        pe.wait_ge(taken, NT * c + t - 1)
                    elif c == 1:
                        pe.wait_ge(taken, NT - 1 + t)
                    elif c >= 2:
                        pe.wait_ge(added, 2 * (c - 2) + t + 1)
                    w, rows = (wq, 128) if t < JQ else (wk, 128) if t < TQK else (wv, WD)
                    j = t if t < JQ else t - JQ if t < TQK else t - TQK
                    for a in range(2):
                        last = nc.tensor.matmul(ps[2 + t % 2][0:rows, 0:CW], w[:, a, j * rows:(j + 1) * rows],
                                                chunk(x2, c)[:, a], start=a == 0, stop=a == 1)
                    last.then_inc(projected, 1)

            def scores(g):
                c = g // GPC
                pe.wait_ge(turned, TQK * (c + 1))
                if g >= 1:
                    pe.wait_ge(masked, g)
                for i in range(GI):
                    i16 = (g % GPC) * GI + i
                    for e in range(2):
                        last = nc.tensor.matmul(ps[4 + e][0:R, i * KC:(i + 1) * KC], q[e * WD:(e + 1) * WD, c % 2, i16, :],
                                                k[e * WD:(e + 1) * WD, c % 2, :, i16 * N:(i16 + 1) * N], start=True, stop=True)
                last.then_inc(scored, 1)

            def bank(g, j):
                n = fill_of(g, j)
                if n >= 2:
                    pe.wait_ge(moved, n - 1)
                return ps[6 + n % 2]

            def turn_values(g):
                c = g // GPC
                pe.wait_ge(taken, NT * (c + 1))
                to = bank(g, 0)
                for i in range(GI):
                    last = nc.tensor.transpose(to[0:KS, i * WD:(i + 1) * WD],
                                               vs[:, c % 2, (g % GPC) * GI + i].rearrange("p g k -> p (g k)"), env.ident[0:WD, 0:WD])
                last.then_inc(filled, 1)

            def weigh(g):
                pe.wait_ge(normed, g + 1)
                for j in range(4):
                    to, e = bank(g, 1 + j), j % 2
                    for i in range(4):
                        last = nc.tensor.transpose(to[0:KS, i * R:(i + 1) * R],
                                                   p[:, g % 2, e, 4 * (j // 2) + i].rearrange("p g k -> p (g k)"), env.ident[0:R, 0:R])
                    last.then_inc(filled, 1)
                for j in range(2):
                    pe.wait_ge(moved, fill_of(g, 2 + 2 * j) + 1)
                    to = bank(g, 5 + j)
                    for i in range(4):
                        for e in range(2):
                            last = nc.tensor.matmul(to[e * WD:(e + 1) * WD, i * R:(i + 1) * R], vt[:, g % 2, 4 * j + i, :],
                                                    pt[:, g % 2, e, 4 * j + i, :], start=True, stop=True)
                    last.then_inc(filled, 1)

            def project_out(c):
                pe.wait_ge(moved, fill_of(GPC * c + GPC - 1, 6) + 1)
                for m in range(2):
                    pe.wait_ge(taken, NT * min(c + 1, NC - 1) + NT - 1 + m)
                    if c == NC - 1:
                        pe.wait_ge(added, 2 * (c - 1) + m + 1)
                    for j in range(JQ):
                        last = nc.tensor.matmul(ps[2 + m][0:HD, 0:CW], wo[:, j, m * HD:(m + 1) * HD], cx[:, c % 2, j],
                                                start=j == 0, stop=j == JQ - 1)
                    last.then_inc(out_ready, 1)

            for c in range(2):
                ln.mean(pe, c)
                ln.var(pe, c)
                n1.mean(pe, c)
            pe.wait_ge(w_in, 64)
            project(0)
            for c in range(NC):
                if c + 2 < NC:
                    ln.mean(pe, c + 2)
                for g in (2 * c, 2 * c + 1):
                    scores(g)
                    turn_values(g)
                if c >= 1:
                    pe.wait_ge(n1.log_mean, min(NC, c + 2))
                    n2.mean(pe, c - 1)
                if c + 2 < NC:
                    ln.var(pe, c + 2)
                    if c >= 1:
                        pe.wait_ge(n2.log_mean, c)
                    n1.mean(pe, c + 2)
                if c + 1 < NC:
                    project(c + 1)
                for g in (2 * c, 2 * c + 1):
                    weigh(g)
                project_out(c)
            n2.mean(pe, NC - 1)

        @block.scalar
        def _(act):
            def take(c):
                for t in range(NT):
                    n = NT * c + t
                    act.wait_ge(projected, n + 1)
                    if t < TQK:
                        r = TQK * c + t
                        if r >= 2:
                            act.wait_ge(turned, r - 1)
                        nc.scalar.activation(raw[:, r % 2], ps[2 + t % 2][:, 0:CW], ACT.Copy).then_inc(taken, 1)
                    else:
                        if c >= 2 and t == TQK:
                            act.wait_ge(filled, fill_of(GPC * (c - 2) + GPC - 1, 0) + 1)
                        nc.scalar.activation(vs[:, c % 2, :, t - TQK, 0:N],
                                             ps[2 + t % 2][0:WD, 0:CW].rearrange("p (i k) -> p i k", k=N), ACT.Copy).then_inc(taken, 1)

            def take_values(g):
                n = fill_of(g, 0)
                act.wait_ge(filled, n + 1)
                if g >= 2:
                    act.wait_ge(filled, fill_of(g - 2, 6) + 1)
                nc.scalar.activation(vt[:, g % 2].rearrange("p i d -> p (i d)"), ps[6 + n % 2][0:KS, 0:GI * WD], ACT.Copy).then_inc(moved, 1)

            def exponent(g):
                act.wait_ge(shifted, g + 1)
                nc.scalar.activation(s[:], s[:], ACT.Exp, scale=WD ** -0.5).then_inc(expd, 1)

            def move_weighed(g):
                c = g // GPC
                for j in range(4):
                    n = fill_of(g, 1 + j)
                    act.wait_ge(filled, n + 1)
                    nc.scalar.activation(pt[:, g % 2, j % 2, 4 * (j // 2):4 * (j // 2) + 4].rearrange("p i r -> p (i r)"),
                                         ps[6 + n % 2][0:KS, 0:4 * R], ACT.Copy).then_inc(moved, 1)
                for j in range(2):
                    n = fill_of(g, 5 + j)
                    act.wait_ge(filled, n + 1)
                    if c >= 2:
                        act.wait_ge(out_ready, 2 * (c - 1))
                    o = ((g % GPC) * GI + 4 * j) * N
                    nc.scalar.activation(cx[:, c % 2, :, o:o + 4 * N].rearrange("p j (i n) -> p i j n", n=N),
                                         ps[6 + n % 2][:, 0:4 * R].rearrange("p (i j n) -> p i j n", i=4, j=JQ), ACT.Copy).then_inc(moved, 1)

            for c in range(2):
                ln.square(act, c)
                ln.rstd(act, c)
                n1.square(act, c)
                n1.factor(act, c)
            act.wait_ge(zeroed, 2)
            take(0)
            for c in range(NC):
                if c + 2 < NC:
                    ln.square(act, c + 2)
                if c >= 1:
                    n2.square(act, c - 1)
                for g in (2 * c, 2 * c + 1):
                    take_values(g)
                    exponent(g)
                if c >= 1:
                    n2.factor(act, c - 1)
                if c + 2 < NC:
                    ln.rstd(act, c + 2)
                    n1.square(act, c + 2)
                    n1.factor(act, c + 2)
                if c + 1 < NC:
                    take(c + 1)
                for g in (2 * c, 2 * c + 1):
                    move_weighed(g)
            n2.square(act, NC - 1)
            n2.factor(act, NC - 1)

        @block.gpsimd
        def _(pool):
            pool.memset(vs[:, :, :, :, N:], 0.0).then_inc(zeroed, 1)
            pool.memset(p[:], 0.0).then_inc(zeroed, 1)

            def table(tab):
                return tab[:, None, :].broadcast_to([128, IC, N])

            def by_token(ap):
                return ap.rearrange("p (i n) -> p i n", n=N)

            def turn(c):
                for t in range(TQK):
                    r = TQK * c + t
                    pool.wait_ge(swapped, r + 1)
                    nc.gpsimd.tensor_tensor(by_token(raw[:, r % 2]), by_token(raw[:, r % 2]), table(env.cos), ALU.mult).then_inc(cos_done, 1)
                    nc.gpsimd.tensor_tensor(by_token(swp[:, r % 2]), by_token(swp[:, r % 2]), table(env.sin), ALU.mult).then_inc(sin_done, 1)

            turn(0)
            for c in range(NC):
                if c + 1 < NC:
                    turn(c + 1)
                pool.wait_ge(added, 2 * c + 2)
                nc.gpsimd.tensor_tensor(chunk(env.h, c), chunk(env.h, c), chunk(x, c), ALU.add).then_inc(h_added, 1)
            pool.wait_ge(h_added, NC)

        @block.vector
        def _(dve):
            def swap(r):
                dve.wait_ge(taken, NT * (r // TQK) + r % TQK + 1)
                nc.vector.stream_shuffle(swp[:, r % 2], raw[:, r % 2], [i ^ 1 for i in range(32)]).then_inc(swapped, 1)

            def turn(c):
                for t in range(TQK + 1):
                    r = TQK * c + t
                    if t < TQK:
                        swap(r)
                    if t == 0:
                        continue
                    r, u = r - 1, t - 1
                    dve.wait_ge(cos_done, r + 1)
                    dve.wait_ge(sin_done, r + 1)
                    if c >= 2 and u == 0:
                        dve.wait_ge(scored, GPC * (c - 1))
                    if u < JQ:
                        nc.vector.tensor_tensor(q[:, c % 2, :, u * N:(u + 1) * N], raw[:, r % 2].rearrange("p (i n) -> p i n", n=N),
                                                swp[:, r % 2].rearrange("p (i n) -> p i n", n=N), ALU.add).then_inc(turned, 1)
                    else:
                        nc.vector.tensor_tensor(k[:, c % 2, u - JQ], raw[:, r % 2], swp[:, r % 2], ALU.add).then_inc(turned, 1)

            def softmax(g):
                sc = env.psall[0:R, 4:6, 0:GI * KC].rearrange("p e (i k) -> p e i k", k=KC)
                if g >= 1:
                    dve.wait_ge(normed, g)
                dve.wait_ge(scored, g + 1)
                nc.vector.tensor_tensor(s[:], sc, env.causal[:, None, None, :].broadcast_to([R, 2, GI, KC]), ALU.add).then_inc(masked, 1)
                dve.wait_ge(masked, g + 1)
                nc.vector.reduce_max(mx[:], s[:], AX_X).then_inc(maxed, 1)
                dve.wait_ge(maxed, g + 1)
                nc.vector.tensor_tensor(s[:], s[:], mx[:, :, :, None].broadcast_to([R, 2, GI, KC]), ALU.subtract).then_inc(shifted, 1)
                dve.wait_ge(expd, g + 1)
                nc.vector.reduce_sum(sm[:], s[:], AX_X).then_inc(summed, 1)
                dve.wait_ge(summed, g + 1)
                nc.vector.reciprocal(sm[:], sm[:]).then_inc(inverted, 1)
                dve.wait_ge(inverted, g + 1)
                if g >= 2:
                    dve.wait_ge(filled, fill_of(g - 2, 4) + 1)
                for e in range(2):
                    last = nc.vector.tensor_tensor(p[:, g % 2, e, :, :, 0:N], s[:, e].rearrange("p i (g k) -> p i g k", k=N),
                                                   sm[:, e, :, None, None].broadcast_to([R, GI, KVH, N]), ALU.mult)
                last.then_inc(normed, 1)

            for c in range(2):
                ln.centre(dve, c)
                ln.scale(dve, c)
                n1.scale(dve, c)
            turn(0)
            dve.wait_ge(zeroed, 2)
            for c in range(NC):
                if c + 2 < NC:
                    ln.centre(dve, c + 2)
                softmax(2 * c)
                softmax(2 * c + 1)
                if c >= 1:
                    n2.scale(dve, c - 1)
                if c + 2 < NC:
                    ln.scale(dve, c + 2)
                    n1.scale(dve, c + 2)
                if c + 1 < NC:
                    turn(c + 1)
                for m in range(2):
                    dve.wait_ge(out_ready, 2 * c + m + 1)
                    xc = chunk(x, c)[:, m]
                    nc.vector.tensor_tensor(xc, ps[2 + m][0:HD, 0:CW], xc, ALU.add).then_inc(added, 1)
            n2.scale(dve, NC - 1)
            dve.wait_ge(n2.ready, 2 * NC)


def stage_experts(env, name, dram):
    nc = env.nc
    x2, ps = env.x2, env.ps
    RT = 64
    NR = T // RT
    NF = EF // 128
    STEPS = 2 * NC
    ITS = NE // 2
    with ExitStack() as ctx:
        def sb(n, shape, dt=F32):
            return ctx.enter_context(nc.sbuf_tensor(name + "_" + n, shape, dt))

        def sem(n):
            return env.sem(name + "_" + n)

        wr = sb("wr", [HD, 2, NE])
        wgu = sb("wgu", [HD, 2, 2, 2 * EF])
        wd = sb("wd", [128, 2, NF, D])
        cb = sb("cb", [HD, 2, T])
        pr = sb("pr", [RT, NR, NE])
        t0, t1, t2, t3 = (sb(f"t{i}", [RT, NR, NE]) for i in range(4))
        r0, r1 = sb("r0", [RT, NR]), sb("r1", [RT, NR])
        top8 = sb("top8", [RT, NR, 8])
        cbt = sb("cbt", [NE, T])
        gs = sb("gs", [128, 2, CW])
        hid = sb("hid", [128, 2, NF, CW])
        wy = sb("wy", [HD, 2, 2, CW])
        comb_dram = nc.dram_tensor(name + "_comb", (NE, T), F32).ap()
        wr_in, routed, exp_in, exp_out, turned, comb_moved, comb_out = (
            sem(n) for n in ("wr_in", "routed", "logits_shifted", "logits_exp", "comb_turned", "comb_moved", "comb_out"))
        chain = sem("router_steps")
        w_in = [sem("w0_in"), sem("w1_in")]
        gate_ready, up_ready, silu_ready, hid_ready, down_ready, weighted, h_added = (
            sem(n) for n in ("gate_ready", "up_ready", "silu_ready", "hid_ready", "down_ready", "weighted", "h_added"))
        block = ctx.enter_context(nc.Block())

        def wait(eng, s, value):
            if not isinstance(value, int) or value > 0:
                eng.wait_ge(s, value)

        def iterations(eng, body):
            body(0, False)
            with eng.Fori(1, ITS - 1) as it:
                body(it, False)
            body(ITS - 1, True)

        @block.sync
        def _(sp):
            sp.dma_start(wr[:], dram["wr"]).then_inc(wr_in, 16)

            def load_weights(e, par):
                sp.dma_start(wgu[:, par], dram["gate_up"][bass.ds(e, 1)].rearrange("e (a p) f -> p (e a) f", a=2)).then_inc(w_in[par], 16)
                sp.dma_start(wd[:, par], dram["down"][bass.ds(e, 1)].rearrange("e (j p) f -> p (e j) f", p=128)).then_inc(w_in[par], 16)

            def load_comb(e, par):
                sp.dma_start(cb[:, par], comb_dram[bass.ds(e, 1), :].broadcast_to([HD, T])).then_inc(w_in[par], 16)

            for par in range(2):
                load_weights(par, par)
            sp.wait_ge(comb_moved, 3)
            sp.dma_start(comb_dram, cbt[:]).then_inc(comb_out, 16)
            sp.wait_ge(comb_out, 16)
            for par in range(2):
                load_comb(par, par)
            with sp.Fori(1, ITS) as it:
                for par in range(2):
                    sp.wait_ge(down_ready, it * STEPS + (par - 1) * NC)
                    load_weights(it * 2 + par, par)
                    sp.wait_ge(weighted, it * STEPS + (par - 1) * NC)
                    load_comb(it * 2 + par, par)

        @block.tensor
        def _(pe):
            pe.wait_ge(wr_in, 16)
            for t in range(NR):
                for a in range(2):
                    last = nc.tensor.matmul(ps[0][0:RT, t * NE:(t + 1) * NE], x2[:, a, t * RT:(t + 1) * RT], wr[:, a], start=a == 0, stop=a == 1)
            last.then_inc(routed, 1)
            pe.wait_ge(chain, ROUTER_STEPS)
            for t in range(NR):
                last = nc.tensor.transpose(ps[1 + t // 8][0:NE, (t % 8) * RT:(t % 8 + 1) * RT], pr[:, t], env.ident[0:RT, 0:RT])
            last.then_inc(turned, 1)
            pe.wait_ge(comb_moved, 3)

            def gate_up(it, u):
                par, c = (u // NC) % 2, u % NC
                if c == 0:
                    pe.wait_ge(w_in[par], (it + (1 if u >= STEPS else 0)) * 48 + 48)
                for f in range(NF):
                    n = it * (STEPS * NF) + (u * NF + f)
                    b = (u * NF + f) % 2
                    wait(pe, silu_ready, n - 1)
                    for a in range(2):
                        last = nc.tensor.matmul(ps[b][:, 0:CW], wgu[:, par, a, f * 128:(f + 1) * 128], chunk(x2, c)[:, a], start=a == 0, stop=a == 1)
                    last.then_inc(gate_ready, 1)
                    wait(pe, hid_ready, n - 1)
                    for a in range(2):
                        last = nc.tensor.matmul(ps[2 + b][:, 0:CW], wgu[:, par, a, EF + f * 128:EF + (f + 1) * 128], chunk(x2, c)[:, a],
                                                start=a == 0, stop=a == 1)
                    last.then_inc(up_ready, 1)

            def down(it, u):
                par = (u // NC) % 2
                s = it * STEPS + u
                pe.wait_ge(hid_ready, s * NF + NF)
                wait(pe, weighted, s - 1)
                for m in range(2):
                    for f in range(NF):
                        last = nc.tensor.matmul(ps[4 + 2 * (u % 2) + m][0:HD, 0:CW], wd[:, par, f, m * HD:(m + 1) * HD], hid[:, u % 2, f],
                                                start=f == 0, stop=f == NF - 1)
                last.then_inc(down_ready, 1)

            gate_up(0, 0)

            def body(it, last_it):
                for u in range(STEPS):
                    if not (last_it and u == STEPS - 1):
                        gate_up(it, u + 1)
                    down(it, u)

            iterations(pe, body)

        @block.scalar
        def _(act):
            act.wait_ge(exp_in, 1)
            nc.scalar.activation(pr[:], pr[:], ACT.Exp).then_inc(exp_out, 1)
            act.wait_ge(turned, 1)
            for b in range(3):
                w = min(512, T - 512 * b)
                nc.scalar.activation(cbt[:, 512 * b:512 * b + w], ps[1 + b][0:NE, 0:w], ACT.Copy).then_inc(comb_moved, 1)

            def body(it, last_it):
                for u in range(STEPS):
                    for f in range(NF):
                        b = (u * NF + f) % 2
                        n = it * (STEPS * NF) + (u * NF + f)
                        act.wait_ge(gate_ready, n + 1)
                        wait(act, hid_ready, n - 1)
                        nc.scalar.activation(gs[:, b], ps[b][:, 0:CW], ACT.Silu).then_inc(silu_ready, 1)

            iterations(act, body)

        @block.gpsimd
        def _(pool):
            def body(it, last_it):
                for u in range(STEPS):
                    c = u % NC
                    pool.wait_ge(weighted, it * STEPS + (u + 1))
                    nc.gpsimd.tensor_tensor(chunk(env.h, c), chunk(env.h, c), wy[:, u % 2], ALU.add).then_inc(h_added, 1)

            iterations(pool, body)
            pool.wait_ge(h_added, ITS * STEPS)

        @block.vector
        def _(dve):
            steps = [0]

            def link(ins):
                steps[0] += 1
                ins.then_inc(chain, 1)
                dve.wait_ge(chain, steps[0])

            def over(v):
                return v[:, :, None].broadcast_to([RT, NR, NE])

            V = nc.vector
            logits = ps[0][0:RT, 0:NR * NE].rearrange("p (t e) -> p t e", e=NE)
            dve.wait_ge(routed, 1)
            link(V.reduce_max(r0[:], logits, AX_X))
            V.tensor_tensor(pr[:], logits, over(r0), ALU.subtract).then_inc(exp_in, 1)
            dve.wait_ge(exp_out, 1)
            link(V.reduce_sum(r0[:], pr[:], AX_X))
            link(V.reciprocal(r0[:], r0[:]))
            link(V.tensor_tensor(pr[:], pr[:], over(r0), ALU.mult))
            for t in range(NR):
                last = V.max(top8[:, t], pr[:, t])
            link(last)
            second = top8[:, :, 1:2].broadcast_to([RT, NR, NE])
            link(V.tensor_tensor(t0[:], pr[:], second, ALU.is_gt))
            link(V.tensor_tensor(t1[:], pr[:], second, ALU.is_equal))
            link(V.reduce_sum(r1[:], t0[:], AX_X))
            link(V.tensor_scalar(r1[:], r1[:], -1.0, 2.0, ALU.mult, ALU.add))
            a = t1
            for sh, b in ((1, t2), (2, t3), (4, t2), (8, t3)):
                V.tensor_copy(b[:, :, 0:sh], a[:, :, 0:sh])
                link(V.tensor_tensor(b[:, :, sh:], a[:, :, sh:], a[:, :, 0:NE - sh], ALU.add))
                a = b
            link(V.tensor_tensor(a[:], a[:], over(r1), ALU.is_le))
            link(V.tensor_tensor(a[:], a[:], t1[:], ALU.mult))
            link(V.tensor_tensor(a[:], a[:], t0[:], ALU.add))
            link(V.tensor_tensor(pr[:], pr[:], a[:], ALU.mult))
            link(V.reduce_sum(r0[:], pr[:], AX_X))
            link(V.reciprocal(r0[:], r0[:]))
            link(V.tensor_tensor(pr[:], pr[:], over(r0), ALU.mult))
            assert steps[0] == ROUTER_STEPS, steps[0]

            def body(it, last_it):
                for u in range(STEPS):
                    par, c = (u // NC) % 2, u % NC
                    s = it * STEPS + u
                    for f in range(NF):
                        n = it * (STEPS * NF) + (u * NF + f)
                        b = (u * NF + f) % 2
                        dve.wait_ge(silu_ready, n + 1)
                        dve.wait_ge(up_ready, n + 1)
                        if f == 0:
                            wait(dve, down_ready, s - 1)
                        V.tensor_tensor(hid[:, u % 2, f], ps[2 + b][:, 0:CW], gs[:, b], ALU.mult).then_inc(hid_ready, 1)
                    if u > 0 or not isinstance(it, int) or it > 0:
                        weight(it, u - 1)
                if last_it:
                    weight(it, STEPS - 1)

            def weight(it, u):
                par, c = (u // NC) % 2, u % NC
                s = it * STEPS + u
                dve.wait_ge(down_ready, s + 1)
                if c == 0:
                    dve.wait_ge(w_in[par], it * 48 + 48)
                wait(dve, h_added, s - 1)
                V.tensor_tensor(wy[:, u % 2], env.psall[0:HD, 4 + 2 * (u % 2):6 + 2 * (u % 2), 0:CW],
                                cb[:, par, None, c * CW:(c + 1) * CW].broadcast_to([HD, 2, CW]), ALU.mult).then_inc(weighted, 1)

            iterations(dve, body)


def complex_product(link, V, out_re, out_im, a_re, a_im, b_re, b_im, tmp):
    link(V.tensor_tensor(out_re, a_re, b_re, ALU.mult))
    link(V.tensor_tensor(tmp, a_im, b_im, ALU.mult))
    link(V.tensor_tensor(out_re, out_re, tmp, ALU.subtract))
    link(V.tensor_tensor(out_im, a_re, b_im, ALU.mult))
    link(V.tensor_tensor(tmp, a_im, b_re, ALU.mult))
    link(V.tensor_tensor(out_im, out_im, tmp, ALU.add))


def stage_convolution(env, name, dram):
    nc = env.nc
    x = env.x
    x4 = x[:, :, :].rearrange("p a (b n) -> p a b n", n=N)
    with ExitStack() as ctx:
        def sb(n, shape, dt=F32):
            return ctx.enter_context(nc.sbuf_tensor(name + "_" + n, shape, dt))

        def sem(n):
            return env.sem(name + "_" + n)

        prm = sb("prm", [HD, 4, 2, SN])
        d = sb("delta", [HD, 2, 6])
        t = sb("t", [HD, 12, 2, SN])
        pw = sb("pw", [HD, 5, 2, 2, SN])
        wr, wi, wt = (sb(n, [HD, 2, N, SN]) for n in ("wr", "wi", "wt"))
        taps = sb("taps", [HD, 2, N])
        prm_in, dve_step, act_step, pool_step = sem("prm_in"), sem("dve_step"), sem("act_step"), sem("pool_step")
        powers_ready, response_ready, taps_ready, added = (sem(n) for n in ("powers_ready", "response_ready", "taps_ready", "added"))
        ln = Norm(env, name + "_ln", x)
        ld = cols(env, "s1_ld")[0:HD, :]
        C1, C2 = 6.28125, 0.0019353071795864769
        block = ctx.enter_context(nc.Block())

        @block.sync
        def _(sp):
            sp.dma_start(prm[:], dram["prm"]).then_inc(prm_in, 16)

        @block.tensor
        def _(pe):
            for c in range(NC):
                ln.mean(pe, c)
                ln.var(pe, c)

        @block.scalar
        def _(act):
            act.wait_ge(dve_step, 1)
            nc.scalar.activation(d[:, :, 1], d[:, :, 0], ACT.Exp, scale=-1.0).then_inc(act_step, 1)
            act.wait_ge(dve_step, 2)
            nc.scalar.activation(d[:, :, 3], d[:, :, 2], ACT.Ln).then_inc(act_step, 1)
            act.wait_ge(dve_step, 8)
            nc.scalar.activation(t[:, 0], t[:, 0], ACT.Exp).then_inc(act_step, 1)
            for c in range(NC):
                ln.square(act, c)
                ln.rstd(act, c)
            act.wait_ge(dve_step, 20)
            nc.scalar.activation(t[:, 3], t[:, 3], ACT.Sin).then_inc(act_step, 1)
            nc.scalar.activation(t[:, 4], t[:, 4], ACT.Sin).then_inc(act_step, 1)

        @block.gpsimd
        def _(pool):
            steps = [0]

            def link(ins):
                steps[0] += 1
                ins.then_inc(pool_step, 1)
                pool.wait_ge(pool_step, steps[0])

            pool.wait_ge(powers_ready, 1)
            for i, (at, n) in enumerate(((1, 1), (2, 2), (4, 4), (8, 8), (16, 1))):
                def power(part):
                    return pw[:, i, part, :, None, :].broadcast_to([HD, 2, n, SN])
                complex_product(link, nc.gpsimd, wr[:, :, at:at + n], wi[:, :, at:at + n], wr[:, :, 0:n], wi[:, :, 0:n],
                                power(0), power(1), wt[:, :, 0:n])
            pool.sem_inc(response_ready, 1)

        @block.vector
        def _(dve):
            V = nc.vector
            steps = [0]

            def link(ins):
                steps[0] += 1
                ins.then_inc(dve_step, 1)
                dve.wait_ge(dve_step, steps[0])

            def after_act(n):
                dve.wait_ge(act_step, n)

            dve.wait_ge(prm_in, 16)
            V.tensor_scalar(d[:, :, 4], ld, -1.0, None, ALU.mult).then_inc(taps_ready, 1)
            dve.wait_ge(taps_ready, 1)
            link(V.tensor_tensor(d[:, :, 0], ld, d[:, :, 4], ALU.max))
            after_act(1)
            link(V.tensor_scalar(d[:, :, 2], d[:, :, 1], 1.0, None, ALU.add))
            link(V.tensor_scalar(d[:, :, 4], d[:, :, 2], 1.0, None, ALU.subtract))
            link(V.tensor_tensor(d[:, :, 4], d[:, :, 1], d[:, :, 4], ALU.subtract))
            link(V.reciprocal(d[:, :, 5], d[:, :, 2]))
            after_act(2)
            link(V.tensor_tensor(d[:, :, 4], d[:, :, 4], d[:, :, 5], ALU.mult))
            V.tensor_scalar(d[:, :, 5], ld, 0.0, None, ALU.max)
            link(V.tensor_tensor(d[:, :, 3], d[:, :, 3], d[:, :, 4], ALU.add))
            V.tensor_tensor(d[:, :, 0], d[:, :, 3], d[:, :, 5], ALU.add).then_inc(taps_ready, 1)
            dve.wait_ge(taps_ready, 2)
            delta = d[:, :, 0:1].broadcast_to([HD, 2, SN])
            ar, ai, bm, cm = (prm[:, i] for i in range(4))
            link(V.tensor_tensor(t[:, 0], ar, delta, ALU.mult))
            link(V.tensor_tensor(t[:, 1], ai, delta, ALU.mult))
            link(V.tensor_scalar(t[:, 2], t[:, 1], float(1 / (2 * np.pi)), ROUND, ALU.mult, ALU.add))
            link(V.tensor_scalar(t[:, 2], t[:, 2], ROUND, None, ALU.subtract))
            link(V.scalar_tensor_tensor(t[:, 1], t[:, 2], -C1, t[:, 1], ALU.mult, ALU.add))
            link(V.scalar_tensor_tensor(t[:, 1], t[:, 2], -C2, t[:, 1], ALU.mult, ALU.add))
            link(V.tensor_scalar(t[:, 3], t[:, 1], PI_DOWN, -PI_DOWN, ALU.min, ALU.max))
            link(V.tensor_scalar(t[:, 4], t[:, 1], float(np.pi / 2), None, ALU.add))
            link(V.tensor_scalar(t[:, 5], t[:, 4], PI_DOWN, float(2 * np.pi), ALU.is_gt, ALU.mult))
            link(V.tensor_tensor(t[:, 4], t[:, 4], t[:, 5], ALU.subtract))
            link(V.tensor_scalar(t[:, 4], t[:, 4], PI_DOWN, -PI_DOWN, ALU.min, ALU.max))
            link(V.tensor_tensor(t[:, 6], ar, ar, ALU.mult))
            link(V.tensor_tensor(t[:, 7], ai, ai, ALU.mult))
            link(V.tensor_tensor(t[:, 6], t[:, 6], t[:, 7], ALU.add))
            link(V.reciprocal(t[:, 6], t[:, 6]))
            for c in range(NC):
                ln.centre(dve, c)
                ln.scale(dve, c)
            after_act(5)
            abr, abi = pw[:, 0, 0], pw[:, 0, 1]
            link(V.tensor_tensor(abi, t[:, 0], t[:, 3], ALU.mult))
            link(V.tensor_tensor(abr, t[:, 0], t[:, 4], ALU.mult))
            for i in range(4):
                complex_product(link, V, pw[:, i + 1, 0], pw[:, i + 1, 1], pw[:, i, 0], pw[:, i, 1], pw[:, i, 0], pw[:, i, 1], t[:, 8])
            link(V.tensor_scalar(t[:, 9], abr, 1.0, None, ALU.subtract))
            link(V.tensor_scalar(t[:, 10], ai, -1.0, None, ALU.mult))
            complex_product(link, V, wr[:, :, 0], wi[:, :, 0], t[:, 9], abi, ar, t[:, 10], t[:, 8])
            link(V.tensor_tensor(t[:, 6], t[:, 6], bm, ALU.mult))
            link(V.tensor_tensor(t[:, 6], t[:, 6], cm, ALU.mult))
            link(V.tensor_tensor(wr[:, :, 0], wr[:, :, 0], t[:, 6], ALU.mult))
            link(V.tensor_tensor(wi[:, :, 0], wi[:, :, 0], t[:, 6], ALU.mult))
            dve.sem_inc(powers_ready, 1)
            dve.wait_ge(response_ready, 1)
            V.reduce_sum(taps[:], wr[:], AX_X).then_inc(taps_ready, 1)
            dve.wait_ge(taps_ready, 3)
            n = 0
            for j in range(N):
                for a in range(2):
                    if n >= 2:
                        dve.wait_ge(added, n - 1)
                    V.scalar_tensor_tensor(env.h4[:, a, :, j:N], x4[:, a, :, 0:N - j], taps[:, a, j:j + 1], env.h4[:, a, :, j:N],
                                           ALU.mult, ALU.add).then_inc(added, 1)
                    n += 1
            dve.wait_ge(added, 2 * N)


def stage_quantised_ffn(env, name, dram):
    nc = env.nc
    x, ps = env.x, env.ps
    NF = FF // 128
    with ExitStack() as ctx:
        def sb(n, shape, dt=F32):
            return ctx.enter_context(nc.sbuf_tensor(name + "_" + n, shape, dt))

        def sem(n):
            return env.sem(name + "_" + n)

        w1, w2 = sb("w1", [HD, 2, FF]), sb("w2", [128, NF, D])
        a1r, a2r = sb("a1r", [HD, FF]), sb("a2r", [128, D])
        m1r, m2r = sb("m1r", [128, D]), sb("m2r", [128, FF])
        q1, q2 = sb("q1", [HD, 2, FF], BF16), sb("q2", [128, NF, D], BF16)
        mean1, mean2, inv1, inv2 = (sb(n, [128, 1]) for n in ("mean1", "mean2", "inv1", "inv2"))
        s1, s2 = sb("s1", [128, NF]), sb("s2", [HD, 2])
        xt = sb("xt", [HD, 2, CW])
        xq = sb("xq", [HD, 2, 2, CW], BF16)
        g = sb("g", [128, 2, NF, CW])
        gq = sb("gq", [128, 2, NF, CW], BF16)
        y = sb("y", [HD, 2, 2, CW])
        ln = Norm(env, name + "_ln", x)
        w_in = sem("w_in")
        prep, qstep, gstep = sem("prep"), sem("x_quant_step"), sem("g_quant_step")
        up_ready, gelu_ready, down_ready, y_ready, added = (sem(n) for n in ("up_ready", "gelu_ready", "down_ready", "y_ready", "added"))
        block = ctx.enter_context(nc.Block())

        @block.sync
        def _(sp):
            sp.dma_start(w1[:], dram["w1"]).then_inc(w_in, 16)
            sp.dma_start(w2[:], dram["w2"]).then_inc(w_in, 16)
            sp.dma_start(a1r[:], dram["aw1"].broadcast_to([HD, FF])).then_inc(w_in, 16)
            sp.dma_start(a2r[:], dram["aw2"].broadcast_to([128, D])).then_inc(w_in, 16)
            sp.dma_start(m1r[:], dram["aa1"].broadcast_to([128, D])).then_inc(w_in, 16)
            sp.dma_start(m2r[:], dram["aa2"].broadcast_to([128, FF])).then_inc(w_in, 16)

        @block.tensor
        def _(pe):
            for c in range(NC):
                ln.mean(pe, c)
                ln.var(pe, c)
            pe.wait_ge(prep, PREP_STEPS)

            def up(c):
                pe.wait_ge(qstep, 3 * (c + 1))
                for f in range(NF):
                    n = c * NF + f
                    if n >= 4:
                        pe.wait_ge(gelu_ready, n - 3)
                    for a in range(2):
                        last = nc.tensor.matmul(ps[n % 4][:, 0:CW], q1[:, a, f * 128:(f + 1) * 128], xq[:, c % 2, a], start=a == 0, stop=a == 1)
                    last.then_inc(up_ready, 1)

            def down(c):
                pe.wait_ge(gstep, 4 * (c + 1))
                if c >= 2:
                    pe.wait_ge(y_ready, 2 * (c - 1))
                for m in range(2):
                    for f in range(NF):
                        last = nc.tensor.matmul(ps[4 + 2 * (c % 2) + m][0:HD, 0:CW], q2[:, f, m * HD:(m + 1) * HD], gq[:, c % 2, f],
                                                start=f == 0, stop=f == NF - 1)
                    last.then_inc(down_ready, 1)

            up(0)
            for c in range(NC):
                if c + 1 < NC:
                    up(c + 1)
                down(c)

        @block.scalar
        def _(act):
            for c in range(NC):
                ln.square(act, c)
                ln.rstd(act, c)

            def gelu(c):
                for f in range(NF):
                    n = c * NF + f
                    act.wait_ge(up_ready, n + 1)
                    if c >= 2 and f == 0:
                        act.wait_ge(gstep, 4 * (c - 1))
                    nc.scalar.activation(g[:, c % 2, f], ps[n % 4][:, 0:CW], ACT.Gelu, bias=cols(env, name + "_b1")[:, f:f + 1],
                                         scale=s1[:, f:f + 1]).then_inc(gelu_ready, 1)

            def out(c):
                for m in range(2):
                    act.wait_ge(down_ready, 2 * c + m + 1)
                    if c >= 2:
                        act.wait_ge(added, c - 1)
                    nc.scalar.activation(y[:, c % 2, m], ps[4 + 2 * (c % 2) + m][0:HD, 0:CW], ACT.Identity,
                                         bias=cols(env, name + "_b2")[0:HD, m:m + 1], scale=s2[:, m:m + 1]).then_inc(y_ready, 1)

            act.wait_ge(prep, PREP_STEPS)
            gelu(0)
            for c in range(NC):
                if c + 1 < NC:
                    gelu(c + 1)
                out(c)

        @block.gpsimd
        def _(pool):
            for c in range(NC):
                pool.wait_ge(y_ready, 2 * (c + 1))
                nc.gpsimd.tensor_tensor(chunk(env.h, c), chunk(env.h, c), y[:, c % 2], ALU.add).then_inc(added, 1)
            pool.wait_ge(added, NC)

        @block.vector
        def _(dve):
            V = nc.vector
            steps = [0]

            def link(ins):
                steps[0] += 1
                ins.then_inc(prep, 1)
                dve.wait_ge(prep, steps[0])

            ln.centre(dve, 0)
            ln.scale(dve, 0)
            dve.wait_ge(w_in, 96)
            link(V.reduce_sum(mean1[:], m1r[:], AX_X))
            link(V.tensor_scalar(mean1[:], mean1[:], 1.0 / D, None, ALU.mult))
            link(V.reciprocal(inv1[:], mean1[:]))
            link(V.reduce_sum(mean2[:], m2r[:], AX_X))
            link(V.tensor_scalar(mean2[:], mean2[:], 1.0 / FF, None, ALU.mult))
            link(V.reciprocal(inv2[:], mean2[:]))
            link(V.tensor_scalar(s1[:], cols(env, name + "_aw1"), mean1[:, 0:1], None, ALU.mult))
            link(V.tensor_scalar(s2[:], cols(env, name + "_aw2")[0:HD, :], mean2[0:HD, 0:1], None, ALU.mult))
            for w, r, q, shape in ((w1, a1r, q1, [HD, 2, FF]), (w2, a2r, q2, [128, NF, D])):
                link(V.reciprocal(r[:], r[:]))
                link(V.tensor_tensor(w[:], w[:], r[:, None, :].broadcast_to(shape), ALU.mult))
                link(V.tensor_scalar(w[:], w[:], QHI, QLO, ALU.min, ALU.max))
                link(V.tensor_scalar(w[:], w[:], ROUND, None, ALU.add))
                link(V.tensor_scalar(q[:], w[:], ROUND, None, ALU.subtract))
            assert steps[0] == PREP_STEPS, steps[0]
            for c in range(1, NC):
                ln.centre(dve, c)
                ln.scale(dve, c)

            def quant_x(c):
                dve.wait_ge(ln.ready, c + 1)
                if c >= 1:
                    dve.wait_ge(qstep, 3 * c)
                V.tensor_scalar(xt[:], chunk(x, c), inv1[0:HD, 0:1], QHI, ALU.mult, ALU.min).then_inc(qstep, 1)
                dve.wait_ge(qstep, 3 * c + 1)
                V.tensor_scalar(xt[:], xt[:], QLO, ROUND, ALU.max, ALU.add).then_inc(qstep, 1)
                dve.wait_ge(qstep, 3 * c + 2)
                if c >= 2:
                    dve.wait_ge(up_ready, NF * (c - 1))
                V.tensor_scalar(xq[:, c % 2], xt[:], ROUND, None, ALU.subtract).then_inc(qstep, 1)

            def quant_g(c):
                gc = g[:, c % 2]
                dve.wait_ge(gelu_ready, NF * (c + 1))
                V.tensor_scalar(gc, gc, 10.0, -10.0, ALU.min, ALU.max).then_inc(gstep, 1)
                dve.wait_ge(gstep, 4 * c + 1)
                V.tensor_scalar(gc, gc, inv2[:, 0:1], QHI, ALU.mult, ALU.min).then_inc(gstep, 1)
                dve.wait_ge(gstep, 4 * c + 2)
                V.tensor_scalar(gc, gc, QLO, ROUND, ALU.max, ALU.add).then_inc(gstep, 1)
                dve.wait_ge(gstep, 4 * c + 3)
                if c >= 2:
                    dve.wait_ge(down_ready, 2 * (c - 1))
                V.tensor_scalar(gq[:, c % 2], gc, ROUND, None, ALU.subtract).then_inc(gstep, 1)

            quant_x(0)
            quant_x(1)
            for c in range(NC):
                quant_g(c)
                if c + 2 < NC:
                    quant_x(c + 2)


def stage_class_ffn(env, name, dram):
    nc = env.nc
    x, ps = env.x, env.ps
    x4 = x[:, :, :].rearrange("p a (b n) -> p a b n", n=N)
    NF = FF // 128
    NPT = N - NCLS
    PI = 32
    NPS = B // PI
    PW = PI * NPT
    XW = NCLS * B
    with ExitStack() as ctx:
        def sb(n, shape, dt=F32):
            return ctx.enter_context(nc.sbuf_tensor(name + "_" + n, shape, dt))

        def sem(n):
            return env.sem(name + "_" + n)

        w1, w2 = sb("w1", [HD, 6, 2, FF]), sb("w2", [128, 6, NF, D])
        gw = sb("gw", [HD, 2, NCLS, 2])
        gwx = sb("gwx", [HD, 2, NCLS, 2, HD])
        z1 = sb("z1", [HD, NCLS, B])
        gate = sb("gate", [HD, 2, NCLS, B])
        hp = sb("hp", [128, 2, NF, PW])
        hx = sb("hx", [128, 2, NF, NCLS, B])
        wy = sb("wy", [HD, 2, 2, NCLS, B])
        ln = Norm(env, name + "_ln", x)
        gw_in, gw_spread, z_ready, z1_moved, gates_ready = (sem(n) for n in ("gw_in", "gw_spread", "z_ready", "z1_moved", "gates_ready"))
        w_in = [sem(f"w{i}_in") for i in range(6)]
        up_ready, gelu_ready, down_ready, patch_added = (sem(n) for n in ("up_ready", "gelu_ready", "down_ready", "patch_added"))
        pair_ready, gated, pair_added = sem("pair_ready"), sem("gated"), sem("pair_added")
        block = ctx.enter_context(nc.Block())
        ups = [(0, slice(2 * a, 2 * a + 2)) for a in range(3)] + [(1, slice(a, NCLS, 2)) for a in range(2)]
        downs = [(1, slice(2 * e, 2 * e + 2)) for e in range(3)] + [(0, slice(e, NCLS, 2)) for e in range(2)]
        NU = NPS * NF

        @block.sync
        def _(sp):
            sp.dma_start(gw[:], dram["gw"]).then_inc(gw_in, 16)
            for i in range(6):
                w1d = dram["p1"] if i == 0 else dram["e1"][i - 1]
                w2d = dram["p2"] if i == 0 else dram["e2"][i - 1]
                sp.dma_start(w1[:, i], w1d.rearrange("(a p) f -> p a f", p=HD)).then_inc(w_in[i], 16)
                sp.dma_start(w2[:, i], w2d.rearrange("(j p) f -> p j f", p=128)).then_inc(w_in[i], 16)

        @block.tensor
        def _(pe):
            for c in range(NC):
                ln.mean(pe, c)
                ln.var(pe, c)
            pe.wait_ge(ln.ready, NC)

            def up(s):
                for f in range(NF):
                    n = s * NF + f
                    if n >= 2:
                        pe.wait_ge(gelu_ready, n - 1)
                    for a in range(2):
                        last = nc.tensor.matmul(ps[2 + n % 2][:, 0:PW], w1[:, 0, a, f * 128:(f + 1) * 128],
                                                x4[:, a, s * PI:(s + 1) * PI, NCLS:N], start=a == 0, stop=a == 1)
                    last.then_inc(up_ready, 1)

            def down(s):
                pe.wait_ge(gelu_ready, NF * (s + 1))
                for m in range(2):
                    for f in range(NF):
                        last = nc.tensor.matmul(ps[4 + 2 * s + m][0:HD, 0:PW], w2[:, 0, f, m * HD:(m + 1) * HD], hp[:, s, f],
                                                start=f == 0, stop=f == NF - 1)
                    last.then_inc(down_ready, 1)

            pe.wait_ge(w_in[0], 32)
            up(0)
            up(1)
            down(0)
            pe.wait_ge(gw_spread, 1)
            for j in range(2):
                for i in range(NCLS):
                    for a in range(2):
                        last = nc.tensor.matmul(ps[j][0:HD, i * B:(i + 1) * B], gwx[:, a, i, j], x4[:, a, :, i], start=a == 0, stop=a == 1)
            last.then_inc(z_ready, 1)
            down(1)
            n = NU
            for e, (member, pos) in enumerate(ups):
                pe.wait_ge(w_in[1 + e], 32)
                w = B * len(range(NCLS)[pos])
                for f in range(NF):
                    pe.wait_ge(gelu_ready, n - 1)
                    for a in range(2):
                        last = nc.tensor.matmul(ps[2 + n % 2][:, 0:w], w1[:, 1 + e, a, f * 128:(f + 1) * 128],
                                                x4[:, a, :, pos].rearrange("p b n -> p n b"), start=a == 0, stop=a == 1)
                    last.then_inc(up_ready, 1)
                    n += 1
            pe.wait_ge(gelu_ready, n)
            pe.wait_ge(patch_added, 2 * NPS)
            for member in (1, 0):
                for m in range(2):
                    for e, (mem, pos) in enumerate(downs):
                        if mem != member:
                            continue
                        to = ps[4 + 2 * member + m][0:HD, 0:XW].rearrange("p (n b) -> p n b", b=B)[:, pos]
                        for f in range(NF):
                            last = nc.tensor.matmul(to, w2[:, 1 + e, f, m * HD:(m + 1) * HD], hx[:, member, f, pos],
                                                    start=f == 0, stop=f == NF - 1)
                    last.then_inc(pair_ready, 1)

        @block.scalar
        def _(act):
            act.wait_ge(gw_in, 16)
            nc.scalar.activation(gwx[:].rearrange("p a n g d -> p (a n g) d"),
                                 gw[:].rearrange("p a n g -> p (a n g)")[:, :, None].broadcast_to([HD, 4 * NCLS, HD]), ACT.Copy).then_inc(gw_spread, 1)
            for c in range(NC):
                ln.square(act, c)
                ln.rstd(act, c)
            for n in range(NU):
                act.wait_ge(up_ready, n + 1)
                s, f = n // NF, n % NF
                nc.scalar.activation(hp[:, s, f], ps[2 + n % 2][:, 0:PW], ACT.Gelu, bias=cols(env, name + "_pb1")[:, f:f + 1]).then_inc(gelu_ready, 1)
            act.wait_ge(z_ready, 1)
            nc.scalar.activation(z1[:].rearrange("p n b -> p (n b)"), ps[1][0:HD, 0:XW], ACT.Copy).then_inc(z1_moved, 1)
            n = NU
            for e, (member, pos) in enumerate(ups):
                w = B * len(range(NCLS)[pos])
                for f in range(NF):
                    act.wait_ge(up_ready, n + 1)
                    nc.scalar.activation(hx[:, member, f, pos], ps[2 + n % 2][:, 0:w].rearrange("p (n b) -> p n b", b=B), ACT.Gelu,
                                         bias=cols(env, f"{name}_eb1{e}")[:, f:f + 1]).then_inc(gelu_ready, 1)
                    n += 1

        @block.vector
        def _(dve):
            V = nc.vector
            for c in range(NC):
                ln.centre(dve, c)
                ln.scale(dve, c)
            for s in range(NPS):
                for m in range(2):
                    dve.wait_ge(down_ready, 2 * s + m + 1)
                    hc = env.h4[:, m, s * PI:(s + 1) * PI, NCLS:N]
                    V.scalar_tensor_tensor(hc, ps[4 + 2 * s + m][0:HD, 0:PW].rearrange("p (b n) -> p b n", n=NPT),
                                           cols(env, name + "_pb2")[0:HD, m:m + 1], hc, ALU.add, ALU.add).then_inc(patch_added, 1)
                if s == 0:
                    dve.wait_ge(z1_moved, 1)
                    z0 = ps[0][0:HD, 0:XW].rearrange("p (n b) -> p n b", b=B)
                    V.tensor_tensor(gate[:, 0], z0, z1[:], ALU.is_gt).then_inc(gates_ready, 1)
                    V.tensor_tensor(gate[:, 1], z0, z1[:], ALU.is_lt).then_inc(gates_ready, 1)
            dve.wait_ge(gates_ready, 2)
            ng = 0
            for k, member in enumerate((1, 0)):
                for m in range(2):
                    dve.wait_ge(pair_ready, 2 * k + m + 1)
                    for e, (mem, pos) in enumerate(downs):
                        if mem == member:
                            src = ps[4 + 2 * member + m][0:HD, 0:XW].rearrange("p (n b) -> p n b", b=B)[:, pos]
                            V.scalar_tensor_tensor(wy[:, member, m, pos], src, cols(env, f"{name}_eb2{e}")[0:HD, m:m + 1],
                                                   gate[:, member, pos], ALU.add, ALU.mult).then_inc(gated, 1)
                            ng += 1
                    hc = env.h4[:, m, :, 0:NCLS].rearrange("p b n -> p n b")
                    dve.wait_ge(gated, ng)
                    if k == 1:
                        dve.wait_ge(pair_added, m + 1)
                    V.tensor_tensor(hc, hc, wy[:, member, m], ALU.add).then_inc(pair_added, 1)
            dve.wait_ge(pair_added, 4)


def stage_top1_ffn(env, name, dram):
    nc = env.nc
    x, ps = env.x, env.ps
    NF = FF // 128
    RT = 64
    NR = T // RT
    NX = 4
    with ExitStack() as ctx:
        def sb(n, shape, dt=F32):
            return ctx.enter_context(nc.sbuf_tensor(name + "_" + n, shape, dt))

        def sem(n):
            return env.sem(name + "_" + n)

        w1, w2 = sb("w1", [HD, NX, 2, FF]), sb("w2", [128, NX, NF, D])
        wg, bg = sb("wg", [HD, 2, NX]), sb("bg", [RT, NX])
        lg, t0, t1 = (sb(n, [RT, NR, NX]) for n in ("lg", "t0", "t1"))
        r0 = sb("r0", [RT, NR])
        oht = sb("oht", [NX, T])
        oh = sb("oh", [HD, NX, T])
        g = sb("g", [128, 2, NF, CW])
        wy = sb("wy", [HD, 2, 2, CW])
        choice_dram = nc.dram_tensor(name + "_choice", (NX, T), F32).ap()
        ln = Norm(env, name + "_ln", x)
        g_in, gated, chain, turned, oh_moved, oh_out, oh_in = (sem(n) for n in ("gate_in", "gate_logits", "gate_step", "turned", "oh_moved", "oh_out", "oh_in"))
        w_in = [sem(f"w{i}_in") for i in range(NX)]
        up_ready, gelu_ready, down_ready, weighted, added = (sem(n) for n in ("up_ready", "gelu_ready", "down_ready", "weighted", "added"))
        GATE_STEPS = 9
        block = ctx.enter_context(nc.Block())

        @block.sync
        def _(sp):
            sp.dma_start(wg[:], dram["wg"]).then_inc(g_in, 16)
            sp.dma_start(bg[:], dram["bg"].broadcast_to([RT, NX])).then_inc(g_in, 16)
            for i in range(NX):
                sp.dma_start(w1[:, i], dram["w1"][i].rearrange("(a p) f -> p a f", p=HD)).then_inc(w_in[i], 16)
                sp.dma_start(w2[:, i], dram["w2"][i].rearrange("(j p) f -> p j f", p=128)).then_inc(w_in[i], 16)
            sp.wait_ge(oh_moved, 3)
            sp.dma_start(choice_dram, oht[:]).then_inc(oh_out, 16)
            sp.wait_ge(oh_out, 16)
            for i in range(NX):
                sp.dma_start(oh[:, i], choice_dram[i:i + 1, :].broadcast_to([HD, T])).then_inc(oh_in, 16)

        @block.tensor
        def _(pe):
            for c in range(NC):
                ln.mean(pe, c)
                ln.var(pe, c)
            pe.wait_ge(ln.ready, NC)
            pe.wait_ge(g_in, 32)
            for t in range(NR):
                for a in range(2):
                    last = nc.tensor.matmul(ps[1][0:RT, t * NX:(t + 1) * NX], x[:, a, t * RT:(t + 1) * RT], wg[:, a], start=a == 0, stop=a == 1)
            last.then_inc(gated, 1)

            def up(s):
                e, c = s // NC, s % NC
                if c == 0:
                    pe.wait_ge(w_in[e], 32)
                for f in range(NF):
                    n = s * NF + f
                    if n >= 2:
                        pe.wait_ge(gelu_ready, n - 1)
                    for a in range(2):
                        last = nc.tensor.matmul(ps[2 + n % 2][:, 0:CW], w1[:, e, a, f * 128:(f + 1) * 128], chunk(x, c)[:, a], start=a == 0, stop=a == 1)
                    last.then_inc(up_ready, 1)

            def down(s):
                e = s // NC
                pe.wait_ge(gelu_ready, NF * (s + 1))
                if s >= 2:
                    pe.wait_ge(weighted, 2 * (s - 1))
                for m in range(2):
                    for f in range(NF):
                        last = nc.tensor.matmul(ps[4 + 2 * (s % 2) + m][0:HD, 0:CW], w2[:, e, f, m * HD:(m + 1) * HD], g[:, s % 2, f],
                                                start=f == 0, stop=f == NF - 1)
                last.then_inc(down_ready, 1)

            up(0)
            pe.wait_ge(chain, GATE_STEPS)
            for t in range(NR):
                b = (0, 1, 4)[t // 8]
                last = nc.tensor.transpose(ps[b][0:NX, (t % 8) * RT:(t % 8 + 1) * RT], t1[:, t], env.ident[0:RT, 0:RT])
            last.then_inc(turned, 1)
            pe.wait_ge(oh_moved, 3)
            for s in range(NX * NC):
                if s + 1 < NX * NC:
                    up(s + 1)
                down(s)

        @block.scalar
        def _(act):
            for c in range(NC):
                ln.square(act, c)
                ln.rstd(act, c)

            def gelu(s):
                e = s // NC
                for f in range(NF):
                    n = s * NF + f
                    act.wait_ge(up_ready, n + 1)
                    if s >= 2 and f == 0:
                        act.wait_ge(down_ready, s - 1)
                    nc.scalar.activation(g[:, s % 2, f], ps[2 + n % 2][:, 0:CW], ACT.Gelu, bias=cols(env, f"{name}_b1{e}")[:, f:f + 1]).then_inc(gelu_ready, 1)

            gelu(0)
            act.wait_ge(turned, 1)
            for b in range(3):
                w = min(512, T - 512 * b)
                nc.scalar.activation(oht[:, 512 * b:512 * b + w], ps[(0, 1, 4)[b]][0:NX, 0:w], ACT.Copy).then_inc(oh_moved, 1)
            for s in range(1, NX * NC):
                gelu(s)

        @block.gpsimd
        def _(pool):
            for s in range(NX * NC):
                c = s % NC
                pool.wait_ge(weighted, 2 * (s + 1))
                nc.gpsimd.tensor_tensor(chunk(env.h, c), chunk(env.h, c), wy[:, s % 2], ALU.add).then_inc(added, 1)
            pool.wait_ge(added, NX * NC)

        @block.vector
        def _(dve):
            V = nc.vector
            for c in range(NC):
                ln.centre(dve, c)
                ln.scale(dve, c)
            steps = [0]

            def link(ins):
                steps[0] += 1
                ins.then_inc(chain, 1)
                dve.wait_ge(chain, steps[0])

            dve.wait_ge(gated, 1)
            link(V.tensor_tensor(lg[:], ps[1][0:RT, 0:NR * NX].rearrange("p (t e) -> p t e", e=NX),
                                 bg[:, None, :].broadcast_to([RT, NR, NX]), ALU.add))
            link(V.reduce_max(r0[:], lg[:], AX_X))
            link(V.tensor_tensor(lg[:], lg[:], r0[:, :, None].broadcast_to([RT, NR, NX]), ALU.is_equal))
            a = lg
            for sh, b in ((1, t0), (2, t1)):
                link(V.tensor_copy(b[:, :, 0:sh], a[:, :, 0:sh]))
                link(V.tensor_tensor(b[:, :, sh:], a[:, :, sh:], a[:, :, 0:NX - sh], ALU.add))
                a = b
            link(V.tensor_scalar(t1[:], t1[:], 1.0, None, ALU.is_le))
            link(V.tensor_tensor(t1[:], t1[:], lg[:], ALU.mult))
            assert steps[0] == GATE_STEPS, steps[0]
            dve.wait_ge(oh_in, 16 * NX)
            for s in range(NX * NC):
                e, c = s // NC, s % NC
                dve.wait_ge(down_ready, s + 1)
                if s >= 2:
                    dve.wait_ge(added, s - 1)
                for m in range(2):
                    V.scalar_tensor_tensor(wy[:, s % 2, m], ps[4 + 2 * (s % 2) + m][0:HD, 0:CW], cols(env, f"{name}_b2{e}")[0:HD, m:m + 1],
                                           oh[:, e, c * CW:(c + 1) * CW], ALU.add, ALU.mult).then_inc(weighted, 1)


ROUTER_STEPS = 20
PREP_STEPS = 18
ROUND = 1.5 * 2.0 ** 23
QLO, QHI = -8.0, 7.0
PI_DOWN = 3.1415925
SN = 64
NCLS = 6


def halves(v):
    return np.ascontiguousarray(np.moveaxis(np.asarray(v).reshape(2, HD, *np.shape(v)[1:]), 0, 1))


def tiles(v):
    return np.ascontiguousarray(np.asarray(v).reshape(-1, 128).T)


COLS = {}


def pack_columns(parts):
    out, at = [], 0
    for name, v in parts:
        v = np.asarray(v)
        n = v.shape[1]
        col = np.zeros((128, n), np.float32)
        col[:v.shape[0]] = v
        COLS[name] = (at, n)
        at += n
        out.append(col)
    return np.concatenate(out, 1)


def constants():
    f = np.arange(HD)
    mean_w = np.zeros((128, HD), np.float32)
    mean_w[:HD] = 1.0 / D
    head_mask = np.zeros((128, HH), np.float32)
    head_mask[:HD] = (f[:, None] // HW == np.arange(HH)[None])
    head_mean = np.zeros((128, HD), np.float32)
    head_mean[:HD] = (f[:, None] // HW == f[None] // HW) / HW
    ident = np.eye(128, dtype=np.float32)
    d = np.arange(WD)
    inv = (1.0 / np.float32(THETA) ** (np.arange(0, WD, 2, dtype=np.float32) / np.float32(WD))).astype(np.float32)
    angle = (inv[d // 2][:, None] * np.arange(N, dtype=np.float32)[None]).astype(np.float32)
    cos = np.tile(np.cos(angle), (2, 1)).astype(np.float32)
    sin = np.tile(np.sin(angle) * np.where(d % 2, 1, -1)[:, None], (2, 1)).astype(np.float32)
    causal = np.full((128, KVH * N), MASKED, np.float32)
    r = np.arange(QH // 2 * N)
    kc = np.arange(KVH * N)
    seen = ((r[:, None] // N) // (QH // KVH // 2) == kc[None] // N) & (kc[None] % N <= r[:, None] % N)
    causal[:len(r)][seen] = 0.0
    ones = np.ones((128, 2 * QB), np.float32)
    image_mask = (np.arange(128)[:, None] // SLOT == np.arange(4)[None]).astype(np.float32)
    conj = np.where(np.arange(128) < QB, 1, -1).astype(np.float32)[:, None]
    return [("ones", ones), ("image_mask", image_mask), ("conj", conj), ("cos", cos), ("sin", sin), ("causal", causal),
            ("mean_w", mean_w), ("head_mask", head_mask), ("head_mean", head_mean), ("ident", ident)]


def build(nc, d, out, stages, con_at, con_n):
    ctx = ExitStack()
    with ctx:
        env = Env(nc, ctx)
        env.h = env.sb("h", [HD, 2, T])
        env.h4 = env.h[:, :, :].rearrange("p a (b n) -> p a b n", n=N)
        env.x = env.sb("x", [HD, 2, T])
        env.x2 = env.sb("x2", [HD, 2, T])
        env.sq = env.sb("ln_sq", [HD, 2, 2, CW])
        env.rs = env.sb("ln_rs", [HD, 2, CW])
        env.ln_eps = env.sb("ln_eps", [128, 1])
        env.rms_eps = env.sb("rms_eps", [128, 1])
        env.vec = env.sb("vec", [128, d["vec"].shape[1]])
        env.vec_dram = d["vec"]
        env.vec_in = env.keep_sem("vec_in")
        env.con = env.sb("con", [128, con_n])
        env.con_dram = d["con"]
        env.con_in = env.keep_sem("con_in")

        def con(name, rows):
            a, n = con_at[name]
            return env.con[0:rows, a:a + n]
        env.mean_w, env.head_mask, env.head_mean, env.ident = con("mean_w", HD), con("head_mask", HD), con("head_mean", HD), con("ident", 128)
        env.ones, env.image_mask, env.conj = con("ones", 2 * QB), con("image_mask", 128), con("conj", 2 * QB)
        env.cos, env.sin, env.causal = con("cos", 128), con("sin", 128), con("causal", QH // 2 * N)
        env.psall = ctx.enter_context(nc.psum_tensor("banks", [128, 8, 512], F32))
        env.ps = [env.psall[:, i, :] for i in range(8)]

        def of(name):
            return {n[len(name) + 1:]: ap for n, ap in d.items() if n.startswith(name + "_")}

        plan = [lambda: stage_tokens(env, d["patches"], d["tok_w"], d["tok_pos"]),
                lambda: stage_narrow_attention(env, "a0", of("a0"), rms=True),
                lambda: stage_wide_attention(env, "g0", of("g0")),
                lambda: stage_experts(env, "moe", of("moe")),
                lambda: stage_convolution(env, "s1", of("s1")),
                lambda: stage_quantised_ffn(env, "f1", of("f1")),
                lambda: stage_narrow_attention(env, "a2", of("a2")),
                lambda: stage_class_ffn(env, "f2", of("f2")),
                lambda: stage_narrow_attention(env, "a3", of("a3"), quantum=True),
                lambda: stage_top1_ffn(env, "f3", of("f3"))]
        for stage in plan[:stages]:
            stage()
            env.end_stage()

        stored = env.sem("out_stored")
        with nc.Block() as block:
            @block.sync
            def _(sp):
                sp.dma_start(out, env.h[:]).then_inc(stored, 16)
                sp.wait_ge(stored, 16)


def prepare(inp):
    g = {k: np.asarray(v) for k, v in inp.items()}
    x = g["x"].reshape(NC, IC, 4, 16, 4, 16, 3)
    px = x.transpose(3, 5, 6, 0, 1, 2, 4).reshape(KP, 128, NC, IC * NP)
    a = {"patches": np.ascontiguousarray(px.transpose(2, 1, 0, 3)),
         "tok_w": np.ascontiguousarray(g["L0_tok_W"].reshape(KP, 128, D).transpose(1, 0, 2)),
         "tok_pos": halves(g["L0_tok_pos_emb"].T)}
    a["a0_wqkv"] = halves(g["L0_attn_qkv_w"].T)
    a["a0_wo"] = halves(g["L0_attn_proj_w"].T)
    w = g["L0_ffn_w_qkv"]
    a["g0_wq"] = halves(w[:, 0:QH * WD])
    wk = w[:, QH * WD:(QH + KVH) * WD].reshape(D, KVH, 1, WD)
    a["g0_wk"] = halves(np.broadcast_to(wk, (D, KVH, 2, WD)).reshape(D, KVH * 2 * WD))
    a["g0_wv"] = halves(w[:, (QH + KVH) * WD:])
    a["g0_wo"] = np.ascontiguousarray(g["L0_ffn_w_out"].reshape(QH // 2, 128, D).transpose(1, 0, 2))
    a["moe_wr"] = halves(g["L0_ffn_w_router"])
    a["moe_gate_up"], a["moe_down"] = g["L0_ffn_w_gate_up"], g["L0_ffn_w_down"]
    b = g["L0_attn_qkv_b"]
    a["s1_prm"] = np.ascontiguousarray(np.stack([halves(g["L1_attn_" + n]) for n in ("A_real", "A_imag", "B_mat", "C_mat")], 1))
    a["f1_w1"] = halves(g["L1_ffn_w1"].T)
    a["f1_w2"] = np.ascontiguousarray(g["L1_ffn_w2"].T.reshape(FF // 128, 128, D).transpose(1, 0, 2))
    for n, src in (("aw1", "alpha_w1"), ("aw2", "alpha_w2"), ("aa1", "alpha_a1"), ("aa2", "alpha_a2")):
        a["f1_" + n] = g["L1_ffn_" + src][None]
    a["a2_wqkv"], a["a2_wo"] = halves(g["L2_attn_qkv_w"].T), halves(g["L2_attn_proj_w"].T)
    a["f2_p1"], a["f2_p2"], a["f2_e1"], a["f2_e2"] = (g["L2_ffn_" + n] for n in ("moe0_W1", "moe0_W2", "A1_W", "A2_W"))
    a["f2_gw"] = halves(g["L2_ffn_G_W"].transpose(1, 0, 2))
    a["a3_wqkv"], a["a3_wo"] = halves(g["L3_attn_in_w"].T), halves(g["L3_attn_out_w"].T)
    swap = np.r_[8:16, 0:8]
    a["a3_wsp"] = halves(np.concatenate([g["L3_attn_sp_w"].T, g["L3_attn_sp_w"].T[:, swap]], 1))
    a["a3_qw"] = g["L3_attn_qw"].reshape(1, 1)
    a["f3_wg"], a["f3_bg"], a["f3_w1"], a["f3_w2"] = halves(g["L3_ffn_Wg"]), g["L3_ffn_bg"][None], g["L3_ffn_W1"], g["L3_ffn_W2"]
    more = [("s1_ld", halves(g["L1_attn_log_delta"])), ("f1_b1", tiles(g["L1_ffn_b1"])), ("f1_aw1", tiles(g["L1_ffn_alpha_w1"])),
            ("f1_b2", halves(g["L1_ffn_b2"])), ("f1_aw2", halves(g["L1_ffn_alpha_w2"])),
            ("f2_pb1", tiles(g["L2_ffn_moe0_b1"])), ("f2_pb2", halves(g["L2_ffn_moe0_b2"])),
            ("a3_spb", g["L3_attn_sp_b"][:, None]), ("a3_spbx", g["L3_attn_sp_b"][swap][:, None])]
    for e in range(5):
        more += [(f"f2_eb1{e}", tiles(g["L2_ffn_A1_b"][e])), (f"f2_eb2{e}", halves(g["L2_ffn_A2_b"][e]))]
    for e in range(4):
        more += [(f"f3_b1{e}", tiles(g["L3_ffn_b1"][e])), (f"f3_b2{e}", halves(g["L3_ffn_b2"][e]))]
    for n, bias, out in (("a2", g["L2_attn_qkv_b"], g["L2_attn_proj_b"]), ("a3", g["L3_attn_in_b"], g["L3_attn_out_b"])):
        more += [(f"{n}_{v}b", halves(bias[i * D:(i + 1) * D])) for i, v in enumerate("qkv")] + [(n + "_ob", halves(out))]
    parts = more + [("tok_b", halves(g["L0_tok_b"])), ("cls", halves(g["cls_tok"].reshape(D))),
             ("a0_qb", halves(b[0:D])), ("a0_kb", halves(b[D:2 * D])), ("a0_vb", halves(b[2 * D:])),
             ("n1w", halves(g["L0_ffn_norm1_w"])), ("n2w", halves(g["L0_ffn_norm2_w"])),
             ("a0_ob", halves(g["L0_attn_proj_b"])),
             ("a0_qn", np.tile(g["L0_attn_q_norm_w"], HH)[:, None]), ("a0_kn", np.tile(g["L0_attn_k_norm_w"], HH)[:, None])]
    a["vec"] = pack_columns(parts)
    cons = constants()
    at, con_at = 0, {}
    for n, v in cons:
        con_at[n] = (at, v.shape[1])
        at += v.shape[1]
    a["con"] = np.concatenate([v for _, v in cons], 1)
    return a, con_at, at


STAGES = 99


def kernel(**inputs):
    import concourse.bacc as _bacc
    from concourse.bass_utils import run_bass_kernel_spmd as _run

    nc = _bacc.Bacc("TRN2", target_bir_lowering=False, num_devices=1)
    arrays, con_at, con_n = prepare(inputs)
    arrays = {"in_" + n: a for n, a in arrays.items()}
    d = {n[3:]: nc.dram_tensor(n, a.shape, mybir.dt.from_np(a.dtype), kind="ExternalInput").ap() for n, a in arrays.items()}
    out = nc.dram_tensor("out", (HD, 2, T), F32, kind="ExternalOutput").ap()
    build(nc, d, out, STAGES, con_at, con_n)
    r = _run(nc, [arrays], core_ids=[0])
    got = np.asarray(r.results[0]["out"])
    return np.ascontiguousarray(got.transpose(2, 1, 0)).reshape(B, N, D)
```

```python
from contextlib import ExitStack

import numpy as np

import concourse.bass as bass
from concourse import mybir
from concourse.alu_op_type import AluOpType as ALU

F32 = mybir.dt.float32
BF16 = mybir.dt.bfloat16
I32 = mybir.dt.int32
U32 = mybir.dt.uint32
ACT = mybir.ActivationFunctionType
AX_X = mybir.AxisListType.X

B = 64
NP = 16
N = NP + 1
T = B * N
D = 192
HD = 96
HN = 12
HW = 16
HH = HN // 2
NC = 4
IC = B // NC
CW = IC * N
GI = 8
GPC = IC // GI
NG = B // GI
GW = GI * N
SLOT = 32
PD = 768
KP = PD // 128
LN_EPS = 1e-5
RMS_EPS = 1e-6
FF = 768
QH = 12
KVH = 3
WD = 64
THETA = 10000.0
QB = 8
QR = 3 * SLOT + N
NE = 16
EF = 384
NX = 4
MOE_TILES = (2 * T + NE * 127) // 128
TOP1_TILES = (T + NX * 127) // 128
MASKED = -1e30


class Env:

    def __init__(self, nc, ctx):
        self.nc, self.ctx, self.of_stage = nc, ctx, []

    def sb(self, name, shape, dt=F32):
        return self.ctx.enter_context(self.nc.sbuf_tensor(name, shape, dt))

    def keep_sem(self, name):
        return self.ctx.enter_context(self.nc.semaphore(name))

    def sem(self, name):
        self.of_stage.append(self.nc.alloc_semaphore(name))
        return self.of_stage[-1]

    def end_stage(self):
        self.nc.clear_and_free_semaphores(self.of_stage)
        self.of_stage = []
        self.nc.all_engine_barrier()


def cols(env, name):
    a, n = COLS[name]
    return env.vec[:, a:a + n]


def chunk(ap3, c):
    return ap3[:, :, c * CW:(c + 1) * CW]


class Norm:

    def __init__(self, env, name, x):
        self.env, self.x = env, x
        self.mean_ready = env.sem(name + "_mean_ready")
        self.centred = env.sem(name + "_centred")
        self.squared = env.sem(name + "_squared")
        self.var_ready = env.sem(name + "_var_ready")
        self.log_var = env.sem(name + "_log_var")
        self.rstd_ready = env.sem(name + "_rstd_ready")
        self.ready = env.sem(name + "_x_ready")

    def mean(self, pe, c):
        if c > 0:
            pe.wait_ge(self.log_var, c)
        nc, env = self.env.nc, self.env
        for a in range(2):
            last = nc.tensor.matmul(env.ps[0][0:HD, 0:CW], env.mean_w, chunk(env.h, c)[:, a], start=a == 0, stop=a == 1)
        last.then_inc(self.mean_ready, 1)

    def var(self, pe, c):
        nc, env = self.env.nc, self.env
        pe.wait_ge(self.centred, c + 1)
        pe.wait_ge(self.squared, c + 1)
        for a in range(2):
            last = nc.tensor.matmul(env.ps[0][0:HD, 0:CW], env.mean_w, env.sq[:, c % 2, a], start=a == 0, stop=a == 1)
        last.then_inc(self.var_ready, 1)

    def centre(self, dve, c):
        nc, env = self.env.nc, self.env
        dve.wait_ge(self.mean_ready, c + 1)
        nc.vector.tensor_tensor(chunk(self.x, c), chunk(env.h, c), env.ps[0][0:HD, None, 0:CW].broadcast_to([HD, 2, CW]),
                                ALU.subtract).then_inc(self.centred, 1)

    def square(self, act, c):
        nc, env = self.env.nc, self.env
        act.wait_ge(self.centred, c + 1)
        if c >= 2:
            act.wait_ge(self.var_ready, c - 1)
        nc.scalar.activation(env.sq[:, c % 2], chunk(self.x, c), ACT.Square).then_inc(self.squared, 1)

    def rstd(self, act, c):
        nc, env = self.env.nc, self.env
        act.wait_ge(self.var_ready, c + 1)
        if c >= 2:
            act.wait_ge(self.ready, c - 1)
        nc.scalar.activation(env.rs[:, c % 2], env.ps[0][0:HD, 0:CW], ACT.Ln, bias=env.ln_eps[0:HD, :]).then_inc(self.log_var, 1)
        act.wait_ge(self.log_var, c + 1)
        nc.scalar.activation(env.rs[:, c % 2], env.rs[:, c % 2], ACT.Exp, scale=-0.5).then_inc(self.rstd_ready, 1)

    def scale(self, dve, c):
        nc, env = self.env.nc, self.env
        dve.wait_ge(self.rstd_ready, c + 1)
        nc.vector.tensor_tensor(chunk(self.x, c), chunk(self.x, c), env.rs[:, c % 2, None, :].broadcast_to([HD, 2, CW]),
                                ALU.mult).then_inc(self.ready, 1)


def stage_tokens(env, patches, w, pos):
    nc = env.nc
    with ExitStack() as ctx:
        px = ctx.enter_context(nc.sbuf_tensor("patch_px", [128, NC, KP, IC * NP], F32))
        ws = ctx.enter_context(nc.sbuf_tensor("patch_w", [128, KP, D], F32))
        posb = ctx.enter_context(nc.sbuf_tensor("patch_pos", [HD, 2, NP], F32))
        zero = ctx.enter_context(nc.sbuf_tensor("slots_zeros", [128, D], F32))
        w_in, pos_in, zero_ready = env.sem("tok_w_in"), env.sem("tok_pos_in"), env.sem("zero_ready")
        px_in = [env.sem(f"tok_px{c}_in") for c in range(NC)]
        posb_ready, embedded, cls_in, placed = (env.sem("tok_" + n) for n in ("posb_ready", "embedded", "cls_placed", "placed"))
        block = ctx.enter_context(nc.Block())

        @block.sync
        def _(sp):
            sp.dma_start(ws[:], w).then_inc(w_in, 16)
            for c in range(NC):
                sp.dma_start(px[:, c], patches[c]).then_inc(px_in[c], 16)
            sp.wait_ge(zero_ready, 1)
            sp.dma_start(env.x_slots.rearrange("(t p) f -> p t f", p=128), zero[:, None, :].broadcast_to([128, MOE_TILES, D]))\
                .then_inc(env.slots_zero, 16)
            sp.wait_ge(env.slots_zero, 16)

        @block.scalar
        def _(act):
            act.preload_act_table_set("natural_log_exp_and_others")
            act.dma_start(env.vec[:], env.vec_dram).then_inc(env.vec_in, 16)
            act.dma_start(posb[:], pos).then_inc(pos_in, 16)
            act.dma_start(env.con[:], env.con_dram).then_inc(env.con_in, 16)
            act.wait_ge(env.vec_in, 16)
            c3 = cols(env, "cls")[0:HD, :]
            nc.scalar.activation(env.h4[:, :, :, 0], c3[:, :, None].broadcast_to([HD, 2, B]), ACT.Copy).then_inc(cls_in, 1)
            act.wait_ge(cls_in, 1)

        @block.gpsimd
        def _(pool):
            pool.memset(zero[:], 0.0).then_inc(zero_ready, 1)
            pool.memset(env.ln_eps[:], LN_EPS)
            pool.memset(env.rms_eps[:], RMS_EPS)

        @block.tensor
        def _(pe):
            pe.wait_ge(w_in, 16)
            for c in range(NC):
                pe.wait_ge(px_in[c], 16)
                for m in range(2):
                    for k in range(KP):
                        last = nc.tensor.matmul(env.ps[2 * c + m][0:HD, 0:IC * NP], ws[:, k, m * HD:(m + 1) * HD],
                                                px[:, c, k], start=k == 0, stop=k == KP - 1)
                    last.then_inc(embedded, 1)

        @block.vector
        def _(dve):
            dve.wait_ge(env.vec_in, 16)
            dve.wait_ge(pos_in, 16)
            tb = cols(env, "tok_b")[0:HD, :]
            nc.vector.tensor_tensor(posb[:], posb[:], tb[:, :, None].broadcast_to([HD, 2, NP]), ALU.add).then_inc(posb_ready, 1)
            dve.wait_ge(posb_ready, 1)
            for c in range(NC):
                for m in range(2):
                    dve.wait_ge(embedded, 2 * c + m + 1)
                    src = env.ps[2 * c + m][0:HD, 0:IC * NP].rearrange("p (i n) -> p i n", n=NP)
                    nc.vector.tensor_tensor(env.h4[:, m, c * IC:(c + 1) * IC, 1:N], src,
                                            posb[:, m, None, :].broadcast_to([HD, IC, NP]), ALU.add).then_inc(placed, 1)
            dve.wait_ge(placed, 2 * NC)


def stage_narrow_attention(env, name, dram, rms=False, quantum=False):
    nc = env.nc
    x, ps = env.x, env.ps
    HP = HN + 1 if quantum else HN
    with ExitStack() as ctx:
        def sb(n, shape, dt=F32):
            return ctx.enter_context(nc.sbuf_tensor(name + "_" + n, shape, dt))

        def sem(n):
            return env.sem(name + "_" + n)

        wqkv = sb("wqkv", [HD, 2, 3 * D])
        wo = sb("wo", [HD, 2, D])
        q = sb("q", [HD, 2, 2, CW + SLOT - N])
        k = sb("k", [HD, 2, 2, CW])
        kx = sb("kx", [HD, 2, 2, IC, HH * N])
        vx = sb("vx", [HD, 2, 2, IC, HH * N])
        vt = sb("vt", [HH * N, 2, GI, 2, HD])
        p = sb("p", [128, 2, 2, HP * N])
        pt = sb("pt", [HH * N, 2, 4, 128])
        mx = sb("mx", [128, 2, 2, HP])
        sm = sb("sm", [128, 2, 2, HP])
        cx = sb("cx", [HD, 2, 2, CW])
        w_in, gate_in = sem("w_in"), sem("gate_in")
        ln = Norm(env, name + "_ln", x)
        pad_zero = sem("pad_zero")
        proj = [sem(f"{n}_proj") for n in "qkvo"]
        qk_evicted, k_spread, v_spread = sem("qk_evicted"), sem("k_spread"), sem("v_spread")
        if rms:
            rsq = sb("rsq", [HD, 2, CW])
            rrs = sb("rrs", [HD, 2, CW])
            raw_evicted, head_sq, head_ms, head_log, head_rstd, head_scaled = (
                sem(n) for n in ("raw_evicted", "head_squared", "head_ms", "head_log", "head_rstd", "head_scaled"))
        if quantum:
            wsp = sb("wsp", [HD, 2, 4 * QB])
            st = sb("st", [2 * QB, 2, 2, CW + SLOT - N])
            ssq, srs = sb("ssq", [2 * QB, CW]), sb("srs", [2 * QB, CW])
            osq = sb("osq", [128, 2, 2, 2, N])
            px = sb("px", [128, 2, 2, 4, N])
            xt = sb("xt", [4 * N, 2, 2, 2, HD])
            qt = sb("qt", [4 * N, 2, 2, 128])
            gate = sb("gate", [128, 2])
            gated_b = sb("gated_b", [HD, 2, 2])
            tiny = sb("tiny", [128, 2])
            (s_proj, s_taken, s_squared, s_norm, s_factor, s_scaled, ov_squared, fid_ready, spread, qt_ready, qt_moved, gate_step,
             weighted) = (sem(n) for n in (
                 "s_proj", "s_taken", "s_squared", "s_norm", "s_factor", "s_scaled", "overlap_squared", "fidelity_ready",
                 "q_spread", "qt_ready", "qt_moved", "gate_step", "sm_weighted"))
        FV = GI // 2 + (1 if quantum else 0)
        scored, vt_ready, vt_evicted = sem("scored"), sem("vt_ready"), sem("vt_evicted")
        maxed, shifted, expd, summed, inverted, normed = (sem(n) for n in ("maxed", "shifted", "expd", "summed", "inverted", "normed"))
        pt_ready, pt_evicted, ctx_ready, ctx_evicted, added = (sem(n) for n in ("pt_ready", "pt_evicted", "ctx_ready", "ctx_evicted", "added"))
        block = ctx.enter_context(nc.Block())
        NT = 4

        @block.sync
        def _(sp):
            sp.dma_start(wqkv[:], dram["wqkv"]).then_inc(w_in, 16)
            sp.dma_start(wo[:], dram["wo"]).then_inc(w_in, 16)
            if quantum:
                sp.dma_start(wsp[:], dram["wsp"]).then_inc(w_in, 16)
                sp.dma_start(gate[:, 0:1], dram["qw"].broadcast_to([128, 1])).then_inc(gate_in, 16)

        @block.tensor
        def _(pe):
            if name == "a0":
                pe.wait_ge(env.con_in, 16)

            def project(c):
                pe.wait_ge(ln.ready, c + 1)
                raw = raw_evicted if rms else qk_evicted
                for j in range(3):
                    for m in range(2):
                        if j == 0 and c == 1:
                            pe.wait_ge(s_taken if quantum else v_spread, m + 1)
                        if j == 0 and c >= 2:
                            pe.wait_ge(added, 2 * (c - 2) + m + 1)
                        if j >= 1:
                            pe.wait_ge(raw, NT * c + 2 * (j - 1) + m + 1)
                        for a in range(2):
                            last = nc.tensor.matmul(ps[2 + m][0:HD, 0:CW], wqkv[:, a, j * D + m * HD:j * D + (m + 1) * HD],
                                                    chunk(x, c)[:, a], start=a == 0, stop=a == 1)
                        last.then_inc(proj[j], 1)
                        if rms and j >= 1:
                            head_mean_square(NT * c + 2 * (j - 1) + m)
                if quantum:
                    states(c)

            def states(c):
                for m in range(2):
                    pe.wait_ge(v_spread, 2 * c + m + 1)
                    for a in range(2):
                        last = nc.tensor.matmul(ps[2 + m][0:2 * QB, 0:CW], wsp[:, a, m * 2 * QB:(m + 1) * 2 * QB],
                                                chunk(x, c)[:, a], start=a == 0, stop=a == 1)
                    last.then_inc(s_proj, 1)
                pe.wait_ge(s_squared, c + 1)
                pe.wait_ge(ln.log_var, min(NC, c + 2))
                if c >= 1:
                    pe.wait_ge(s_factor, 4 * c - 3)
                if c >= 2:
                    pe.wait_ge(qt_moved, GPC * (c - 1))
                nc.tensor.matmul(ps[0][0:2 * QB, 0:CW], env.ones[0:2 * QB, 0:2 * QB], ssq[:], start=True, stop=True).then_inc(s_norm, 1)

            def head_mean_square(t):
                pe.wait_ge(head_sq, t + 1)
                if t % NT == 0:
                    pe.wait_ge(ln.log_var, min(NC, t // NT + 2))
                if t > 0:
                    pe.wait_ge(head_log, t)
                nc.tensor.matmul(ps[0][0:HD, 0:CW], env.head_mean, rsq[:, t % 2], start=True, stop=True).then_inc(head_ms, 1)

            def scores(g):
                c = g // GPC
                pe.wait_ge(head_scaled if rms else qk_evicted, NT * c + NT)
                pe.wait_ge(k_spread, 2 * c + 2)
                if quantum:
                    pe.wait_ge(s_scaled, 2 * c + 2)
                if g >= 1:
                    pe.wait_ge(shifted, g)
                for i in range(GI):
                    i16 = (g % GPC) * GI + i
                    for a in range(2):
                        o = (i // 4) * HN * N + a * HH * N
                        last = nc.tensor.matmul(ps[4][SLOT * (i % 4):SLOT * (i % 4 + 1), o:o + HH * N],
                                                q[:, c % 2, a, i16 * N:i16 * N + SLOT], kx[:, c % 2, a, i16, :],
                                                start=True, stop=True)
                    if quantum:
                        o = 2 * HN * N + (i // 4) * 2 * N
                        last = nc.tensor.matmul(ps[4][SLOT * (i % 4):SLOT * (i % 4 + 1), o:o + 2 * N],
                                                st[:, c % 2, 0, i16 * N:i16 * N + SLOT], st[:, c % 2, :, i16 * N:(i16 + 1) * N],
                                                start=True, stop=True)
                last.then_inc(scored, 1)

            def turn_values(g):
                c = g // GPC
                pe.wait_ge(v_spread, 2 * c + 2)
                for f in range(GI // 2):
                    n = g * FV + f
                    if n >= 2:
                        pe.wait_ge(vt_evicted, n - 1)
                    for i in range(2):
                        for a in range(2):
                            o = (2 * i + a) * HD
                            last = nc.tensor.transpose(ps[5 + n % 2][0:HH * N, o:o + HD],
                                                       vx[:, c % 2, a, (g % GPC) * GI + 2 * f + i, :], env.ident[0:HD, 0:HD])
                    last.then_inc(vt_ready, 1)
                if quantum:
                    n = g * FV + FV - 1
                    pe.wait_ge(vt_evicted, n - 1)
                    for f in range(2):
                        for a in range(2):
                            o = (g * GI + 4 * f) * N
                            last = nc.tensor.transpose(ps[5 + n % 2][0:4 * N, (2 * f + a) * HD:(2 * f + a + 1) * HD],
                                                       x[:, a, o:o + 4 * N], env.ident[0:HD, 0:HD])
                    last.then_inc(vt_ready, 1)

            def weigh(g):
                c = g // GPC
                pe.wait_ge(normed, g + 1)
                if g >= 1:
                    pe.wait_ge(pt_evicted, g)
                for f in range(2):
                    for a in range(2):
                        j = 2 * f + a
                        last = nc.tensor.transpose(ps[7][0:HH * N, j * 128:(j + 1) * 128],
                                                   p[:, g % 2, f, a * HH * N:(a + 1) * HH * N], env.ident)
                last.then_inc(pt_ready, 1)
                if quantum:
                    pe.wait_ge(spread, g + 1)
                    pe.wait_ge(s_factor, 4 * min(NC, c + 2) - 3)
                    pe.wait_ge(ln.log_var, min(NC, c + 3))
                    if g >= 1:
                        pe.wait_ge(qt_moved, g)
                    for f in range(2):
                        last = nc.tensor.transpose(ps[0][0:4 * N, f * 128:f * 128 + QR],
                                                   px[0:QR, g % 2, f].rearrange("p i k -> p (i k)"), env.ident[0:QR, 0:QR])
                    last.then_inc(qt_ready, 1)
                pe.wait_ge(pt_evicted, g + 1)
                pe.wait_ge(vt_evicted, (g + 1) * FV)
                if g >= 1:
                    pe.wait_ge(ctx_evicted, 2 * g)
                for i in range(GI):
                    for a in range(2):
                        o = a * GW + i * N
                        last = nc.tensor.matmul(ps[1][0:HD, o:o + N], vt[:, g % 2, i, a, :],
                                                pt[:, g % 2, 2 * (i // 4) + a, SLOT * (i % 4):SLOT * (i % 4) + N],
                                                start=True, stop=True)
                last.then_inc(ctx_ready, 1)

            def project_out(c):
                pe.wait_ge(ctx_evicted, 2 * GPC * (c + 1))
                for m in range(2):
                    pe.wait_ge(s_taken if quantum else v_spread, 2 * min(c + 1, NC - 1) + m + 1)
                    if quantum:
                        pe.wait_ge(qt_moved, GPC * (c + 1))
                    if c == NC - 1:
                        pe.wait_ge(added, 2 * (c - 1) + m + 1)
                    for a in range(2):
                        last = nc.tensor.matmul(ps[2 + m][0:HD, 0:CW], wo[:, a, m * HD:(m + 1) * HD], cx[:, c % 2, a],
                                                start=a == 0, stop=a == 1 and not quantum)
                    for f in range(2 * GPC if quantum else 0):
                        last = nc.tensor.matmul(ps[2 + m][0:HD, f * 4 * N:(f + 1) * 4 * N], xt[:, f // 2, f % 2, m],
                                                qt[:, f // 2, f % 2].rearrange("p (i n) -> p i n", n=SLOT)[:, :, 0:N],
                                                start=False, stop=f == 2 * GPC - 1)
                    last.then_inc(proj[3], 1)

            for c in range(2):
                ln.mean(pe, c)
                ln.var(pe, c)
            pe.wait_ge(w_in, 48 if quantum else 32)
            project(0)
            for c in range(NC):
                if c + 2 < NC:
                    if rms:
                        pe.wait_ge(head_log, NT * (c + 1))
                    if quantum:
                        pe.wait_ge(s_factor, 4 * c + 1)
                        if c >= 1:
                            pe.wait_ge(qt_moved, GPC * c)
                    ln.mean(pe, c + 2)
                for g in (2 * c, 2 * c + 1):
                    scores(g)
                    turn_values(g)
                if c + 2 < NC:
                    ln.var(pe, c + 2)
                if c + 1 < NC:
                    project(c + 1)
                for g in (2 * c, 2 * c + 1):
                    weigh(g)
                project_out(c)

        @block.scalar
        def _(act):
            pre = name

            def take_qk(c):
                for j in range(2):
                    for m in range(2):
                        t = NT * c + 2 * j + m
                        act.wait_ge(proj[j], 2 * c + m + 1)
                        if c >= 2 and j == 0:
                            act.wait_ge(scored, GPC * (c - 1))
                        if c >= 2 and j == 1:
                            act.wait_ge(k_spread, 2 * (c - 1))
                        dst = (q if j == 0 else k)[:, c % 2, m, 0:CW]
                        bias = cols(env, pre + ("_qb" if j == 0 else "_kb"))[0:HD, m:m + 1]
                        nc.scalar.activation(dst, ps[2 + m][0:HD, 0:CW], ACT.Identity, bias=bias)\
                            .then_inc(raw_evicted if rms else qk_evicted, 1)
                        if rms:
                            act.wait_ge(raw_evicted, t + 1)
                            if t >= 2:
                                act.wait_ge(head_ms, t - 1)
                            nc.scalar.activation(rsq[:, t % 2], dst, ACT.Square).then_inc(head_sq, 1)
                            if t % NT:
                                head_rms(t - 1)
                if rms:
                    head_rms(NT * c + NT - 1)
                if quantum:
                    take_states(c)

            def take_states(c):
                for m in range(2):
                    act.wait_ge(s_proj, 2 * c + m + 1)
                    if c >= 2:
                        act.wait_ge(scored, GPC * (c - 1))
                    nc.scalar.activation(st[:, c % 2, m, 0:CW], ps[2 + m][0:2 * QB, 0:CW], ACT.Identity,
                                         bias=cols(env, name + ("_spb", "_spbx")[m])[0:2 * QB, :]).then_inc(s_taken, 1)
                act.wait_ge(s_taken, 2 * c + 1)
                if c >= 1:
                    act.wait_ge(s_norm, c)
                nc.scalar.activation(ssq[:], st[:, c % 2, 0, 0:CW], ACT.Square).then_inc(s_squared, 1)
                act.wait_ge(s_norm, c + 1)
                if c >= 1:
                    act.wait_ge(s_scaled, 2 * c)
                nc.scalar.activation(srs[:], ps[0][0:2 * QB, 0:CW], ACT.Ln, bias=tiny[0:2 * QB, 0:1]).then_inc(s_factor, 1)
                act.wait_ge(s_factor, 4 * c + 1)
                nc.scalar.activation(srs[:], srs[:], ACT.Exp, scale=0.5).then_inc(s_factor, 1)
                act.wait_ge(s_factor, 4 * c + 2)
                nc.scalar.activation(srs[:], srs[:], ACT.Ln, bias=tiny[0:2 * QB, 1:2]).then_inc(s_factor, 1)
                act.wait_ge(s_factor, 4 * c + 3)
                nc.scalar.activation(srs[:], srs[:], ACT.Exp, scale=-1.0).then_inc(s_factor, 1)

            def square_overlaps(g):
                act.wait_ge(scored, g + 1)
                if g >= 2:
                    act.wait_ge(fid_ready, g - 1)
                nc.scalar.activation(osq[:, g % 2].rearrange("p f e k -> p (f e k)"), ps[4][:, 2 * HN * N:2 * HN * N + 4 * N],
                                     ACT.Square, scale=HW ** 0.25).then_inc(ov_squared, 1)

            def head_rms(t):
                act.wait_ge(head_ms, t + 1)
                if t >= 2:
                    act.wait_ge(head_scaled, t - 1)
                nc.scalar.activation(rrs[:, t % 2], ps[0][0:HD, 0:CW], ACT.Ln, bias=env.rms_eps[0:HD, :]).then_inc(head_log, 1)
                act.wait_ge(head_log, t + 1)
                nc.scalar.activation(rrs[:, t % 2], rrs[:, t % 2], ACT.Exp, scale=-0.5).then_inc(head_rstd, 1)

            def take_values(g):
                for f in range(GI // 2):
                    n = g * FV + f
                    act.wait_ge(vt_ready, n + 1)
                    if g >= 2 and f == 0:
                        act.wait_ge(ctx_ready, g - 1)
                    nc.scalar.activation(vt[:, g % 2, 2 * f:2 * f + 2].rearrange("p i a f -> p (i a f)"),
                                         ps[5 + n % 2][0:HH * N, 0:4 * HD], ACT.Copy).then_inc(vt_evicted, 1)
                if quantum:
                    n = g * FV + FV - 1
                    act.wait_ge(vt_ready, n + 1)
                    if g >= 2:
                        act.wait_ge(proj[3], 2 * (g // GPC))
                    nc.scalar.activation(xt[:, g % 2].rearrange("p f a d -> p (f a d)"), ps[5 + n % 2][0:4 * N, 0:4 * HD],
                                         ACT.Copy).then_inc(vt_evicted, 1)

            def exponent(g):
                act.wait_ge(shifted, g + 1)
                nc.scalar.activation(p[:, g % 2], p[:, g % 2], ACT.Exp, scale=HW ** -0.5).then_inc(expd, 1)

            def take_context(g):
                c = g // GPC
                act.wait_ge(pt_ready, g + 1)
                if g >= 2:
                    act.wait_ge(ctx_ready, g - 1)
                nc.scalar.activation(pt[:, g % 2].rearrange("p a b -> p (a b)"), ps[7][0:HH * N, 0:512], ACT.Copy).then_inc(pt_evicted, 1)
                if quantum:
                    act.wait_ge(qt_ready, g + 1)
                    if g >= 2:
                        act.wait_ge(proj[3], 2 * c)
                    nc.scalar.activation(qt[:, g % 2, :, 0:QR], ps[0][0:4 * N, 0:256].rearrange("p (f q) -> p f q", f=2)[:, :, 0:QR],
                                         ACT.Copy).then_inc(qt_moved, 1)
                act.wait_ge(ctx_ready, g + 1)
                if c >= 2:
                    act.wait_ge(proj[3], 2 * (c - 1))
                for a in range(2):
                    o = (g % GPC) * GW
                    bias, scale = (gated_b[:, 0, a:a + 1], gate[0:HD, 1:2]) if quantum else (cols(env, pre + "_vb")[0:HD, a:a + 1], 1.0)
                    nc.scalar.activation(cx[:, c % 2, a, o:o + GW], ps[1][0:HD, a * GW:(a + 1) * GW], ACT.Identity,
                                         bias=bias, scale=scale).then_inc(ctx_evicted, 1)

            act.preload_act_table_set("natural_log_exp_and_others")
            if quantum:
                act.wait_ge(gate_in, 16)
                nc.scalar.activation(gate[:, 0:1], gate[:, 0:1], ACT.Exp, scale=-1.0).then_inc(gate_step, 1)
            for c in range(2):
                ln.square(act, c)
                ln.rstd(act, c)
            act.wait_ge(pad_zero, 3 if quantum else 1)
            if quantum:
                act.wait_ge(gate_step, 5)
            take_qk(0)
            for c in range(NC):
                if c + 2 < NC:
                    ln.square(act, c + 2)
                for g in (2 * c, 2 * c + 1):
                    if quantum:
                        square_overlaps(g)
                    take_values(g)
                    exponent(g)
                if c + 2 < NC:
                    ln.rstd(act, c + 2)
                if c + 1 < NC:
                    take_qk(c + 1)
                for g in (2 * c, 2 * c + 1):
                    take_context(g)

        @block.gpsimd
        def _(pool):
            pool.memset(q[:, :, :, CW:], 0.0).then_inc(pad_zero, 1)
            if quantum:
                pool.memset(st[:, :, :, CW:], 0.0).then_inc(pad_zero, 1)
                pool.memset(tiny[:, 0:1], 1e-19)
                pool.memset(tiny[:, 1:2], 1e-8).then_inc(pad_zero, 1)

            def spread_fidelities(g):
                pool.wait_ge(normed, g + 1)
                if g >= 2:
                    pool.wait_ge(qt_ready, g - 1)
                nc.gpsimd.tensor_tensor(px[:, g % 2], p[:, g % 2, :, None, HN * N:HP * N].broadcast_to([128, 2, 4, N]),
                                        env.image_mask[:, None, :, None].broadcast_to([128, 2, 4, N]), ALU.mult).then_inc(spread, 1)

            for c in range(NC):
                for a in range(2):
                    pool.wait_ge(head_scaled if rms else qk_evicted, NT * c + 2 + a + 1)
                    if c >= 2:
                        pool.wait_ge(scored, GPC * (c - 1))
                    nc.gpsimd.tensor_tensor(kx[:, c % 2, a].rearrange("p i (h k) -> p i h k", h=HH),
                                            k[:, c % 2, a].rearrange("p (i k) -> p i k", k=N)[:, :, None, :].broadcast_to([HD, IC, HH, N]),
                                            env.head_mask[:, None, :, None].broadcast_to([HD, IC, HH, N]), ALU.mult).then_inc(k_spread, 1)
                if quantum and c >= 1:
                    spread_fidelities(2 * c - 2)
                    spread_fidelities(2 * c - 1)
            if quantum:
                spread_fidelities(NG - 2)
                spread_fidelities(NG - 1)
                pool.wait_ge(spread, NG)

        @block.vector
        def _(dve):
            def head_scale(c):
                for t in range(NT * c, NT * c + NT):
                    j, m = (t % NT) // 2, t % 2
                    dst = (q if j == 0 else k)[:, c % 2, m, 0:CW]
                    dve.wait_ge(head_rstd, t + 1)
                    wcol = cols(env, name + ("_qn" if j == 0 else "_kn"))[0:HD, 0:1]
                    nc.vector.scalar_tensor_tensor(dst, dst, wcol, rrs[:, t % 2], ALU.mult, ALU.mult).then_inc(head_scaled, 1)

            def spread_values(c):
                for a in range(2):
                    dve.wait_ge(proj[2], 2 * c + a + 1)
                    if c >= 2:
                        dve.wait_ge(vt_ready, FV * GPC * (c - 1))
                    nc.vector.tensor_tensor(vx[:, c % 2, a].rearrange("p i (h k) -> p i h k", h=HH),
                                            ps[2 + a][0:HD, 0:CW].rearrange("p (i k) -> p i k", k=N)[:, :, None, :].broadcast_to([HD, IC, HH, N]),
                                            env.head_mask[:, None, :, None].broadcast_to([HD, IC, HH, N]), ALU.mult).then_inc(v_spread, 1)

            def softmax(g):
                s = ps[4][:, 0:2 * HN * N].rearrange("p (f h k) -> p f h k", f=2, k=N)
                pg = p[:, g % 2].rearrange("p f (h k) -> p f h k", k=N)
                dve.wait_ge(scored, g + 1)
                if g >= 2:
                    dve.wait_ge(pt_ready, g - 1)
                if quantum:
                    dve.wait_ge(ov_squared, g + 1)
                    if g >= 2:
                        dve.wait_ge(spread, g - 1)
                    nc.vector.tensor_tensor(pg[:, :, HN], osq[:, g % 2, :, 0], osq[:, g % 2, :, 1], ALU.add).then_inc(fid_ready, 1)
                nc.vector.reduce_max(mx[:, g % 2, :, 0:HN], s, AX_X).then_inc(maxed, 1)
                if quantum:
                    dve.wait_ge(fid_ready, g + 1)
                    nc.vector.reduce_max(mx[:, g % 2, :, HN], pg[:, :, HN], AX_X).then_inc(maxed, 1)
                    dve.wait_ge(maxed, 2 * g + 2)
                    nc.vector.tensor_tensor(pg[:, :, HN], pg[:, :, HN], mx[:, g % 2, :, HN, None].broadcast_to([128, 2, N]), ALU.subtract)
                else:
                    dve.wait_ge(maxed, g + 1)
                nc.vector.tensor_tensor(pg[:, :, 0:HN], s, mx[:, g % 2, :, 0:HN, None].broadcast_to([128, 2, HN, N]), ALU.subtract)\
                    .then_inc(shifted, 1)
                dve.wait_ge(expd, g + 1)
                nc.vector.reduce_sum(sm[:, g % 2], pg, AX_X).then_inc(summed, 1)
                dve.wait_ge(summed, g + 1)
                nc.vector.reciprocal(sm[:, g % 2], sm[:, g % 2]).then_inc(inverted, 1)
                dve.wait_ge(inverted, g + 1)
                if quantum:
                    nc.vector.tensor_scalar(sm[:, g % 2, :, HN], sm[:, g % 2, :, HN], gate[:, 0:1], None, ALU.mult).then_inc(weighted, 1)
                    dve.wait_ge(weighted, g + 1)
                nc.vector.tensor_tensor(pg, pg, sm[:, g % 2, :, :, None].broadcast_to([128, 2, HP, N]), ALU.mult).then_inc(normed, 1)

            def scale_states(c):
                dve.wait_ge(s_factor, 4 * c + 4)
                nc.vector.tensor_tensor(st[:, c % 2, 0, 0:CW], st[:, c % 2, 0, 0:CW], srs[:], ALU.mult).then_inc(s_scaled, 1)
                dve.wait_ge(s_taken, 2 * c + 2)
                nc.vector.scalar_tensor_tensor(st[:, c % 2, 1, 0:CW], st[:, c % 2, 1, 0:CW], env.conj[:, 0:1], srs[:], ALU.mult, ALU.mult)\
                    .then_inc(s_scaled, 1)

            if quantum:
                dve.wait_ge(gate_step, 1)
                nc.vector.tensor_scalar(gate[:, 0:1], gate[:, 0:1], 1.0, None, ALU.add).then_inc(gate_step, 1)
                dve.wait_ge(gate_step, 2)
                nc.vector.reciprocal(gate[:, 0:1], gate[:, 0:1]).then_inc(gate_step, 1)
                dve.wait_ge(gate_step, 3)
                nc.vector.tensor_scalar(gate[:, 1:2], gate[:, 0:1], -1.0, 1.0, ALU.mult, ALU.add).then_inc(gate_step, 1)
                dve.wait_ge(gate_step, 4)
                nc.vector.tensor_scalar(gated_b[:, 1], cols(env, name + "_ob")[0:HD, :], gate[0:HD, 1:2], None, ALU.mult)
                nc.vector.tensor_scalar(gated_b[:, 0], cols(env, name + "_vb")[0:HD, :], gate[0:HD, 1:2], None, ALU.mult).then_inc(gate_step, 1)
                dve.wait_ge(gate_step, 5)
            for c in range(2):
                ln.centre(dve, c)
                ln.scale(dve, c)
            if rms:
                head_scale(0)
            spread_values(0)
            if quantum:
                scale_states(0)
            for c in range(NC):
                if c + 2 < NC:
                    ln.centre(dve, c + 2)
                softmax(2 * c)
                softmax(2 * c + 1)
                if c + 2 < NC:
                    ln.scale(dve, c + 2)
                if c + 1 < NC:
                    if rms:
                        head_scale(c + 1)
                    spread_values(c + 1)
                    if quantum:
                        scale_states(c + 1)
                ob = gated_b[:, 1] if quantum else cols(env, name + "_ob")[0:HD, :]
                for m in range(2):
                    dve.wait_ge(proj[3], 2 * c + m + 1)
                    hc = chunk(env.h, c)[:, m]
                    nc.vector.scalar_tensor_tensor(hc, ps[2 + m][0:HD, 0:CW], ob[:, m:m + 1], hc,
                                                   ALU.add, ALU.add).then_inc(added, 1)
            dve.wait_ge(added, 2 * NC)


class Rms:

    def __init__(self, env, name, src, dst, w, ready_src, per_chunk):
        self.env, self.src, self.dst, self.w, self.ready_src, self.per_chunk = env, src, dst, w, ready_src, per_chunk
        self.squared = env.sem(name + "_squared")
        self.mean_ready = env.sem(name + "_mean_ready")
        self.log_mean = env.sem(name + "_log_mean")
        self.factor_ready = env.sem(name + "_factor_ready")
        self.ready = env.sem(name + "_ready")

    def square(self, act, c):
        nc, env = self.env.nc, self.env
        act.wait_ge(self.ready_src, self.per_chunk * (c + 1))
        if c >= 2:
            act.wait_ge(self.mean_ready, c - 1)
        nc.scalar.activation(self.sq[:, c % 2], chunk(self.src, c), ACT.Square).then_inc(self.squared, 1)

    def mean(self, pe, c):
        nc, env = self.env.nc, self.env
        pe.wait_ge(self.squared, c + 1)
        if c > 0:
            pe.wait_ge(self.log_mean, c)
        for a in range(2):
            last = nc.tensor.matmul(env.ps[1][0:HD, 0:CW], env.mean_w, self.sq[:, c % 2, a], start=a == 0, stop=a == 1)
        last.then_inc(self.mean_ready, 1)

    def factor(self, act, c):
        nc, env = self.env.nc, self.env
        act.wait_ge(self.mean_ready, c + 1)
        if c >= 2:
            act.wait_ge(self.ready, 2 * (c - 1))
        nc.scalar.activation(self.rs[:, c % 2], env.ps[1][0:HD, 0:CW], ACT.Ln, bias=env.rms_eps[0:HD, :]).then_inc(self.log_mean, 1)
        act.wait_ge(self.log_mean, c + 1)
        nc.scalar.activation(self.rs[:, c % 2], self.rs[:, c % 2], ACT.Exp, scale=-0.5).then_inc(self.factor_ready, 1)

    def scale(self, dve, c):
        nc = self.env.nc
        dve.wait_ge(self.factor_ready, c + 1)
        for a in range(2):
            nc.vector.scalar_tensor_tensor(chunk(self.dst, c)[:, a], chunk(self.src, c)[:, a], self.w[0:HD, a:a + 1],
                                           self.rs[:, c % 2], ALU.mult, ALU.mult).then_inc(self.ready, 1)


def stage_wide_attention(env, name, dram):
    nc = env.nc
    x, x2, ps = env.x, env.x2, env.ps
    JQ = QH // 2
    R = JQ * N
    KC = KVH * N
    KS = KVH * SLOT
    TQK, TV = JQ + KVH, KVH
    NT = TQK + TV
    with ExitStack() as ctx:
        def sb(n, shape, dt=F32):
            return ctx.enter_context(nc.sbuf_tensor(name + "_" + n, shape, dt))

        def sem(n):
            return env.sem(name + "_" + n)

        wq = sb("wq", [HD, 2, QH * WD])
        wk = sb("wk", [HD, 2, KVH * 2 * WD])
        wv = sb("wv", [HD, 2, KVH * WD])
        wo = sb("wo", [128, JQ, D])
        raw = sb("raw", [128, 2, CW])
        swp = sb("swapped", [128, 2, CW])
        q = sb("q", [128, 2, IC, R])
        k = sb("k", [128, 2, KVH, CW])
        vs = sb("vs", [WD, 2, IC, KVH, SLOT])
        vt = sb("vt", [KS, 2, GI, WD])
        s = sb("s", [R, 2, GI, KC])
        mx = sb("mx", [R, 2, GI])
        sm = sb("sm", [R, 2, GI])
        p = sb("p", [R, 2, 2, GI, KVH, SLOT])
        pt = sb("pt", [KS, 2, 2, GI, R])
        cx = sb("cx", [128, 2, JQ, CW])
        rsq1, rrs1, rsq2, rrs2 = sb("rsq1", [HD, 2, 2, CW]), sb("rrs1", [HD, 2, CW]), sb("rsq2", [HD, 2, 2, CW]), sb("rrs2", [HD, 2, CW])
        w_in = sem("w_in")
        ln = Norm(env, name + "_ln", x)
        added = sem("added")
        n1 = Rms(env, name + "_n1", x, x2, cols(env, "n1w"), ln.ready, 1)
        n2 = Rms(env, name + "_n2", x, x2, cols(env, "n2w"), added, 2)
        n1.sq, n1.rs, n2.sq, n2.rs = rsq1, rrs1, rsq2, rrs2
        zeroed, projected, taken, swapped, sin_done, cos_done, turned = (
            sem(n) for n in ("zeroed", "projected", "taken", "swapped", "sin_done", "cos_done", "turned"))
        scored, masked, maxed, shifted, expd, summed, inverted, normed = (
            sem(n) for n in ("scored", "masked", "maxed", "shifted", "expd", "summed", "inverted", "normed"))
        filled, moved, out_ready, h_added = (sem(n) for n in ("filled", "moved", "out_ready", "h_added"))
        FG = 1 + 6
        FC = GPC * FG

        def fill_of(g, j):
            base = FC * (g // GPC)
            return base + g % GPC if j == 0 else base + GPC + (FG - 1) * (g % GPC) + j - 1

        block = ctx.enter_context(nc.Block())

        @block.sync
        def _(sp):
            sp.dma_start(wq[:], dram["wq"]).then_inc(w_in, 16)
            sp.dma_start(wk[:], dram["wk"]).then_inc(w_in, 16)
            sp.dma_start(wv[:], dram["wv"]).then_inc(w_in, 16)
            sp.dma_start(wo[:], dram["wo"]).then_inc(w_in, 16)

        @block.tensor
        def _(pe):
            def project(c):
                pe.wait_ge(n1.ready, 2 * (c + 1))
                for t in range(NT):
                    if t >= 2:
                        pe.wait_ge(taken, NT * c + t - 1)
                    elif c == 1:
                        pe.wait_ge(taken, NT - 1 + t)
                    elif c >= 2:
                        pe.wait_ge(added, 2 * (c - 2) + t + 1)
                    w, rows = (wq, 128) if t < JQ else (wk, 128) if t < TQK else (wv, WD)
                    j = t if t < JQ else t - JQ if t < TQK else t - TQK
                    for a in range(2):
                        last = nc.tensor.matmul(ps[2 + t % 2][0:rows, 0:CW], w[:, a, j * rows:(j + 1) * rows],
                                                chunk(x2, c)[:, a], start=a == 0, stop=a == 1)
                    last.then_inc(projected, 1)

            def scores(g):
                c = g // GPC
                pe.wait_ge(turned, TQK * (c + 1))
                if g >= 1:
                    pe.wait_ge(masked, g)
                for i in range(GI):
                    i16 = (g % GPC) * GI + i
                    for e in range(2):
                        last = nc.tensor.matmul(ps[4 + e][0:R, i * KC:(i + 1) * KC], q[e * WD:(e + 1) * WD, c % 2, i16, :],
                                                k[e * WD:(e + 1) * WD, c % 2, :, i16 * N:(i16 + 1) * N], start=True, stop=True)
                last.then_inc(scored, 1)

            def bank(g, j):
                n = fill_of(g, j)
                if n >= 2:
                    pe.wait_ge(moved, n - 1)
                return ps[6 + n % 2]

            def turn_values(g):
                c = g // GPC
                pe.wait_ge(taken, NT * (c + 1))
                to = bank(g, 0)
                for i in range(GI):
                    last = nc.tensor.transpose(to[0:KS, i * WD:(i + 1) * WD],
                                               vs[:, c % 2, (g % GPC) * GI + i].rearrange("p g k -> p (g k)"), env.ident[0:WD, 0:WD])
                last.then_inc(filled, 1)

            def weigh(g):
                pe.wait_ge(normed, g + 1)
                for j in range(4):
                    to, e = bank(g, 1 + j), j % 2
                    for i in range(4):
                        last = nc.tensor.transpose(to[0:KS, i * R:(i + 1) * R],
                                                   p[:, g % 2, e, 4 * (j // 2) + i].rearrange("p g k -> p (g k)"), env.ident[0:R, 0:R])
                    last.then_inc(filled, 1)
                for j in range(2):
                    pe.wait_ge(moved, fill_of(g, 2 + 2 * j) + 1)
                    to = bank(g, 5 + j)
                    for i in range(4):
                        for e in range(2):
                            last = nc.tensor.matmul(to[e * WD:(e + 1) * WD, i * R:(i + 1) * R], vt[:, g % 2, 4 * j + i, :],
                                                    pt[:, g % 2, e, 4 * j + i, :], start=True, stop=True)
                    last.then_inc(filled, 1)

            def project_out(c):
                pe.wait_ge(moved, fill_of(GPC * c + GPC - 1, 6) + 1)
                for m in range(2):
                    pe.wait_ge(taken, NT * min(c + 1, NC - 1) + NT - 1 + m)
                    if c == NC - 1:
                        pe.wait_ge(added, 2 * (c - 1) + m + 1)
                    for j in range(JQ):
                        last = nc.tensor.matmul(ps[2 + m][0:HD, 0:CW], wo[:, j, m * HD:(m + 1) * HD], cx[:, c % 2, j],
                                                start=j == 0, stop=j == JQ - 1)
                    last.then_inc(out_ready, 1)

            for c in range(2):
                ln.mean(pe, c)
                ln.var(pe, c)
                n1.mean(pe, c)
            pe.wait_ge(w_in, 64)
            project(0)
            for c in range(NC):
                if c + 2 < NC:
                    ln.mean(pe, c + 2)
                for g in (2 * c, 2 * c + 1):
                    scores(g)
                    turn_values(g)
                if c >= 1:
                    pe.wait_ge(n1.log_mean, min(NC, c + 2))
                    n2.mean(pe, c - 1)
                if c + 2 < NC:
                    ln.var(pe, c + 2)
                    if c >= 1:
                        pe.wait_ge(n2.log_mean, c)
                    n1.mean(pe, c + 2)
                if c + 1 < NC:
                    project(c + 1)
                for g in (2 * c, 2 * c + 1):
                    weigh(g)
                project_out(c)
            n2.mean(pe, NC - 1)

        @block.scalar
        def _(act):
            def take(c):
                for t in range(NT):
                    n = NT * c + t
                    act.wait_ge(projected, n + 1)
                    if t < TQK:
                        r = TQK * c + t
                        if r >= 2:
                            act.wait_ge(turned, r - 1)
                        nc.scalar.activation(raw[:, r % 2], ps[2 + t % 2][:, 0:CW], ACT.Copy).then_inc(taken, 1)
                    else:
                        if c >= 2 and t == TQK:
                            act.wait_ge(filled, fill_of(GPC * (c - 2) + GPC - 1, 0) + 1)
                        nc.scalar.activation(vs[:, c % 2, :, t - TQK, 0:N],
                                             ps[2 + t % 2][0:WD, 0:CW].rearrange("p (i k) -> p i k", k=N), ACT.Copy).then_inc(taken, 1)

            def take_values(g):
                n = fill_of(g, 0)
                act.wait_ge(filled, n + 1)
                if g >= 2:
                    act.wait_ge(filled, fill_of(g - 2, 6) + 1)
                nc.scalar.activation(vt[:, g % 2].rearrange("p i d -> p (i d)"), ps[6 + n % 2][0:KS, 0:GI * WD], ACT.Copy).then_inc(moved, 1)

            def exponent(g):
                act.wait_ge(shifted, g + 1)
                nc.scalar.activation(s[:], s[:], ACT.Exp, scale=WD ** -0.5).then_inc(expd, 1)

            def move_weighed(g):
                c = g // GPC
                for j in range(4):
                    n = fill_of(g, 1 + j)
                    act.wait_ge(filled, n + 1)
                    nc.scalar.activation(pt[:, g % 2, j % 2, 4 * (j // 2):4 * (j // 2) + 4].rearrange("p i r -> p (i r)"),
                                         ps[6 + n % 2][0:KS, 0:4 * R], ACT.Copy).then_inc(moved, 1)
                for j in range(2):
                    n = fill_of(g, 5 + j)
                    act.wait_ge(filled, n + 1)
                    if c >= 2:
                        act.wait_ge(out_ready, 2 * (c - 1))
                    o = ((g % GPC) * GI + 4 * j) * N
                    nc.scalar.activation(cx[:, c % 2, :, o:o + 4 * N].rearrange("p j (i n) -> p i j n", n=N),
                                         ps[6 + n % 2][:, 0:4 * R].rearrange("p (i j n) -> p i j n", i=4, j=JQ), ACT.Copy).then_inc(moved, 1)

            for c in range(2):
                ln.square(act, c)
                ln.rstd(act, c)
                n1.square(act, c)
                n1.factor(act, c)
            act.wait_ge(zeroed, 2)
            take(0)
            for c in range(NC):
                if c + 2 < NC:
                    ln.square(act, c + 2)
                if c >= 1:
                    n2.square(act, c - 1)
                for g in (2 * c, 2 * c + 1):
                    take_values(g)
                    exponent(g)
                if c >= 1:
                    n2.factor(act, c - 1)
                if c + 2 < NC:
                    ln.rstd(act, c + 2)
                    n1.square(act, c + 2)
                    n1.factor(act, c + 2)
                if c + 1 < NC:
                    take(c + 1)
                for g in (2 * c, 2 * c + 1):
                    move_weighed(g)
            n2.square(act, NC - 1)
            n2.factor(act, NC - 1)

        @block.gpsimd
        def _(pool):
            pool.memset(vs[:, :, :, :, N:], 0.0).then_inc(zeroed, 1)
            pool.memset(p[:], 0.0).then_inc(zeroed, 1)

            def table(tab):
                return tab[:, None, :].broadcast_to([128, IC, N])

            def by_token(ap):
                return ap.rearrange("p (i n) -> p i n", n=N)

            def turn(c):
                for t in range(TQK):
                    r = TQK * c + t
                    pool.wait_ge(swapped, r + 1)
                    nc.gpsimd.tensor_tensor(by_token(raw[:, r % 2]), by_token(raw[:, r % 2]), table(env.cos), ALU.mult).then_inc(cos_done, 1)
                    nc.gpsimd.tensor_tensor(by_token(swp[:, r % 2]), by_token(swp[:, r % 2]), table(env.sin), ALU.mult).then_inc(sin_done, 1)

            turn(0)
            for c in range(NC):
                if c + 1 < NC:
                    turn(c + 1)
                pool.wait_ge(added, 2 * c + 2)
                nc.gpsimd.tensor_tensor(chunk(env.h, c), chunk(env.h, c), chunk(x, c), ALU.add).then_inc(h_added, 1)
            pool.wait_ge(h_added, NC)

        @block.vector
        def _(dve):
            def swap(r):
                dve.wait_ge(taken, NT * (r // TQK) + r % TQK + 1)
                nc.vector.stream_shuffle(swp[:, r % 2], raw[:, r % 2], [i ^ 1 for i in range(32)]).then_inc(swapped, 1)

            def turn(c):
                for t in range(TQK + 1):
                    r = TQK * c + t
                    if t < TQK:
                        swap(r)
                    if t == 0:
                        continue
                    r, u = r - 1, t - 1
                    dve.wait_ge(cos_done, r + 1)
                    dve.wait_ge(sin_done, r + 1)
                    if c >= 2 and u == 0:
                        dve.wait_ge(scored, GPC * (c - 1))
                    if u < JQ:
                        nc.vector.tensor_tensor(q[:, c % 2, :, u * N:(u + 1) * N], raw[:, r % 2].rearrange("p (i n) -> p i n", n=N),
                                                swp[:, r % 2].rearrange("p (i n) -> p i n", n=N), ALU.add).then_inc(turned, 1)
                    else:
                        nc.vector.tensor_tensor(k[:, c % 2, u - JQ], raw[:, r % 2], swp[:, r % 2], ALU.add).then_inc(turned, 1)

            def softmax(g):
                sc = env.psall[0:R, 4:6, 0:GI * KC].rearrange("p e (i k) -> p e i k", k=KC)
                if g >= 1:
                    dve.wait_ge(normed, g)
                dve.wait_ge(scored, g + 1)
                nc.vector.tensor_tensor(s[:], sc, env.causal[:, None, None, :].broadcast_to([R, 2, GI, KC]), ALU.add).then_inc(masked, 1)
                dve.wait_ge(masked, g + 1)
                nc.vector.reduce_max(mx[:], s[:], AX_X).then_inc(maxed, 1)
                dve.wait_ge(maxed, g + 1)
                nc.vector.tensor_tensor(s[:], s[:], mx[:, :, :, None].broadcast_to([R, 2, GI, KC]), ALU.subtract).then_inc(shifted, 1)
                dve.wait_ge(expd, g + 1)
                nc.vector.reduce_sum(sm[:], s[:], AX_X).then_inc(summed, 1)
                dve.wait_ge(summed, g + 1)
                nc.vector.reciprocal(sm[:], sm[:]).then_inc(inverted, 1)
                dve.wait_ge(inverted, g + 1)
                if g >= 2:
                    dve.wait_ge(filled, fill_of(g - 2, 4) + 1)
                for e in range(2):
                    last = nc.vector.tensor_tensor(p[:, g % 2, e, :, :, 0:N], s[:, e].rearrange("p i (g k) -> p i g k", k=N),
                                                   sm[:, e, :, None, None].broadcast_to([R, GI, KVH, N]), ALU.mult)
                last.then_inc(normed, 1)

            for c in range(2):
                ln.centre(dve, c)
                ln.scale(dve, c)
                n1.scale(dve, c)
            turn(0)
            dve.wait_ge(zeroed, 2)
            for c in range(NC):
                if c + 2 < NC:
                    ln.centre(dve, c + 2)
                softmax(2 * c)
                softmax(2 * c + 1)
                if c >= 1:
                    n2.scale(dve, c - 1)
                if c + 2 < NC:
                    ln.scale(dve, c + 2)
                    n1.scale(dve, c + 2)
                if c + 1 < NC:
                    turn(c + 1)
                for m in range(2):
                    dve.wait_ge(out_ready, 2 * c + m + 1)
                    xc = chunk(x, c)[:, m]
                    nc.vector.tensor_tensor(xc, ps[2 + m][0:HD, 0:CW], xc, ALU.add).then_inc(added, 1)
            n2.scale(dve, NC - 1)
            dve.wait_ge(n2.ready, 2 * NC)


def stage_routed_ffn(env, name, dram, src, E, K, TL, norm=False):
    nc = env.nc
    ps = env.ps
    top2 = K == 2
    RT = 128
    NR = -(-T // RT)
    LAST = T - (NR - 1) * RT
    FN = EF if top2 else FF
    NH = FN // 128
    BW = 384
    HF = FN // BW
    KU = [HD if top2 else HD + 1, HD]
    assert TL * RT >= T * K + E * (RT - 1) - RT + 1 and TL % 2 == 0
    with ExitStack() as ctx:
        def sb(n, shape, dt=F32):
            return ctx.enter_context(nc.sbuf_tensor(name + "_" + n, shape, dt))

        def sem(n):
            return env.sem(name + "_" + n)

        wr = sb("wr", [HD, 2, E])
        wu = sb("wu", [KU[0], E, 2, 2 * BW])
        wd = sb("wd", [128, E, NH, D])
        chosen = sb("chosen", [RT, NR, E])
        lg, pr, t0, t1, t2, t3 = (sb(n, [RT, NR, E]) for n in ("lg", "pr", "t0", "t1", "t2", "t3"))
        before = sb("before", [RT, NR + 1, E])
        r0, r1 = sb("r0", [RT, NR]), sb("r1", [RT, NR])
        cnt = sb("cnt", [RT, 4, E])
        tile_cmp, tile_sum, tile_expert = sb("tile_cmp", [1, TL, E]), sb("tile_sum", [1, TL]), sb("tile_expert", [1, TL], I32)
        slot = sb("slot", [RT, K, NR], U32)
        share = sb("share", [RT, 2, NR])
        xtok = sb("xtok", [RT, NR, D])
        xs = sb("xs", [RT, 2, D])
        xf = sb("xf", [KU[0], 2, 2, RT])
        hid = sb("hid", [RT, 2, FN])
        hidt = sb("hidt", [128, 2, NH, RT])
        ys = sb("ys", [RT, 2, D])
        yb = [xtok] + [sb("yb", [RT, NR, D]) for _ in range(K - 1)]
        if top2:
            top8 = sb("top8", [RT, NR, 8])
            gs = sb("gs", [RT, 2, BW])
        else:
            bg, b2 = sb("bg", [RT, E]), sb("b2", [RT, E, D])
        x_slots, y_slots = env.x_slots, env.y_slots
        small_in, routed, exp_in, exp_out, chain = (sem(n) for n in ("small_in", "routed", "logits_shifted", "logits_exp", "router_steps"))
        zeroed, prefix_ready, rank_ready, slots_ready, tiles_ready = (
            sem(n) for n in ("zeroed", "prefix_ready", "rank_ready", "slots_ready", "tiles_ready"))
        xt_ready, xt_moved, scattered = sem("xt_ready"), sem("xt_moved"), sem("scattered")
        w_in = [sem(f"w{i}_in") for i in range(E)]
        w_ready = sem("w_ready")
        x_in, y_out = [sem("x0_in"), sem("x1_in")], [sem("y0_out"), sem("y1_out")]
        x_turned, x_moved, up_ready, acted, hid_ready, h_turned, h_moved, down_ready, y_moved = (
            sem(n) for n in ("x_turned", "x_moved", "up_ready", "acted", "hid_ready", "hid_turned", "hid_moved", "down_ready", "y_moved"))
        y_back = [sem(f"y{t}_back") for t in range(NR)]
        summed, weighed, out_turned, added = sem("share_summed"), sem("weighed"), sem("out_turned"), sem("added")
        ones_ready = sem("ones_ready")
        ln = Norm(env, name + "_ln", env.x) if norm else None
        block = ctx.enter_context(nc.Block())

        def rows(t):
            return LAST if t == NR - 1 else RT

        def wait(eng, s, value):
            if not isinstance(value, int) or value > 0:
                eng.wait_ge(s, value)

        def tiles_loop(eng, body):
            for i in range(2):
                body(i, i, 2)
            with eng.Fori(1, TL // 2 - 2) as it:
                for u in range(2):
                    body(it * 2 + u, u, 2)
            for i in range(TL - 4, TL):
                body(i, i % 2, min(2, TL - 1 - i))

        def i_half(i, p):
            return i // 2 if isinstance(i, int) else (i - p) // 2

        @block.sync
        def _(sp):
            sp.dma_start(wr[:], dram["wr"]).then_inc(small_in, 16)
            if not top2:
                sp.dma_start(bg[:], dram["bg"].broadcast_to([RT, E])).then_inc(small_in, 16)
                sp.dma_start(b2[:], dram["b2"].broadcast_to([RT, E, D])).then_inc(small_in, 16)
            for e in range(E):
                sp.dma_start(wu[:, e], dram["up"][e]).then_inc(w_in[e], 16)
                sp.dma_start(wd[:, e], dram["down"][e].rearrange("(j p) f -> p j f", p=128)).then_inc(w_in[e], 16)
            for e in range(E):
                sp.wait_ge(w_in[e], 32)
                sp.sem_inc(w_ready, 1)

        @block.tensor
        def _(pe):
            if norm:
                for c in range(NC):
                    ln.mean(pe, c)
                    ln.var(pe, c)
                pe.wait_ge(ln.ready, NC)
            pe.wait_ge(small_in, 16 if top2 else 48)
            for t in range(NR):
                for a in range(2):
                    last = nc.tensor.matmul(ps[7][0:rows(t), t * E:(t + 1) * E], src[:, a, t * RT:t * RT + rows(t)], wr[:, a], start=a == 0, stop=a == 1)
            last.then_inc(routed, 1)
            for t in range(NR):
                for a in range(2):
                    o = (t % 2) * D + a * HD
                    last = nc.tensor.transpose(ps[1 + t // 2][0:rows(t), o:o + HD], src[:, a, t * RT:t * RT + rows(t)], env.ident[0:HD, 0:HD])
                if t % 2 or t == NR - 1:
                    last.then_inc(xt_ready, 1)
            pe.wait_ge(prefix_ready, 1)
            nc.tensor.matmul(ps[6][:, 0:NR * E], env.earlier, chosen[:].rearrange("p t e -> p (t e)"), start=True, stop=False)
            nc.tensor.matmul(ps[6][:, 0:NR * E], env.ones, before[:, 0:NR].rearrange("p t e -> p (t e)"), start=False, stop=True)
            nc.tensor.matmul(ps[6][:, NR * E:(NR + 1) * E], env.ones, before[:, NR], start=True, stop=True).then_inc(rank_ready, 1)

            def turn_x(i, p):
                pe.wait_ge(x_in[p], i_half(i, p) * 16 + 16)
                wait(pe, x_moved, i)
                for a in range(2):
                    last = nc.tensor.transpose(ps[0][0:HD, a * RT:(a + 1) * RT], xs[:, p, a * HD:(a + 1) * HD], env.ident)
                last.then_inc(x_turned, 1)

            def expert(i):
                return pe.value_load(tile_expert[0:1, bass.ds(i, 1)], min_val=0, max_val=E - 1)

            def up(i, p):
                e = expert(i)
                pe.wait_ge(w_ready, e + 1)
                pe.wait_ge(x_moved, i + 1)
                for u in range(2):
                    if top2:
                        wait(pe, hid_ready if u else acted, i - 1)
                    else:
                        wait(pe, acted, i * 2 + (u - 3))
                    for a in range(2):
                        last = nc.tensor.matmul(ps[2 + 2 * p + u][:, 0:BW], xf[0:KU[a], p, a],
                                                wu[0:KU[a], bass.ds(e, 1), a, u * BW:(u + 1) * BW].rearrange("p e f -> p (e f)"),
                                                start=a == 0, stop=a == 1)
                    last.then_inc(up_ready, 1)

            def turn_hidden(i, p):
                for f in range(HF):
                    n = i * HF + f
                    if top2:
                        pe.wait_ge(hid_ready, i + 1)
                    else:
                        pe.wait_ge(acted, n + 1)
                    wait(pe, h_moved, n - 1)
                    for j in range(3):
                        last = nc.tensor.transpose(ps[(1, 6)[(p * HF + f) % 2]][:, j * RT:(j + 1) * RT],
                                                   hid[:, p, f * BW + j * 128:f * BW + (j + 1) * 128], env.ident)
                    last.then_inc(h_turned, 1)

            def down(i, p):
                e = expert(i)
                pe.wait_ge(h_moved, i * HF + HF)
                wait(pe, y_moved, i)
                for j in range(NH):
                    last = nc.tensor.matmul(ps[7][:, 0:D], hidt[:, p, j], wd[:, bass.ds(e, 1), j, :].rearrange("p e f -> p (e f)"),
                                            start=j == 0, stop=j == NH - 1)
                last.then_inc(down_ready, 1)

            pe.wait_ge(tiles_ready, 1)
            pe.wait_ge(xt_moved, -(-NR // 2))
            pe.wait_ge(slots_ready, 1)
            if not top2:
                pe.wait_ge(ones_ready, 1)
            turn_x(0, 0)
            turn_x(1, 1)
            up(0, 0)

            def body(i, p, ahead):
                if ahead >= 1:
                    up(i + 1, 1 - p)
                turn_hidden(i, p)
                if ahead >= 2:
                    turn_x(i + 2, p)
                down(i, p)

            tiles_loop(pe, body)
            for t in range(NR):
                if top2:
                    pe.wait_ge(weighed, t + 1)
                else:
                    pe.wait_ge(y_back[t], 16)
                if t >= 4:
                    pe.wait_ge(added, t - 3)
                for a in range(2):
                    last = nc.tensor.transpose(ps[2 + t % 4][0:HD, a * RT:a * RT + rows(t)], yb[0][0:rows(t), t, a * HD:(a + 1) * HD],
                                               env.ident[0:rows(t), 0:rows(t)])
                last.then_inc(out_turned, 1)

        @block.scalar
        def _(act):
            if norm:
                act.preload_act_table_set("natural_log_exp_and_others")
                for c in range(NC):
                    ln.square(act, c)
                    ln.rstd(act, c)
            for b in range(-(-NR // 2)):
                act.wait_ge(xt_ready, b + 1)
                n = rows(2 * b)
                w = min(2, NR - 2 * b)
                nc.scalar.activation(xtok[0:n, 2 * b:2 * b + w].rearrange("p t d -> p (t d)"), ps[1 + b][0:n, 0:w * D], ACT.Copy).then_inc(xt_moved, 1)
            if top2:
                act.wait_ge(exp_in, 1)
                nc.scalar.activation(pr[:], pr[:], ACT.Exp).then_inc(exp_out, 1)

            def load_x(i, p):
                act.dma_start(xs[:, p], x_slots[bass.ds(i * RT, RT), :]).then_inc(x_in[p], 16)

            def move_x(i, p, more):
                act.wait_ge(x_turned, i + 1)
                wait(act, up_ready, i * 2 - 2)
                nc.scalar.activation(xf[0:HD, p].rearrange("p a r -> p (a r)"), ps[0][0:HD, 0:2 * RT], ACT.Copy).then_inc(x_moved, 1)
                if more:
                    load_x(i + 2, p)

            def nonlinear(i, p):
                for u in range(1 if top2 else 2):
                    act.wait_ge(up_ready, i * 2 + (u + 1))
                    if top2:
                        wait(act, hid_ready, i - 1)
                        nc.scalar.activation(gs[:, p], ps[2 + 2 * p][:, 0:BW], ACT.Silu).then_inc(acted, 1)
                    else:
                        wait(act, h_turned, i * HF - HF)
                        nc.scalar.activation(hid[:, p, u * BW:(u + 1) * BW], ps[2 + 2 * p + u][:, 0:BW], ACT.Gelu).then_inc(acted, 1)

            def move_hidden(i, p):
                for f in range(HF):
                    act.wait_ge(h_turned, i * HF + (f + 1))
                    wait(act, down_ready, i - 1)
                    nc.scalar.activation(hidt[:, p, 3 * f:3 * f + 3].rearrange("p j r -> p (j r)"),
                                         ps[(1, 6)[(p * HF + f) % 2]][:, 0:BW], ACT.Copy).then_inc(h_moved, 1)

            act.wait_ge(scattered, 16 * K * NR)
            load_x(0, 0)
            load_x(1, 1)
            move_x(0, 0, True)
            move_x(1, 1, True)
            nonlinear(0, 0)

            def body(i, p, ahead):
                if ahead >= 1:
                    nonlinear(i + 1, 1 - p)
                move_hidden(i, p)
                if ahead >= 2:
                    move_x(i + 2, p, not isinstance(i, int) or i + 4 < TL)

            tiles_loop(act, body)

        @block.gpsimd
        def _(pool):
            pool.memset(lg[:], 0.0).then_inc(zeroed, 1)
            if not top2:
                pool.wait_ge(zeroed, 1)
                pool.memset(xf[HD:HD + 1], 1.0).then_inc(ones_ready, 1)
                pool.wait_ge(ones_ready, 1)
            pool.memset(before[:, 0], 0.0).then_inc(zeroed, 1)
            pool.wait_ge(env.slots_zero, 16)
            pool.wait_ge(slots_ready, 1)
            pool.wait_ge(xt_moved, -(-NR // 2))
            for t in range(NR):
                for k in range(K):
                    nc.gpsimd.indirect_dma_start(x_slots, bass.IndirectOffsetOnAxis(ap=slot[0:rows(t), k, t:t + 1], axis=0),
                                                 xtok[0:rows(t), t], None).then_inc(scattered, 16)

            def body(i, p, ahead):
                pool.wait_ge(y_moved, i + 1)
                pool.dma_start(y_slots[bass.ds(i * RT, RT), :], ys[:, p]).then_inc(y_out[p], 16)

            tiles_loop(pool, body)
            for p in range(2):
                pool.wait_ge(y_out[p], 16 * (TL // 2))
            for t in range(NR):
                for k in range(K):
                    nc.gpsimd.indirect_dma_start(yb[k][0:rows(t), t], None, y_slots,
                                                 bass.IndirectOffsetOnAxis(ap=slot[0:rows(t), k, t:t + 1], axis=0)).then_inc(y_back[t], 16)

        @block.vector
        def _(dve):
            V = nc.vector
            steps = [0]

            def link(ins):
                steps[0] += 1
                ins.then_inc(chain, 1)
                dve.wait_ge(chain, steps[0])

            def over(v):
                return v[:, :, None].broadcast_to([RT, NR, E])

            def running(a, free, width):
                sh = 1
                while sh < width:
                    b = free[0]
                    V.tensor_copy(b[..., 0:sh], a[..., 0:sh])
                    link(V.tensor_tensor(b[..., sh:], a[..., sh:], a[..., 0:width - sh], ALU.add))
                    a, free = b, free[1:] + free[:1]
                    sh *= 2
                return a

            if norm:
                for c in range(NC):
                    ln.centre(dve, c)
                    ln.scale(dve, c)
            dve.wait_ge(zeroed, 2)
            dve.wait_ge(routed, 1)
            for lo, hi, n in ((0, NR - 1, RT), (NR - 1, NR, LAST)):
                logits = ps[7][0:n, lo * E:hi * E].rearrange("p (t e) -> p t e", e=E)
                if top2:
                    last = V.tensor_copy(lg[0:n, lo:hi], logits)
                else:
                    last = V.tensor_tensor(lg[0:n, lo:hi], logits, bg[0:n, None, :].broadcast_to([n, hi - lo, E]), ALU.add)
            link(last)
            link(V.reduce_max(r0[:], lg[:], AX_X))
            valid = env.valid[:, :, None].broadcast_to([RT, NR, E])
            if top2:
                V.tensor_tensor(pr[:], lg[:], over(r0), ALU.subtract).then_inc(exp_in, 1)
                dve.wait_ge(exp_out, 1)
                link(V.reduce_sum(r0[:], pr[:], AX_X))
                link(V.reciprocal(r0[:], r0[:]))
                link(V.tensor_tensor(pr[:], pr[:], over(r0), ALU.mult))
                for t in range(NR):
                    last = V.max(top8[:, t], pr[:, t])
                link(last)
                second = top8[:, :, 1:2].broadcast_to([RT, NR, E])
                V.tensor_tensor(t0[:], pr[:], second, ALU.is_gt)
                link(V.tensor_tensor(t1[:], pr[:], second, ALU.is_equal))
                link(V.reduce_sum(r1[:], t0[:], AX_X))
                link(V.tensor_scalar(r1[:], r1[:], -1.0, 2.0, ALU.mult, ALU.add))
                a = running(t1, [t2, t3], E)
                link(V.tensor_tensor(a[:], a[:], over(r1), ALU.is_le))
                link(V.tensor_tensor(a[:], a[:], t1[:], ALU.mult))
                link(V.tensor_tensor(a[:], a[:], t0[:], ALU.add))
            else:
                link(V.tensor_tensor(t1[:], lg[:], over(r0), ALU.is_equal))
                a = running(t1, [t2, t3], E)
                link(V.tensor_scalar(a[:], a[:], 1.0, None, ALU.is_le))
                link(V.tensor_tensor(a[:], a[:], t1[:], ALU.mult))
            link(V.tensor_tensor(chosen[:], a[:], valid, ALU.mult))
            for t in range(NR):
                link(V.tensor_tensor(before[:, t + 1], before[:, t], chosen[:, t], ALU.add))
            dve.sem_inc(prefix_ready, 1)
            if top2:
                a = running(chosen, [t1, t2], E)
                free = t1 if a is t2 else t2
                link(V.tensor_scalar(a[:], a[:], 1.0, None, ALU.is_equal))
                link(V.tensor_tensor(free[:], a[:], chosen[:], ALU.mult))
                link(V.tensor_tensor(a[:], chosen[:], free[:], ALU.subtract))
                choice = [free, a]
                for k in range(2):
                    link(V.tensor_tensor(t3[:], pr[:], choice[k][:], ALU.mult))
                    link(V.reduce_sum(share[:, k], t3[:], AX_X))
            else:
                choice = [chosen]
            dve.wait_ge(rank_ready, 1)
            link(V.tensor_scalar(cnt[:, 0], ps[6][:, NR * E:(NR + 1) * E], 1.0 / RT, (RT - 1.0) / RT - 0.5 + 0.5 / RT, ALU.mult, ALU.add))
            link(V.tensor_scalar(cnt[:, 0], cnt[:, 0], ROUND, ROUND, ALU.add, ALU.subtract))
            upto = running(cnt[:, 0], [cnt[:, 1], cnt[:, 2]], E)
            link(V.tensor_tensor(cnt[:, 3], upto, cnt[:, 0], ALU.subtract))
            link(V.tensor_scalar(cnt[:, 3], cnt[:, 3], float(RT), None, ALU.mult))
            link(V.tensor_tensor(lg[:], ps[6][:, 0:NR * E].rearrange("p (t e) -> p t e", e=E), cnt[:, 3:4].broadcast_to([RT, NR, E]), ALU.add))
            for k in range(K):
                link(V.tensor_tensor(t3[:], lg[:], choice[k][:], ALU.mult))
                link(V.reduce_sum(r0[:], t3[:], AX_X))
                link(V.tensor_copy(slot[:, k], r0[:]))
            dve.sem_inc(slots_ready, 1)
            link(V.tensor_tensor(tile_cmp[:], upto[0:1, None, :].broadcast_to([1, TL, E]),
                                 env.tile_no[:, 0:TL, None].broadcast_to([1, TL, E]), ALU.is_le))
            link(V.reduce_sum(tile_sum[:], tile_cmp[:], AX_X))
            link(V.tensor_scalar(tile_expert[:], tile_sum[:], E - 1.0, None, ALU.min))
            dve.sem_inc(tiles_ready, 1)
            if top2:
                V.tensor_tensor(r0[:], share[:, 0], share[:, 1], ALU.add).then_inc(summed, 1)
                dve.wait_ge(summed, 1)
                link(V.tensor_scalar(r0[:], r0[:], 1e-30, None, ALU.max))
                V.reciprocal(r0[:], r0[:]).then_inc(summed, 1)
                dve.wait_ge(summed, 2)
                V.tensor_tensor(share[:], share[:], r0[:, None, :].broadcast_to([RT, 2, NR]), ALU.mult).then_inc(summed, 1)
                dve.wait_ge(summed, 3)

            def gate(i, p):
                dve.wait_ge(acted, i + 1)
                dve.wait_ge(up_ready, i * 2 + 2)
                wait(dve, h_turned, i - 1)
                V.tensor_tensor(hid[:, p], ps[3 + 2 * p][:, 0:BW], gs[:, p], ALU.mult).then_inc(hid_ready, 1)

            def move_y(i, p):
                dve.wait_ge(down_ready, i + 1)
                wait(dve, y_out[p], i_half(i, p) * 16)
                if top2:
                    V.tensor_copy(ys[:, p], ps[7][:, 0:D]).then_inc(y_moved, 1)
                else:
                    e = dve.value_load(tile_expert[0:1, bass.ds(i, 1)], min_val=0, max_val=E - 1)
                    V.tensor_tensor(ys[:, p], ps[7][:, 0:D], b2[:, bass.ds(e, 1), :].rearrange("p e f -> p (e f)"), ALU.add).then_inc(y_moved, 1)

            if top2:
                gate(0, 0)

            def body(i, p, ahead):
                if top2 and ahead >= 1:
                    gate(i + 1, 1 - p)
                move_y(i, p)

            tiles_loop(dve, body)

            def add(t):
                dve.wait_ge(out_turned, t + 1)
                hc = env.h[:, :, t * RT:t * RT + rows(t)]
                V.tensor_tensor(hc, hc, ps[2 + t % 4][0:HD, 0:2 * RT].rearrange("p (a r) -> p a r", a=2)[:, :, 0:rows(t)], ALU.add)\
                    .then_inc(added, 1)

            for t in range(NR):
                if top2:
                    n = rows(t)
                    dve.wait_ge(y_back[t], 32)
                    V.tensor_scalar(yb[0][0:n, t], yb[0][0:n, t], share[0:n, 0, t:t + 1], None, ALU.mult).then_inc(summed, 1)
                    dve.wait_ge(summed, 4 + t)
                    V.scalar_tensor_tensor(yb[0][0:n, t], yb[1][0:n, t], share[0:n, 1, t:t + 1], yb[0][0:n, t], ALU.mult, ALU.add).then_inc(weighed, 1)
                if t >= 1:
                    add(t - 1)
            add(NR - 1)
            dve.wait_ge(added, NR)


def complex_product(link, V, out_re, out_im, a_re, a_im, b_re, b_im, tmp):
    link(V.tensor_tensor(out_re, a_re, b_re, ALU.mult))
    link(V.tensor_tensor(tmp, a_im, b_im, ALU.mult))
    link(V.tensor_tensor(out_re, out_re, tmp, ALU.subtract))
    link(V.tensor_tensor(out_im, a_re, b_im, ALU.mult))
    link(V.tensor_tensor(tmp, a_im, b_re, ALU.mult))
    link(V.tensor_tensor(out_im, out_im, tmp, ALU.add))


def stage_convolution(env, name, dram):
    nc = env.nc
    x = env.x
    x4 = x[:, :, :].rearrange("p a (b n) -> p a b n", n=N)
    with ExitStack() as ctx:
        def sb(n, shape, dt=F32):
            return ctx.enter_context(nc.sbuf_tensor(name + "_" + n, shape, dt))

        def sem(n):
            return env.sem(name + "_" + n)

        prm = sb("prm", [HD, 4, 2, SN])
        d = sb("delta", [HD, 2, 6])
        t = sb("t", [HD, 12, 2, SN])
        pw = sb("pw", [HD, 5, 2, 2, SN])
        wr, wi, wt = (sb(n, [HD, 2, N, SN]) for n in ("wr", "wi", "wt"))
        taps = sb("taps", [HD, 2, N])
        prm_in, dve_step, act_step, pool_step = sem("prm_in"), sem("dve_step"), sem("act_step"), sem("pool_step")
        powers_ready, response_ready, taps_ready, added = (sem(n) for n in ("powers_ready", "response_ready", "taps_ready", "added"))
        ln = Norm(env, name + "_ln", x)
        ld = cols(env, "s1_ld")[0:HD, :]
        C1, C2 = 6.28125, 0.0019353071795864769
        block = ctx.enter_context(nc.Block())

        @block.sync
        def _(sp):
            sp.dma_start(prm[:], dram["prm"]).then_inc(prm_in, 16)

        @block.tensor
        def _(pe):
            for c in range(NC):
                ln.mean(pe, c)
                ln.var(pe, c)

        @block.scalar
        def _(act):
            act.wait_ge(dve_step, 1)
            nc.scalar.activation(d[:, :, 1], d[:, :, 0], ACT.Exp, scale=-1.0).then_inc(act_step, 1)
            act.wait_ge(dve_step, 2)
            nc.scalar.activation(d[:, :, 3], d[:, :, 2], ACT.Ln).then_inc(act_step, 1)
            act.wait_ge(dve_step, 8)
            nc.scalar.activation(t[:, 0], t[:, 0], ACT.Exp).then_inc(act_step, 1)
            for c in range(NC):
                ln.square(act, c)
                ln.rstd(act, c)
            act.wait_ge(dve_step, 20)
            nc.scalar.activation(t[:, 3], t[:, 3], ACT.Sin).then_inc(act_step, 1)
            nc.scalar.activation(t[:, 4], t[:, 4], ACT.Sin).then_inc(act_step, 1)

        @block.gpsimd
        def _(pool):
            steps = [0]

            def link(ins):
                steps[0] += 1
                ins.then_inc(pool_step, 1)
                pool.wait_ge(pool_step, steps[0])

            pool.wait_ge(powers_ready, 1)
            for i, (at, n) in enumerate(((1, 1), (2, 2), (4, 4), (8, 8), (16, 1))):
                def power(part):
                    return pw[:, i, part, :, None, :].broadcast_to([HD, 2, n, SN])
                complex_product(link, nc.gpsimd, wr[:, :, at:at + n], wi[:, :, at:at + n], wr[:, :, 0:n], wi[:, :, 0:n],
                                power(0), power(1), wt[:, :, 0:n])
            pool.sem_inc(response_ready, 1)

        @block.vector
        def _(dve):
            V = nc.vector
            steps = [0]

            def link(ins):
                steps[0] += 1
                ins.then_inc(dve_step, 1)
                dve.wait_ge(dve_step, steps[0])

            def after_act(n):
                dve.wait_ge(act_step, n)

            dve.wait_ge(prm_in, 16)
            V.tensor_scalar(d[:, :, 4], ld, -1.0, None, ALU.mult).then_inc(taps_ready, 1)
            dve.wait_ge(taps_ready, 1)
            link(V.tensor_tensor(d[:, :, 0], ld, d[:, :, 4], ALU.max))
            after_act(1)
            link(V.tensor_scalar(d[:, :, 2], d[:, :, 1], 1.0, None, ALU.add))
            link(V.tensor_scalar(d[:, :, 4], d[:, :, 2], 1.0, None, ALU.subtract))
            link(V.tensor_tensor(d[:, :, 4], d[:, :, 1], d[:, :, 4], ALU.subtract))
            link(V.reciprocal(d[:, :, 5], d[:, :, 2]))
            after_act(2)
            link(V.tensor_tensor(d[:, :, 4], d[:, :, 4], d[:, :, 5], ALU.mult))
            V.tensor_scalar(d[:, :, 5], ld, 0.0, None, ALU.max)
            link(V.tensor_tensor(d[:, :, 3], d[:, :, 3], d[:, :, 4], ALU.add))
            V.tensor_tensor(d[:, :, 0], d[:, :, 3], d[:, :, 5], ALU.add).then_inc(taps_ready, 1)
            dve.wait_ge(taps_ready, 2)
            delta = d[:, :, 0:1].broadcast_to([HD, 2, SN])
            ar, ai, bm, cm = (prm[:, i] for i in range(4))
            link(V.tensor_tensor(t[:, 0], ar, delta, ALU.mult))
            link(V.tensor_tensor(t[:, 1], ai, delta, ALU.mult))
            link(V.tensor_scalar(t[:, 2], t[:, 1], float(1 / (2 * np.pi)), ROUND, ALU.mult, ALU.add))
            link(V.tensor_scalar(t[:, 2], t[:, 2], ROUND, None, ALU.subtract))
            link(V.scalar_tensor_tensor(t[:, 1], t[:, 2], -C1, t[:, 1], ALU.mult, ALU.add))
            link(V.scalar_tensor_tensor(t[:, 1], t[:, 2], -C2, t[:, 1], ALU.mult, ALU.add))
            link(V.tensor_scalar(t[:, 3], t[:, 1], PI_DOWN, -PI_DOWN, ALU.min, ALU.max))
            link(V.tensor_scalar(t[:, 4], t[:, 1], float(np.pi / 2), None, ALU.add))
            link(V.tensor_scalar(t[:, 5], t[:, 4], PI_DOWN, float(2 * np.pi), ALU.is_gt, ALU.mult))
            link(V.tensor_tensor(t[:, 4], t[:, 4], t[:, 5], ALU.subtract))
            link(V.tensor_scalar(t[:, 4], t[:, 4], PI_DOWN, -PI_DOWN, ALU.min, ALU.max))
            link(V.tensor_tensor(t[:, 6], ar, ar, ALU.mult))
            link(V.tensor_tensor(t[:, 7], ai, ai, ALU.mult))
            link(V.tensor_tensor(t[:, 6], t[:, 6], t[:, 7], ALU.add))
            link(V.reciprocal(t[:, 6], t[:, 6]))
            for c in range(NC):
                ln.centre(dve, c)
                ln.scale(dve, c)
            after_act(5)
            abr, abi = pw[:, 0, 0], pw[:, 0, 1]
            link(V.tensor_tensor(abi, t[:, 0], t[:, 3], ALU.mult))
            link(V.tensor_tensor(abr, t[:, 0], t[:, 4], ALU.mult))
            for i in range(4):
                complex_product(link, V, pw[:, i + 1, 0], pw[:, i + 1, 1], pw[:, i, 0], pw[:, i, 1], pw[:, i, 0], pw[:, i, 1], t[:, 8])
            link(V.tensor_scalar(t[:, 9], abr, 1.0, None, ALU.subtract))
            link(V.tensor_scalar(t[:, 10], ai, -1.0, None, ALU.mult))
            complex_product(link, V, wr[:, :, 0], wi[:, :, 0], t[:, 9], abi, ar, t[:, 10], t[:, 8])
            link(V.tensor_tensor(t[:, 6], t[:, 6], bm, ALU.mult))
            link(V.tensor_tensor(t[:, 6], t[:, 6], cm, ALU.mult))
            link(V.tensor_tensor(wr[:, :, 0], wr[:, :, 0], t[:, 6], ALU.mult))
            link(V.tensor_tensor(wi[:, :, 0], wi[:, :, 0], t[:, 6], ALU.mult))
            dve.sem_inc(powers_ready, 1)
            dve.wait_ge(response_ready, 1)
            V.reduce_sum(taps[:], wr[:], AX_X).then_inc(taps_ready, 1)
            dve.wait_ge(taps_ready, 3)
            n = 0
            for j in range(N):
                for a in range(2):
                    if n >= 2:
                        dve.wait_ge(added, n - 1)
                    V.scalar_tensor_tensor(env.h4[:, a, :, j:N], x4[:, a, :, 0:N - j], taps[:, a, j:j + 1], env.h4[:, a, :, j:N],
                                           ALU.mult, ALU.add).then_inc(added, 1)
                    n += 1
            dve.wait_ge(added, 2 * N)


def stage_quantised_ffn(env, name, dram):
    nc = env.nc
    x, ps = env.x, env.ps
    NF = FF // 128
    with ExitStack() as ctx:
        def sb(n, shape, dt=F32):
            return ctx.enter_context(nc.sbuf_tensor(name + "_" + n, shape, dt))

        def sem(n):
            return env.sem(name + "_" + n)

        w1, w2 = sb("w1", [HD, 2, FF]), sb("w2", [128, NF, D])
        a1r, a2r = sb("a1r", [HD, FF]), sb("a2r", [128, D])
        m1r, m2r = sb("m1r", [128, D]), sb("m2r", [128, FF])
        q1, q2 = sb("q1", [HD, 2, FF], BF16), sb("q2", [128, NF, D], BF16)
        mean1, mean2, inv1, inv2 = (sb(n, [128, 1]) for n in ("mean1", "mean2", "inv1", "inv2"))
        s1, s2 = sb("s1", [128, NF]), sb("s2", [HD, 2])
        xt = sb("xt", [HD, 2, CW])
        xq = sb("xq", [HD, 2, 2, CW], BF16)
        g = sb("g", [128, 2, NF, CW])
        gq = sb("gq", [128, 2, NF, CW], BF16)
        y = sb("y", [HD, 2, 2, CW])
        ln = Norm(env, name + "_ln", x)
        w_in = sem("w_in")
        prep, qstep, gstep = sem("prep"), sem("x_quant_step"), sem("g_quant_step")
        up_ready, gelu_ready, down_ready, y_ready, added = (sem(n) for n in ("up_ready", "gelu_ready", "down_ready", "y_ready", "added"))
        block = ctx.enter_context(nc.Block())

        @block.sync
        def _(sp):
            sp.dma_start(w1[:], dram["w1"]).then_inc(w_in, 16)
            sp.dma_start(w2[:], dram["w2"]).then_inc(w_in, 16)
            sp.dma_start(a1r[:], dram["aw1"].broadcast_to([HD, FF])).then_inc(w_in, 16)
            sp.dma_start(a2r[:], dram["aw2"].broadcast_to([128, D])).then_inc(w_in, 16)
            sp.dma_start(m1r[:], dram["aa1"].broadcast_to([128, D])).then_inc(w_in, 16)
            sp.dma_start(m2r[:], dram["aa2"].broadcast_to([128, FF])).then_inc(w_in, 16)

        @block.tensor
        def _(pe):
            for c in range(NC):
                ln.mean(pe, c)
                ln.var(pe, c)
            pe.wait_ge(prep, PREP_STEPS)

            def up(c):
                pe.wait_ge(qstep, 3 * (c + 1))
                for f in range(NF):
                    n = c * NF + f
                    if n >= 4:
                        pe.wait_ge(gelu_ready, n - 3)
                    for a in range(2):
                        last = nc.tensor.matmul(ps[n % 4][:, 0:CW], q1[:, a, f * 128:(f + 1) * 128], xq[:, c % 2, a], start=a == 0, stop=a == 1)
                    last.then_inc(up_ready, 1)

            def down(c):
                pe.wait_ge(gstep, 4 * (c + 1))
                if c >= 2:
                    pe.wait_ge(y_ready, 2 * (c - 1))
                for m in range(2):
                    for f in range(NF):
                        last = nc.tensor.matmul(ps[4 + 2 * (c % 2) + m][0:HD, 0:CW], q2[:, f, m * HD:(m + 1) * HD], gq[:, c % 2, f],
                                                start=f == 0, stop=f == NF - 1)
                    last.then_inc(down_ready, 1)

            up(0)
            for c in range(NC):
                if c + 1 < NC:
                    up(c + 1)
                down(c)

        @block.scalar
        def _(act):
            for c in range(NC):
                ln.square(act, c)
                ln.rstd(act, c)

            def gelu(c):
                for f in range(NF):
                    n = c * NF + f
                    act.wait_ge(up_ready, n + 1)
                    if c >= 2 and f == 0:
                        act.wait_ge(gstep, 4 * (c - 1))
                    nc.scalar.activation(g[:, c % 2, f], ps[n % 4][:, 0:CW], ACT.Gelu, bias=cols(env, name + "_b1")[:, f:f + 1],
                                         scale=s1[:, f:f + 1]).then_inc(gelu_ready, 1)

            def out(c):
                for m in range(2):
                    act.wait_ge(down_ready, 2 * c + m + 1)
                    if c >= 2:
                        act.wait_ge(added, c - 1)
                    nc.scalar.activation(y[:, c % 2, m], ps[4 + 2 * (c % 2) + m][0:HD, 0:CW], ACT.Identity,
                                         bias=cols(env, name + "_b2")[0:HD, m:m + 1], scale=s2[:, m:m + 1]).then_inc(y_ready, 1)

            act.wait_ge(prep, PREP_STEPS)
            gelu(0)
            for c in range(NC):
                if c + 1 < NC:
                    gelu(c + 1)
                out(c)

        @block.gpsimd
        def _(pool):
            for c in range(NC):
                pool.wait_ge(y_ready, 2 * (c + 1))
                nc.gpsimd.tensor_tensor(chunk(env.h, c), chunk(env.h, c), y[:, c % 2], ALU.add).then_inc(added, 1)
            pool.wait_ge(added, NC)

        @block.vector
        def _(dve):
            V = nc.vector
            steps = [0]

            def link(ins):
                steps[0] += 1
                ins.then_inc(prep, 1)
                dve.wait_ge(prep, steps[0])

            ln.centre(dve, 0)
            ln.scale(dve, 0)
            dve.wait_ge(w_in, 96)
            link(V.reduce_sum(mean1[:], m1r[:], AX_X))
            link(V.tensor_scalar(mean1[:], mean1[:], 1.0 / D, None, ALU.mult))
            link(V.reciprocal(inv1[:], mean1[:]))
            link(V.reduce_sum(mean2[:], m2r[:], AX_X))
            link(V.tensor_scalar(mean2[:], mean2[:], 1.0 / FF, None, ALU.mult))
            link(V.reciprocal(inv2[:], mean2[:]))
            link(V.tensor_scalar(s1[:], cols(env, name + "_aw1"), mean1[:, 0:1], None, ALU.mult))
            link(V.tensor_scalar(s2[:], cols(env, name + "_aw2")[0:HD, :], mean2[0:HD, 0:1], None, ALU.mult))
            for w, r, q, shape in ((w1, a1r, q1, [HD, 2, FF]), (w2, a2r, q2, [128, NF, D])):
                link(V.reciprocal(r[:], r[:]))
                link(V.tensor_tensor(w[:], w[:], r[:, None, :].broadcast_to(shape), ALU.mult))
                link(V.tensor_scalar(w[:], w[:], QHI, QLO, ALU.min, ALU.max))
                link(V.tensor_scalar(w[:], w[:], ROUND, None, ALU.add))
                link(V.tensor_scalar(q[:], w[:], ROUND, None, ALU.subtract))
            assert steps[0] == PREP_STEPS, steps[0]
            for c in range(1, NC):
                ln.centre(dve, c)
                ln.scale(dve, c)

            def quant_x(c):
                dve.wait_ge(ln.ready, c + 1)
                if c >= 1:
                    dve.wait_ge(qstep, 3 * c)
                V.tensor_scalar(xt[:], chunk(x, c), inv1[0:HD, 0:1], QHI, ALU.mult, ALU.min).then_inc(qstep, 1)
                dve.wait_ge(qstep, 3 * c + 1)
                V.tensor_scalar(xt[:], xt[:], QLO, ROUND, ALU.max, ALU.add).then_inc(qstep, 1)
                dve.wait_ge(qstep, 3 * c + 2)
                if c >= 2:
                    dve.wait_ge(up_ready, NF * (c - 1))
                V.tensor_scalar(xq[:, c % 2], xt[:], ROUND, None, ALU.subtract).then_inc(qstep, 1)

            def quant_g(c):
                gc = g[:, c % 2]
                dve.wait_ge(gelu_ready, NF * (c + 1))
                V.tensor_scalar(gc, gc, 10.0, -10.0, ALU.min, ALU.max).then_inc(gstep, 1)
                dve.wait_ge(gstep, 4 * c + 1)
                V.tensor_scalar(gc, gc, inv2[:, 0:1], QHI, ALU.mult, ALU.min).then_inc(gstep, 1)
                dve.wait_ge(gstep, 4 * c + 2)
                V.tensor_scalar(gc, gc, QLO, ROUND, ALU.max, ALU.add).then_inc(gstep, 1)
                dve.wait_ge(gstep, 4 * c + 3)
                if c >= 2:
                    dve.wait_ge(down_ready, 2 * (c - 1))
                V.tensor_scalar(gq[:, c % 2], gc, ROUND, None, ALU.subtract).then_inc(gstep, 1)

            quant_x(0)
            quant_x(1)
            for c in range(NC):
                quant_g(c)
                if c + 2 < NC:
                    quant_x(c + 2)


def stage_class_ffn(env, name, dram):
    nc = env.nc
    x, ps = env.x, env.ps
    x4 = x[:, :, :].rearrange("p a (b n) -> p a b n", n=N)
    NF = FF // 128
    NPT = N - NCLS
    PI = 32
    NPS = B // PI
    PW = PI * NPT
    XW = NCLS * B
    with ExitStack() as ctx:
        def sb(n, shape, dt=F32):
            return ctx.enter_context(nc.sbuf_tensor(name + "_" + n, shape, dt))

        def sem(n):
            return env.sem(name + "_" + n)

        w1, w2 = sb("w1", [HD, 6, 2, FF]), sb("w2", [128, 6, NF, D])
        gw = sb("gw", [HD, 2, NCLS, 2])
        gwx = sb("gwx", [HD, 2, NCLS, 2, HD])
        z1 = sb("z1", [HD, NCLS, B])
        gate = sb("gate", [HD, 2, NCLS, B])
        hp = sb("hp", [128, 2, NF, PW])
        hx = sb("hx", [128, 2, NF, NCLS, B])
        wy = sb("wy", [HD, 2, 2, NCLS, B])
        ln = Norm(env, name + "_ln", x)
        gw_in, gw_spread, z_ready, z1_moved, gates_ready = (sem(n) for n in ("gw_in", "gw_spread", "z_ready", "z1_moved", "gates_ready"))
        w_in = [sem(f"w{i}_in") for i in range(6)]
        up_ready, gelu_ready, down_ready, patch_added = (sem(n) for n in ("up_ready", "gelu_ready", "down_ready", "patch_added"))
        pair_ready, gated, pair_added = sem("pair_ready"), sem("gated"), sem("pair_added")
        block = ctx.enter_context(nc.Block())
        ups = [(0, slice(2 * a, 2 * a + 2)) for a in range(3)] + [(1, slice(a, NCLS, 2)) for a in range(2)]
        downs = [(1, slice(2 * e, 2 * e + 2)) for e in range(3)] + [(0, slice(e, NCLS, 2)) for e in range(2)]
        NU = NPS * NF

        @block.sync
        def _(sp):
            sp.dma_start(gw[:], dram["gw"]).then_inc(gw_in, 16)
            for i in range(6):
                w1d = dram["p1"] if i == 0 else dram["e1"][i - 1]
                w2d = dram["p2"] if i == 0 else dram["e2"][i - 1]
                sp.dma_start(w1[:, i], w1d.rearrange("(a p) f -> p a f", p=HD)).then_inc(w_in[i], 16)
                sp.dma_start(w2[:, i], w2d.rearrange("(j p) f -> p j f", p=128)).then_inc(w_in[i], 16)

        @block.tensor
        def _(pe):
            for c in range(NC):
                ln.mean(pe, c)
                ln.var(pe, c)
            pe.wait_ge(ln.ready, NC)

            def up(s):
                for f in range(NF):
                    n = s * NF + f
                    if n >= 2:
                        pe.wait_ge(gelu_ready, n - 1)
                    for a in range(2):
                        last = nc.tensor.matmul(ps[2 + n % 2][:, 0:PW], w1[:, 0, a, f * 128:(f + 1) * 128],
                                                x4[:, a, s * PI:(s + 1) * PI, NCLS:N], start=a == 0, stop=a == 1)
                    last.then_inc(up_ready, 1)

            def down(s):
                pe.wait_ge(gelu_ready, NF * (s + 1))
                for m in range(2):
                    for f in range(NF):
                        last = nc.tensor.matmul(ps[4 + 2 * s + m][0:HD, 0:PW], w2[:, 0, f, m * HD:(m + 1) * HD], hp[:, s, f],
                                                start=f == 0, stop=f == NF - 1)
                    last.then_inc(down_ready, 1)

            pe.wait_ge(w_in[0], 32)
            up(0)
            up(1)
            down(0)
            pe.wait_ge(gw_spread, 1)
            for j in range(2):
                for i in range(NCLS):
                    for a in range(2):
                        last = nc.tensor.matmul(ps[j][0:HD, i * B:(i + 1) * B], gwx[:, a, i, j], x4[:, a, :, i], start=a == 0, stop=a == 1)
            last.then_inc(z_ready, 1)
            down(1)
            n = NU
            for e, (member, pos) in enumerate(ups):
                pe.wait_ge(w_in[1 + e], 32)
                w = B * len(range(NCLS)[pos])
                for f in range(NF):
                    pe.wait_ge(gelu_ready, n - 1)
                    for a in range(2):
                        last = nc.tensor.matmul(ps[2 + n % 2][:, 0:w], w1[:, 1 + e, a, f * 128:(f + 1) * 128],
                                                x4[:, a, :, pos].rearrange("p b n -> p n b"), start=a == 0, stop=a == 1)
                    last.then_inc(up_ready, 1)
                    n += 1
            pe.wait_ge(gelu_ready, n)
            pe.wait_ge(patch_added, 2 * NPS)
            for member in (1, 0):
                for m in range(2):
                    for e, (mem, pos) in enumerate(downs):
                        if mem != member:
                            continue
                        to = ps[4 + 2 * member + m][0:HD, 0:XW].rearrange("p (n b) -> p n b", b=B)[:, pos]
                        for f in range(NF):
                            last = nc.tensor.matmul(to, w2[:, 1 + e, f, m * HD:(m + 1) * HD], hx[:, member, f, pos],
                                                    start=f == 0, stop=f == NF - 1)
                    last.then_inc(pair_ready, 1)

        @block.scalar
        def _(act):
            act.wait_ge(gw_in, 16)
            nc.scalar.activation(gwx[:].rearrange("p a n g d -> p (a n g) d"),
                                 gw[:].rearrange("p a n g -> p (a n g)")[:, :, None].broadcast_to([HD, 4 * NCLS, HD]), ACT.Copy).then_inc(gw_spread, 1)
            for c in range(NC):
                ln.square(act, c)
                ln.rstd(act, c)
            for n in range(NU):
                act.wait_ge(up_ready, n + 1)
                s, f = n // NF, n % NF
                nc.scalar.activation(hp[:, s, f], ps[2 + n % 2][:, 0:PW], ACT.Gelu, bias=cols(env, name + "_pb1")[:, f:f + 1]).then_inc(gelu_ready, 1)
            act.wait_ge(z_ready, 1)
            nc.scalar.activation(z1[:].rearrange("p n b -> p (n b)"), ps[1][0:HD, 0:XW], ACT.Copy).then_inc(z1_moved, 1)
            n = NU
            for e, (member, pos) in enumerate(ups):
                w = B * len(range(NCLS)[pos])
                for f in range(NF):
                    act.wait_ge(up_ready, n + 1)
                    nc.scalar.activation(hx[:, member, f, pos], ps[2 + n % 2][:, 0:w].rearrange("p (n b) -> p n b", b=B), ACT.Gelu,
                                         bias=cols(env, f"{name}_eb1{e}")[:, f:f + 1]).then_inc(gelu_ready, 1)
                    n += 1

        @block.vector
        def _(dve):
            V = nc.vector
            for c in range(NC):
                ln.centre(dve, c)
                ln.scale(dve, c)
            for s in range(NPS):
                for m in range(2):
                    dve.wait_ge(down_ready, 2 * s + m + 1)
                    hc = env.h4[:, m, s * PI:(s + 1) * PI, NCLS:N]
                    V.scalar_tensor_tensor(hc, ps[4 + 2 * s + m][0:HD, 0:PW].rearrange("p (b n) -> p b n", n=NPT),
                                           cols(env, name + "_pb2")[0:HD, m:m + 1], hc, ALU.add, ALU.add).then_inc(patch_added, 1)
                if s == 0:
                    dve.wait_ge(z1_moved, 1)
                    z0 = ps[0][0:HD, 0:XW].rearrange("p (n b) -> p n b", b=B)
                    V.tensor_tensor(gate[:, 0], z0, z1[:], ALU.is_gt).then_inc(gates_ready, 1)
                    V.tensor_tensor(gate[:, 1], z0, z1[:], ALU.is_lt).then_inc(gates_ready, 1)
            dve.wait_ge(gates_ready, 2)
            ng = 0
            for k, member in enumerate((1, 0)):
                for m in range(2):
                    dve.wait_ge(pair_ready, 2 * k + m + 1)
                    for e, (mem, pos) in enumerate(downs):
                        if mem == member:
                            src = ps[4 + 2 * member + m][0:HD, 0:XW].rearrange("p (n b) -> p n b", b=B)[:, pos]
                            V.scalar_tensor_tensor(wy[:, member, m, pos], src, cols(env, f"{name}_eb2{e}")[0:HD, m:m + 1],
                                                   gate[:, member, pos], ALU.add, ALU.mult).then_inc(gated, 1)
                            ng += 1
                    hc = env.h4[:, m, :, 0:NCLS].rearrange("p b n -> p n b")
                    dve.wait_ge(gated, ng)
                    if k == 1:
                        dve.wait_ge(pair_added, m + 1)
                    V.tensor_tensor(hc, hc, wy[:, member, m], ALU.add).then_inc(pair_added, 1)
            dve.wait_ge(pair_added, 4)


PREP_STEPS = 18
ROUND = 1.5 * 2.0 ** 23
QLO, QHI = -8.0, 7.0
PI_DOWN = 3.1415925
SN = 64
NCLS = 6


def halves(v):
    return np.ascontiguousarray(np.moveaxis(np.asarray(v).reshape(2, HD, *np.shape(v)[1:]), 0, 1))


def tiles(v):
    return np.ascontiguousarray(np.asarray(v).reshape(-1, 128).T)


COLS = {}


def pack_columns(parts):
    out, at = [], 0
    for name, v in parts:
        v = np.asarray(v)
        n = v.shape[1]
        col = np.zeros((128, n), np.float32)
        col[:v.shape[0]] = v
        COLS[name] = (at, n)
        at += n
        out.append(col)
    return np.concatenate(out, 1)


def constants():
    f = np.arange(HD)
    mean_w = np.zeros((128, HD), np.float32)
    mean_w[:HD] = 1.0 / D
    head_mask = np.zeros((128, HH), np.float32)
    head_mask[:HD] = (f[:, None] // HW == np.arange(HH)[None])
    head_mean = np.zeros((128, HD), np.float32)
    head_mean[:HD] = (f[:, None] // HW == f[None] // HW) / HW
    ident = np.eye(128, dtype=np.float32)
    d = np.arange(WD)
    inv = (1.0 / np.float32(THETA) ** (np.arange(0, WD, 2, dtype=np.float32) / np.float32(WD))).astype(np.float32)
    angle = (inv[d // 2][:, None] * np.arange(N, dtype=np.float32)[None]).astype(np.float32)
    cos = np.tile(np.cos(angle), (2, 1)).astype(np.float32)
    sin = np.tile(np.sin(angle) * np.where(d % 2, 1, -1)[:, None], (2, 1)).astype(np.float32)
    causal = np.full((128, KVH * N), MASKED, np.float32)
    r = np.arange(QH // 2 * N)
    kc = np.arange(KVH * N)
    seen = ((r[:, None] // N) // (QH // KVH // 2) == kc[None] // N) & (kc[None] % N <= r[:, None] % N)
    causal[:len(r)][seen] = 0.0
    ones = np.ones((128, 128), np.float32)
    earlier = np.triu(np.ones((128, 128), np.float32), 1)
    valid = np.ones((128, -(-T // 128)), np.float32)
    valid[T % 128 or 128:, -1] = 0
    tile_no = np.tile(np.arange(MOE_TILES, dtype=np.float32), (128, 1))
    image_mask = (np.arange(128)[:, None] // SLOT == np.arange(4)[None]).astype(np.float32)
    conj = np.where(np.arange(128) < QB, 1, -1).astype(np.float32)[:, None]
    return [("earlier", earlier), ("valid", valid), ("tile_no", tile_no), ("ones", ones), ("image_mask", image_mask), ("conj", conj), ("cos", cos), ("sin", sin), ("causal", causal),
            ("mean_w", mean_w), ("head_mask", head_mask), ("head_mean", head_mean), ("ident", ident)]


def build(nc, d, out, stages, con_at, con_n):
    ctx = ExitStack()
    with ctx:
        env = Env(nc, ctx)
        env.h = env.sb("h", [HD, 2, T])
        env.h4 = env.h[:, :, :].rearrange("p a (b n) -> p a b n", n=N)
        env.x = env.sb("x", [HD, 2, T])
        env.x2 = env.sb("x2", [HD, 2, T])
        env.sq = env.sb("ln_sq", [HD, 2, 2, CW])
        env.rs = env.sb("ln_rs", [HD, 2, CW])
        env.ln_eps = env.sb("ln_eps", [128, 1])
        env.rms_eps = env.sb("rms_eps", [128, 1])
        env.vec = env.sb("vec", [128, d["vec"].shape[1]])
        env.vec_dram = d["vec"]
        env.vec_in = env.keep_sem("vec_in")
        env.con = env.sb("con", [128, con_n])
        env.con_dram = d["con"]
        env.con_in = env.keep_sem("con_in")

        def con(name, rows):
            a, n = con_at[name]
            return env.con[0:rows, a:a + n]
        env.mean_w, env.head_mask, env.head_mean, env.ident = con("mean_w", HD), con("head_mask", HD), con("head_mean", HD), con("ident", 128)
        env.ones, env.image_mask, env.conj = con("ones", 128), con("image_mask", 128), con("conj", 2 * QB)
        env.earlier, env.valid, env.tile_no = con("earlier", 128), con("valid", 128), con("tile_no", 1)
        env.x_slots = nc.dram_tensor("x_slots", (MOE_TILES * 128, D), F32).ap()
        env.y_slots = nc.dram_tensor("y_slots", (MOE_TILES * 128, D), F32).ap()
        env.slots_zero = env.keep_sem("slots_zero")
        env.cos, env.sin, env.causal = con("cos", 128), con("sin", 128), con("causal", QH // 2 * N)
        env.psall = ctx.enter_context(nc.psum_tensor("banks", [128, 8, 512], F32))
        env.ps = [env.psall[:, i, :] for i in range(8)]

        def of(name):
            return {n[len(name) + 1:]: ap for n, ap in d.items() if n.startswith(name + "_")}

        plan = [lambda: stage_tokens(env, d["patches"], d["tok_w"], d["tok_pos"]),
                lambda: stage_narrow_attention(env, "a0", of("a0"), rms=True),
                lambda: stage_wide_attention(env, "g0", of("g0")),
                lambda: stage_routed_ffn(env, "moe", of("moe"), env.x2, NE, 2, MOE_TILES),
                lambda: stage_convolution(env, "s1", of("s1")),
                lambda: stage_quantised_ffn(env, "f1", of("f1")),
                lambda: stage_narrow_attention(env, "a2", of("a2")),
                lambda: stage_class_ffn(env, "f2", of("f2")),
                lambda: stage_narrow_attention(env, "a3", of("a3"), quantum=True),
                lambda: stage_routed_ffn(env, "f3", of("f3"), env.x, NX, 1, TOP1_TILES, norm=True)]
        for stage in plan[:stages]:
            stage()
            env.end_stage()

        stored = env.sem("out_stored")
        with nc.Block() as block:
            @block.sync
            def _(sp):
                sp.dma_start(out, env.h[:]).then_inc(stored, 16)
                sp.wait_ge(stored, 16)


def prepare(inp):
    g = {k: np.asarray(v) for k, v in inp.items()}
    x = g["x"].reshape(NC, IC, 4, 16, 4, 16, 3)
    px = x.transpose(3, 5, 6, 0, 1, 2, 4).reshape(KP, 128, NC, IC * NP)
    a = {"patches": np.ascontiguousarray(px.transpose(2, 1, 0, 3)),
         "tok_w": np.ascontiguousarray(g["L0_tok_W"].reshape(KP, 128, D).transpose(1, 0, 2)),
         "tok_pos": halves(g["L0_tok_pos_emb"].T)}
    a["a0_wqkv"] = halves(g["L0_attn_qkv_w"].T)
    a["a0_wo"] = halves(g["L0_attn_proj_w"].T)
    w = g["L0_ffn_w_qkv"]
    a["g0_wq"] = halves(w[:, 0:QH * WD])
    wk = w[:, QH * WD:(QH + KVH) * WD].reshape(D, KVH, 1, WD)
    a["g0_wk"] = halves(np.broadcast_to(wk, (D, KVH, 2, WD)).reshape(D, KVH * 2 * WD))
    a["g0_wv"] = halves(w[:, (QH + KVH) * WD:])
    a["g0_wo"] = np.ascontiguousarray(g["L0_ffn_w_out"].reshape(QH // 2, 128, D).transpose(1, 0, 2))
    a["moe_wr"] = halves(g["L0_ffn_w_router"])
    a["moe_up"] = np.ascontiguousarray(g["L0_ffn_w_gate_up"].reshape(NE, 2, HD, 2 * EF).transpose(0, 2, 1, 3))
    a["moe_down"] = g["L0_ffn_w_down"]
    b = g["L0_attn_qkv_b"]
    a["s1_prm"] = np.ascontiguousarray(np.stack([halves(g["L1_attn_" + n]) for n in ("A_real", "A_imag", "B_mat", "C_mat")], 1))
    a["f1_w1"] = halves(g["L1_ffn_w1"].T)
    a["f1_w2"] = np.ascontiguousarray(g["L1_ffn_w2"].T.reshape(FF // 128, 128, D).transpose(1, 0, 2))
    for n, src in (("aw1", "alpha_w1"), ("aw2", "alpha_w2"), ("aa1", "alpha_a1"), ("aa2", "alpha_a2")):
        a["f1_" + n] = g["L1_ffn_" + src][None]
    a["a2_wqkv"], a["a2_wo"] = halves(g["L2_attn_qkv_w"].T), halves(g["L2_attn_proj_w"].T)
    a["f2_p1"], a["f2_p2"], a["f2_e1"], a["f2_e2"] = (g["L2_ffn_" + n] for n in ("moe0_W1", "moe0_W2", "A1_W", "A2_W"))
    a["f2_gw"] = halves(g["L2_ffn_G_W"].transpose(1, 0, 2))
    a["a3_wqkv"], a["a3_wo"] = halves(g["L3_attn_in_w"].T), halves(g["L3_attn_out_w"].T)
    swap = np.r_[8:16, 0:8]
    a["a3_wsp"] = halves(np.concatenate([g["L3_attn_sp_w"].T, g["L3_attn_sp_w"].T[:, swap]], 1))
    a["a3_qw"] = g["L3_attn_qw"].reshape(1, 1)
    a["f3_wr"], a["f3_bg"], a["f3_b2"], a["f3_down"] = halves(g["L3_ffn_Wg"]), g["L3_ffn_bg"][None], g["L3_ffn_b2"][None], g["L3_ffn_W2"]
    w1 = g["L3_ffn_W1"].reshape(NX, 2, HD, FF).transpose(0, 2, 1, 3)
    b1 = np.broadcast_to(g["L3_ffn_b1"][:, None, None], (NX, 1, 2, FF))
    a["f3_up"] = np.ascontiguousarray(np.concatenate([w1, b1], 1))
    more = [("s1_ld", halves(g["L1_attn_log_delta"])), ("f1_b1", tiles(g["L1_ffn_b1"])), ("f1_aw1", tiles(g["L1_ffn_alpha_w1"])),
            ("f1_b2", halves(g["L1_ffn_b2"])), ("f1_aw2", halves(g["L1_ffn_alpha_w2"])),
            ("f2_pb1", tiles(g["L2_ffn_moe0_b1"])), ("f2_pb2", halves(g["L2_ffn_moe0_b2"])),
            ("a3_spb", g["L3_attn_sp_b"][:, None]), ("a3_spbx", g["L3_attn_sp_b"][swap][:, None])]
    for e in range(5):
        more += [(f"f2_eb1{e}", tiles(g["L2_ffn_A1_b"][e])), (f"f2_eb2{e}", halves(g["L2_ffn_A2_b"][e]))]
    for n, bias, out in (("a2", g["L2_attn_qkv_b"], g["L2_attn_proj_b"]), ("a3", g["L3_attn_in_b"], g["L3_attn_out_b"])):
        more += [(f"{n}_{v}b", halves(bias[i * D:(i + 1) * D])) for i, v in enumerate("qkv")] + [(n + "_ob", halves(out))]
    parts = more + [("tok_b", halves(g["L0_tok_b"])), ("cls", halves(g["cls_tok"].reshape(D))),
             ("a0_qb", halves(b[0:D])), ("a0_kb", halves(b[D:2 * D])), ("a0_vb", halves(b[2 * D:])),
             ("n1w", halves(g["L0_ffn_norm1_w"])), ("n2w", halves(g["L0_ffn_norm2_w"])),
             ("a0_ob", halves(g["L0_attn_proj_b"])),
             ("a0_qn", np.tile(g["L0_attn_q_norm_w"], HH)[:, None]), ("a0_kn", np.tile(g["L0_attn_k_norm_w"], HH)[:, None])]
    a["vec"] = pack_columns(parts)
    cons = constants()
    at, con_at = 0, {}
    for n, v in cons:
        con_at[n] = (at, v.shape[1])
        at += v.shape[1]
    a["con"] = np.concatenate([v for _, v in cons], 1)
    return a, con_at, at


STAGES = 99


def kernel(**inputs):
    import concourse.bacc as _bacc
    from concourse.bass_utils import run_bass_kernel_spmd as _run

    nc = _bacc.Bacc("TRN2", target_bir_lowering=False, num_devices=1)
    arrays, con_at, con_n = prepare(inputs)
    arrays = {"in_" + n: a for n, a in arrays.items()}
    d = {n[3:]: nc.dram_tensor(n, a.shape, mybir.dt.from_np(a.dtype), kind="ExternalInput").ap() for n, a in arrays.items()}
    out = nc.dram_tensor("out", (HD, 2, T), F32, kind="ExternalOutput").ap()
    build(nc, d, out, STAGES, con_at, con_n)
    r = _run(nc, [arrays], core_ids=[0])
    got = np.asarray(r.results[0]["out"])
    return np.ascontiguousarray(got.transpose(2, 1, 0)).reshape(B, N, D)
```

```python
from contextlib import ExitStack

import numpy as np

import concourse.bass as bass
from concourse import mybir
from concourse.alu_op_type import AluOpType as ALU

F32 = mybir.dt.float32
BF16 = mybir.dt.bfloat16
I32 = mybir.dt.int32
U32 = mybir.dt.uint32
ACT = mybir.ActivationFunctionType
AX_X = mybir.AxisListType.X

B = 64
NP = 16
N = NP + 1
T = B * N
D = 192
HD = 96
HN = 12
HW = 16
HH = HN // 2
NC = 4
IC = B // NC
CW = IC * N
GI = 8
GPC = IC // GI
NG = B // GI
GW = GI * N
SLOT = 32
PD = 768
KP = PD // 128
LN_EPS = 1e-5
RMS_EPS = 1e-6
FF = 768
QH = 12
KVH = 3
WD = 64
THETA = 10000.0
QB = 8
QR = 3 * SLOT + N
NE = 16
EF = 384
NX = 4
MOE_TILES = (2 * T + NE * 127) // 128
TOP1_TILES = (T + NX * 127) // 128
MASKED = -1e30


class Env:

    def __init__(self, nc, ctx):
        self.nc, self.ctx, self.of_stage = nc, ctx, []

    def sb(self, name, shape, dt=F32):
        return self.ctx.enter_context(self.nc.sbuf_tensor(name, shape, dt))

    def keep_sem(self, name):
        return self.ctx.enter_context(self.nc.semaphore(name))

    def sem(self, name):
        self.of_stage.append(self.nc.alloc_semaphore(name))
        return self.of_stage[-1]

    def end_stage(self):
        self.nc.clear_and_free_semaphores(self.of_stage)
        self.of_stage = []
        self.nc.all_engine_barrier()


def cols(env, name):
    a, n = COLS[name]
    return env.vec[:, a:a + n]


def chunk(ap3, c):
    return ap3[:, :, c * CW:(c + 1) * CW]


class Norm:

    def __init__(self, env, name, x, done, counts, var_banks=(1,) * NC):
        self.env, self.x, self.done, self.counts, self.var_banks = env, x, done, counts, var_banks
        self.mean_ready = env.sem(name + "_mean_ready")
        self.centred = env.sem(name + "_centred")
        self.squared = env.sem(name + "_squared")
        self.var_ready = env.sem(name + "_var_ready")
        self.log_var = env.sem(name + "_log_var")
        self.rstd_ready = env.sem(name + "_rstd_ready")
        self.ready = env.sem(name + "_x_ready")

    def mean(self, pe, c):
        if c > 0:
            pe.wait_ge(self.centred, c)
        for v in range(c - 1, -1, -1):
            if self.var_banks[v] == 0:
                pe.wait_ge(self.log_var, v + 1)
                break
        pe.wait_ge(self.done, self.counts[c])
        nc, env = self.env.nc, self.env
        for a in range(2):
            last = nc.tensor.matmul(env.ps[0][0:HD, 0:CW], env.mean_w, chunk(env.h, c)[:, a], start=a == 0, stop=a == 1)
        last.then_inc(self.mean_ready, 1)

    def centre(self, dve, c):
        nc, env = self.env.nc, self.env
        dve.wait_ge(self.mean_ready, c + 1)
        nc.vector.tensor_tensor(chunk(self.x, c), chunk(env.h, c), env.ps[0][0:HD, None, 0:CW].broadcast_to([HD, 2, CW]),
                                ALU.subtract).then_inc(self.centred, 1)

    def square(self, act, c):
        nc, env = self.env.nc, self.env
        act.wait_ge(self.centred, c + 1)
        if c >= 2:
            act.wait_ge(self.var_ready, c - 1)
        nc.scalar.activation(env.sq[:, c % 2], chunk(self.x, c), ACT.Square).then_inc(self.squared, 1)

    def var(self, pe, c):
        nc, env = self.env.nc, self.env
        pe.wait_ge(self.squared, c + 1)
        if c > 0:
            pe.wait_ge(self.log_var, c)
        for a in range(2):
            last = nc.tensor.matmul(env.ps[self.var_banks[c]][0:HD, 0:CW], env.mean_w, env.sq[:, c % 2, a], start=a == 0, stop=a == 1)
        last.then_inc(self.var_ready, 1)

    def rstd(self, act, c):
        nc, env = self.env.nc, self.env
        act.wait_ge(self.var_ready, c + 1)
        if c >= 2:
            act.wait_ge(self.ready, c - 1)
        nc.scalar.activation(env.rs[:, c % 2], env.ps[self.var_banks[c]][0:HD, 0:CW], ACT.Ln, bias=env.ln_eps[0:HD, :]).then_inc(self.log_var, 1)
        act.wait_ge(self.log_var, c + 1)
        nc.scalar.activation(env.rs[:, c % 2], env.rs[:, c % 2], ACT.Exp, scale=-0.5).then_inc(self.rstd_ready, 1)

    def scale(self, dve, c):
        nc, env = self.env.nc, self.env
        dve.wait_ge(self.rstd_ready, c + 1)
        nc.vector.tensor_tensor(chunk(self.x, c), chunk(self.x, c), env.rs[:, c % 2, None, :].broadcast_to([HD, 2, CW]),
                                ALU.mult).then_inc(self.ready, 1)

    def overlapped(self, first, second, engine, start, stop=NC, begun=False):
        for c in range(start, stop):
            if c > start or not begun:
                first(engine, c)
            if c > start:
                second(engine, c - 1)
        second(engine, stop - 1)


class Weights:

    def __init__(self, env, region, name, dram):
        self.env, self.region, self.name, self.dram = env, region, name, dram
        self.allocate()

    def sb(self, n, shape, dt=F32):
        return self.region.enter_context(self.env.nc.sbuf_tensor(f"{self.name}_{n}", shape, dt))

    def sem(self, n):
        return self.env.keep_sem(f"{self.name}_{n}")


class NarrowWeights(Weights):
    def allocate(self):
        self.wqkv, self.wo = self.sb("wqkv", [HD, 2, 3 * D]), self.sb("wo", [HD, 2, D])
        self.w_in, self.wo_in = self.sem("w_in"), self.sem("wo_in")
        if "wsp" in self.dram:
            self.wsp = self.sb("wsp", [HD, 2, 4 * QB])
            self.gate = self.sb("gate", [128, 2])
            self.gate_in = self.sem("gate_in")

    def load(self, sp):
        sp.dma_start(self.wqkv[:], self.dram["wqkv"]).then_inc(self.w_in, 16)
        sp.dma_start(self.wo[:], self.dram["wo"]).then_inc(self.wo_in, 16)
        if "wsp" in self.dram:
            sp.dma_start(self.wsp[:], self.dram["wsp"]).then_inc(self.wo_in, 16)
            sp.dma_start(self.gate[:, 0:1], self.dram["qw"].broadcast_to([128, 1])).then_inc(self.gate_in, 16)


class WideWeights(Weights):
    def allocate(self):
        self.wq, self.wk = self.sb("wq", [HD, 2, QH * WD]), self.sb("wk", [HD, 2, KVH * 2 * WD])
        self.wv, self.wo = self.sb("wv", [HD, 2, KVH * WD]), self.sb("wo", [128, QH // 2, D])
        self.w_in = self.sem("w_in")

    def load(self, sp):
        for n, w in (("wq", self.wq), ("wk", self.wk), ("wv", self.wv), ("wo", self.wo)):
            sp.dma_start(w[:], self.dram[n]).then_inc(self.w_in, 16)


class QuantisedWeights(Weights):

    def allocate(self):
        NF = FF // 128
        self.w1, self.w2 = self.sb("w1", [HD, 2, FF]), self.sb("w2", [128, NF, D])
        self.rows = self.sb("rows", [(FF + D) // HD, HD])
        self.a1r, self.a2r = self.sb("a1r", [HD, FF]), self.sb("a2r", [128, D])
        self.m1r, self.m2r = self.sb("m1r", [128, D]), self.sb("m2r", [128, FF])
        self.q1, self.q2 = self.sb("q1", [HD, 2, FF], BF16), self.sb("q2", [128, NF, D], BF16)
        self.mean1, self.mean2, self.inv1, self.inv2 = (self.sb(n, [128, 1]) for n in ("mean1", "mean2", "inv1", "inv2"))
        self.s1, self.s2 = self.sb("s1", [128, NF]), self.sb("s2", [HD, 2])
        self.w_in, self.rows_in, self.m_in, self.inverse_in = (self.sem(n) for n in ("w_in", "rows_in", "m_in", "inverse_in"))
        self.inverse_dram = self.env.nc.dram_tensor(self.name + "_inverse", (FF + D,), F32).ap()

    def load(self, sp):
        d = self.dram
        sp.dma_start(self.rows[0:FF // HD], d["aw1"].rearrange("o (p f) -> (o p) f", f=HD)).then_inc(self.rows_in, 16)
        sp.dma_start(self.rows[FF // HD:], d["aw2"].rearrange("o (p f) -> (o p) f", f=HD)).then_inc(self.rows_in, 16)
        sp.dma_start(self.w1[:], d["w1"]).then_inc(self.w_in, 16)
        sp.dma_start(self.w2[:], d["w2"]).then_inc(self.w_in, 16)
        sp.dma_start(self.m1r[:], d["aa1"].broadcast_to([128, D])).then_inc(self.m_in, 16)
        sp.dma_start(self.m2r[:], d["aa2"].broadcast_to([128, FF])).then_inc(self.m_in, 16)


class ClassWeights(Weights):
    def allocate(self):
        self.w1, self.w2 = self.sb("w1", [HD, 6, 2, FF]), self.sb("w2", [128, 6, FF // 128, D])
        self.gw = self.sb("gw", [HD, 2, NCLS, 2])
        self.gw_in, self.w_in = self.sem("gw_in"), [self.sem(f"w{i}_in") for i in range(6)]

    def load(self, sp):
        sp.dma_start(self.gw[:], self.dram["gw"]).then_inc(self.gw_in, 16)
        for i in range(6):
            w1d = self.dram["p1"] if i == 0 else self.dram["e1"][i - 1]
            w2d = self.dram["p2"] if i == 0 else self.dram["e2"][i - 1]
            sp.dma_start(self.w1[:, i], w1d.rearrange("(a p) f -> p a f", p=HD)).then_inc(self.w_in[i], 16)
            sp.dma_start(self.w2[:, i], w2d.rearrange("(j p) f -> p j f", p=128)).then_inc(self.w_in[i], 16)


class RouterWeights(Weights):

    def allocate(self):
        E = self.dram["wr"].shape[2]
        self.wr, self.small_in = self.sb("wr", [HD, 2, E]), self.sem("small_in")
        if "bg" in self.dram:
            self.bg, self.b2 = self.sb("bg", [128, E]), self.sb("b2", [128, E, D])

    def load(self, sp):
        sp.dma_start(self.wr[:], self.dram["wr"]).then_inc(self.small_in, 16)
        if "bg" in self.dram:
            sp.dma_start(self.bg[:], self.dram["bg"].broadcast_to(self.bg.shape)).then_inc(self.small_in, 16)
            sp.dma_start(self.b2[:], self.dram["b2"].broadcast_to(self.b2.shape)).then_inc(self.small_in, 16)


class ExpertWeights(Weights):
    def allocate(self):
        up, down = self.dram["up"], self.dram["down"]
        self.E, rows = up.shape[0], up.shape[1]
        self.wu = self.sb("wu", [rows, self.E, 2, up.shape[3]])
        self.wd = self.sb("wd", [128, self.E, down.shape[1] // 128, D])
        self.w_in = [self.sem(f"w{e}_in") for e in range(self.E)]

    def load(self, sp):
        for e in range(self.E):
            sp.dma_start(self.wu[:, e], self.dram["up"][e]).then_inc(self.w_in[e], 16)
            sp.dma_start(self.wd[:, e], self.dram["down"][e].rearrange("(j p) f -> p j f", p=128)).then_inc(self.w_in[e], 16)


def complex_product(link, V, out_re, out_im, a_re, a_im, b_re, b_im, tmp):
    link(V.tensor_tensor(out_re, a_re, b_re, ALU.mult))
    link(V.tensor_tensor(tmp, a_im, b_im, ALU.mult))
    link(V.tensor_tensor(out_re, out_re, tmp, ALU.subtract))
    link(V.tensor_tensor(out_im, a_re, b_im, ALU.mult))
    link(V.tensor_tensor(tmp, a_im, b_re, ALU.mult))
    link(V.tensor_tensor(out_im, out_im, tmp, ALU.add))


class Response:

    def __init__(self, env, region, dram):
        nc = env.nc

        def sb(n, shape):
            return region.enter_context(nc.sbuf_tensor("response_" + n, shape, F32))

        self.env, self.prm_dram = env, dram["prm"]
        self.prm = sb("prm", [HD, 4, 2, SN])
        self.d = sb("delta", [HD, 2, 6])
        self.t = sb("t", [HD, 12, 2, SN])
        self.pw = sb("powers", [HD, 5, 2, 2, SN])
        self.wr, self.wi, self.wt = (sb(n, [HD, 2, N, SN]) for n in ("re", "im", "tmp"))
        self.prm_in, self.dve_step, self.act_step, self.pool_step, self.ready = (
            env.keep_sem("response_" + n) for n in ("prm_in", "dve_step", "act_step", "pool_step", "ready"))

    def on_scalar(self, act):
        nc, d, t = self.env.nc, self.d, self.t
        act.wait_ge(self.dve_step, 2)
        nc.scalar.activation(d[:, :, 1], d[:, :, 0], ACT.Exp, scale=-1.0).then_inc(self.act_step, 1)
        act.wait_ge(self.dve_step, 3)
        nc.scalar.activation(d[:, :, 3], d[:, :, 2], ACT.Ln).then_inc(self.act_step, 1)
        act.wait_ge(self.dve_step, 10)
        nc.scalar.activation(t[:, 0], t[:, 0], ACT.Exp).then_inc(self.act_step, 1)
        act.wait_ge(self.dve_step, 20)
        nc.scalar.activation(t[:, 3], t[:, 3], ACT.Sin).then_inc(self.act_step, 1)
        nc.scalar.activation(t[:, 4], t[:, 4], ACT.Sin).then_inc(self.act_step, 1)

    def on_vector(self, dve):
        nc, d, t, prm = self.env.nc, self.d, self.t, self.prm
        V = nc.vector
        ld = cols(self.env, "s1_ld")[0:HD, :]
        C1, C2 = 6.28125, 0.0019353071795864769
        steps = [0]

        def link(ins):
            steps[0] += 1
            ins.then_inc(self.dve_step, 1)
            dve.wait_ge(self.dve_step, steps[0])

        link(V.tensor_scalar(d[:, :, 4], ld, -1.0, None, ALU.mult))
        link(V.tensor_tensor(d[:, :, 0], ld, d[:, :, 4], ALU.max))
        dve.wait_ge(self.act_step, 1)
        link(V.tensor_scalar(d[:, :, 2], d[:, :, 1], 1.0, None, ALU.add))
        link(V.tensor_scalar(d[:, :, 4], d[:, :, 2], 1.0, None, ALU.subtract))
        link(V.tensor_tensor(d[:, :, 4], d[:, :, 1], d[:, :, 4], ALU.subtract))
        link(V.reciprocal(d[:, :, 5], d[:, :, 2]))
        dve.wait_ge(self.act_step, 2)
        link(V.tensor_tensor(d[:, :, 4], d[:, :, 4], d[:, :, 5], ALU.mult))
        V.tensor_scalar(d[:, :, 5], ld, 0.0, None, ALU.max)
        link(V.tensor_tensor(d[:, :, 3], d[:, :, 3], d[:, :, 4], ALU.add))
        link(V.tensor_tensor(d[:, :, 0], d[:, :, 3], d[:, :, 5], ALU.add))
        dve.wait_ge(self.prm_in, 16)
        delta = d[:, :, 0:1].broadcast_to([HD, 2, SN])
        ar, ai = prm[:, 0], prm[:, 1]
        link(V.tensor_tensor(t[:, 0], ar, delta, ALU.mult))
        link(V.tensor_tensor(t[:, 1], ai, delta, ALU.mult))
        link(V.tensor_scalar(t[:, 2], t[:, 1], float(1 / (2 * np.pi)), ROUND, ALU.mult, ALU.add))
        link(V.tensor_scalar(t[:, 2], t[:, 2], ROUND, None, ALU.subtract))
        link(V.scalar_tensor_tensor(t[:, 1], t[:, 2], -C1, t[:, 1], ALU.mult, ALU.add))
        link(V.scalar_tensor_tensor(t[:, 1], t[:, 2], -C2, t[:, 1], ALU.mult, ALU.add))
        link(V.tensor_scalar(t[:, 3], t[:, 1], PI_DOWN, -PI_DOWN, ALU.min, ALU.max))
        link(V.tensor_scalar(t[:, 4], t[:, 1], float(np.pi / 2), None, ALU.add))
        link(V.tensor_scalar(t[:, 5], t[:, 4], PI_DOWN, float(2 * np.pi), ALU.is_gt, ALU.mult))
        link(V.tensor_tensor(t[:, 4], t[:, 4], t[:, 5], ALU.subtract))
        link(V.tensor_scalar(t[:, 4], t[:, 4], PI_DOWN, -PI_DOWN, ALU.min, ALU.max))
        link(V.tensor_tensor(t[:, 6], ar, ar, ALU.mult))
        link(V.tensor_tensor(t[:, 7], ai, ai, ALU.mult))
        link(V.tensor_tensor(t[:, 6], t[:, 6], t[:, 7], ALU.add))
        link(V.reciprocal(t[:, 6], t[:, 6]))

    def on_pool(self, pool, part):
        V, t, pw, wr, wi, wt, prm = self.env.nc.gpsimd, self.t, self.pw, self.wr, self.wi, self.wt, self.prm

        def link(ins):
            self.steps += 1
            ins.then_inc(self.pool_step, 1)
            pool.wait_ge(self.pool_step, self.steps)

        if part == 0:
            self.steps = 0
            ar, ai, bm, cm = (prm[:, i] for i in range(4))
            abr, abi = pw[:, 0, 0], pw[:, 0, 1]
            link(V.tensor_tensor(abi, t[:, 0], t[:, 3], ALU.mult))
            link(V.tensor_tensor(abr, t[:, 0], t[:, 4], ALU.mult))
            for i in range(4):
                complex_product(link, V, pw[:, i + 1, 0], pw[:, i + 1, 1], pw[:, i, 0], pw[:, i, 1], pw[:, i, 0], pw[:, i, 1], t[:, 8])
            link(V.tensor_scalar(t[:, 9], abr, 1.0, None, ALU.subtract))
            link(V.tensor_scalar(t[:, 10], ai, -1.0, None, ALU.mult))
            complex_product(link, V, wr[:, :, 0], wi[:, :, 0], t[:, 9], abi, ar, t[:, 10], t[:, 8])
            link(V.tensor_tensor(t[:, 6], t[:, 6], bm, ALU.mult))
            link(V.tensor_tensor(t[:, 6], t[:, 6], cm, ALU.mult))
            link(V.tensor_tensor(wr[:, :, 0], wr[:, :, 0], t[:, 6], ALU.mult))
            link(V.tensor_tensor(wi[:, :, 0], wi[:, :, 0], t[:, 6], ALU.mult))
        doublings = ((), ((0, 1, 1), (1, 2, 2), (2, 4, 4)), ((3, 8, 8),), ((4, 16, 1),))[part]
        for i, at, n in doublings:
            power = [pw[:, i, q, :, None, :].broadcast_to([HD, 2, n, SN]) for q in range(2)]
            complex_product(link, V, wr[:, :, at:at + n], wi[:, :, at:at + n], wr[:, :, 0:n], wi[:, :, 0:n],
                            power[0], power[1], wt[:, :, 0:n])
        if part == 3:
            pool.sem_inc(self.ready, 1)

    def sum_up(self, dve):
        dve.wait_ge(self.ready, 1)
        self.env.nc.vector.reduce_sum(self.env.taps[:], self.wr[:], AX_X)


def stage_tokens(env, patches, w, pos, response, ahead=()):
    nc = env.nc
    with ExitStack() as ctx:
        px = ctx.enter_context(nc.sbuf_tensor("patch_px", [128, NC, KP, IC * NP], F32))
        ws = ctx.enter_context(nc.sbuf_tensor("patch_w", [128, KP, D], F32))
        posb = ctx.enter_context(nc.sbuf_tensor("patch_pos", [HD, 2, NP], F32))
        zero = ctx.enter_context(nc.sbuf_tensor("slots_zeros", [128, D], F32))
        w_in, pos_in, zero_ready = env.sem("tok_w_in"), env.sem("tok_pos_in"), env.sem("zero_ready")
        px_in = [env.sem(f"tok_px{c}_in") for c in range(NC)]
        posb_ready, embedded, cls_in, placed = (env.sem("tok_" + n) for n in ("posb_ready", "embedded", "cls_placed", "placed"))
        eps_ready = env.sem("eps_ready")
        ln = Norm(env, "tok_ln", env.x, placed, [2 * (c + 1) for c in range(NC)])
        block = ctx.enter_context(nc.Block())

        @block.sync
        def _(sp):
            sp.dma_start(ws[:], w).then_inc(w_in, 16)
            for c in range(NC):
                sp.dma_start(px[:, c], patches[c]).then_inc(px_in[c], 16)
            sp.wait_ge(zero_ready, 1)
            sp.dma_start(env.x_slots.rearrange("(t p) f -> p t f", p=128), zero[:, None, :].broadcast_to([128, MOE_TILES, D]))\
                .then_inc(env.slots_zero, 16)
            for weights in ahead:
                weights.load(sp)
            sp.wait_ge(env.slots_zero, 16)

        @block.scalar
        def _(act):
            act.preload_act_table_set("natural_log_exp_and_others")
            act.dma_start(env.vec[:], env.vec_dram).then_inc(env.vec_in, 16)
            act.dma_start(posb[:], pos).then_inc(pos_in, 16)
            act.dma_start(response.prm[:], response.prm_dram).then_inc(response.prm_in, 16)
            act.dma_start(env.con[:], env.con_dram).then_inc(env.con_in, 16)
            act.wait_ge(env.vec_in, 16)
            c3 = cols(env, "cls")[0:HD, :]
            nc.scalar.activation(env.h4[:, :, :, 0], c3[:, :, None].broadcast_to([HD, 2, B]), ACT.Copy).then_inc(cls_in, 1)
            response.on_scalar(act)
            act.preload_act_table_set("natural_log_exp_and_others")
            act.wait_ge(eps_ready, 1)
            ln.overlapped(ln.square, ln.rstd, act, 0)

        @block.gpsimd
        def _(pool):
            pool.memset(zero[:], 0.0).then_inc(zero_ready, 1)
            pool.memset(env.ln_eps[:], LN_EPS)
            pool.memset(env.rms_eps[:], RMS_EPS).then_inc(eps_ready, 1)

        @block.tensor
        def _(pe):
            pe.wait_ge(w_in, 16)
            for c in range(NC):
                pe.wait_ge(px_in[c], 16)
                for m in range(2):
                    for k in range(KP):
                        last = nc.tensor.matmul(env.ps[2 * c + m][0:HD, 0:IC * NP], ws[:, k, m * HD:(m + 1) * HD],
                                                px[:, c, k], start=k == 0, stop=k == KP - 1)
                    last.then_inc(embedded, 1)
                if c == 0:
                    pe.wait_ge(env.con_in, 16)
                    pe.wait_ge(cls_in, 1)
                else:
                    ln.mean(pe, c - 1)
                if c >= 2:
                    ln.var(pe, c - 2)
            ln.mean(pe, NC - 1)
            ln.var(pe, NC - 2)
            ln.var(pe, NC - 1)

        @block.vector
        def _(dve):
            dve.wait_ge(env.vec_in, 16)
            response.on_vector(dve)
            dve.wait_ge(pos_in, 16)
            tb = cols(env, "tok_b")[0:HD, :]
            nc.vector.tensor_tensor(posb[:], posb[:], tb[:, :, None].broadcast_to([HD, 2, NP]), ALU.add).then_inc(posb_ready, 1)
            dve.wait_ge(posb_ready, 1)
            for c in range(NC):
                for m in range(2):
                    dve.wait_ge(embedded, 2 * c + m + 1)
                    src = env.ps[2 * c + m][0:HD, 0:IC * NP].rearrange("p (i n) -> p i n", n=NP)
                    nc.vector.tensor_tensor(env.h4[:, m, c * IC:(c + 1) * IC, 1:N], src,
                                            posb[:, m, None, :].broadcast_to([HD, IC, NP]), ALU.add).then_inc(placed, 1)
                if c == 0:
                    dve.wait_ge(cls_in, 1)
                else:
                    ln.centre(dve, c - 1)
                if c >= 2:
                    ln.scale(dve, c - 2)
            ln.centre(dve, NC - 1)
            ln.scale(dve, NC - 2)
            ln.scale(dve, NC - 1)


def stage_narrow_attention(env, name, weights, rms=False, quantum=False, response=None, ahead=()):
    nc = env.nc
    x, ps = env.x, env.ps
    HP = HN + 1 if quantum else HN
    with ExitStack() as ctx:
        def sb(n, shape, dt=F32):
            return ctx.enter_context(nc.sbuf_tensor(name + "_" + n, shape, dt))

        def sem(n):
            return env.sem(name + "_" + n)

        wqkv, wo, w_in, wo_in = weights.wqkv, weights.wo, weights.w_in, weights.wo_in
        q = sb("q", [HD, 2, 2, CW + SLOT - N])
        k = sb("k", [HD, 2, 2, CW])
        kx = sb("kx", [HD, 2, 2, IC, HH * N])
        vx = sb("vx", [HD, 2, 2, IC, HH * N])
        vt = sb("vt", [HH * N, 2, GI, 2, HD])
        p = sb("p", [128, 2, 2, HP * N])
        pt = sb("pt", [HH * N, 2, 4, 128])
        mx = sb("mx", [128, 2, 2, HP])
        sm = sb("sm", [128, 2, 2, HP])
        cx = sb("cx", [HD, 2, 2, CW])
        pad_zero = sem("pad_zero")
        proj = [sem(f"{n}_proj") for n in "qkvo"]
        qk_evicted, k_spread, v_spread = sem("qk_evicted"), sem("k_spread"), sem("v_spread")
        if rms:
            rsq = sb("rsq", [HD, 2, CW])
            rrs = sb("rrs", [HD, 2, CW])
            raw_evicted, head_sq, head_ms, head_log, head_rstd, head_scaled = (
                sem(n) for n in ("raw_evicted", "head_squared", "head_ms", "head_log", "head_rstd", "head_scaled"))
        if quantum:
            wsp, gate, gate_in = weights.wsp, weights.gate, weights.gate_in
            st = sb("st", [2 * QB, 2, 2, CW + SLOT - N])
            ssq, srs = sb("ssq", [2 * QB, CW]), sb("srs", [2 * QB, CW])
            osq = sb("osq", [128, 2, 2, 2, N])
            px = sb("px", [128, 2, 2, 4, N])
            xt = sb("xt", [4 * N, 2, 2, 2, HD])
            qt = sb("qt", [4 * N, 2, 2, 128])
            gated_b = sb("gated_b", [HD, 2, 2])
            tiny = sb("tiny", [128, 2])
            (s_proj, s_taken, s_squared, s_norm, s_factor, s_scaled, ov_squared, fid_ready, spread, qt_ready, qt_moved, gate_step,
             weighted) = (sem(n) for n in (
                 "s_proj", "s_taken", "s_squared", "s_norm", "s_factor", "s_scaled", "overlap_squared", "fidelity_ready",
                 "q_spread", "qt_ready", "qt_moved", "gate_step", "sm_weighted"))
        FV = GI // 2 + (1 if quantum else 0)
        scored, vt_ready, vt_evicted = sem("scored"), sem("vt_ready"), sem("vt_evicted")
        maxed, shifted, expd, summed, inverted, normed = (sem(n) for n in ("maxed", "shifted", "expd", "summed", "inverted", "normed"))
        pt_ready, pt_evicted, ctx_ready, ctx_evicted, added = (sem(n) for n in ("pt_ready", "pt_evicted", "ctx_ready", "ctx_evicted", "added"))
        ln = Norm(env, name + "_ln", x, added, [2 * (c + 1) for c in range(NC)], var_banks=(0, 0, 1, 1))
        block = ctx.enter_context(nc.Block())
        NT = 4

        @block.sync
        def _(sp):
            for w in ahead:
                w.load(sp)

        @block.tensor
        def _(pe):
            if name == "a0":
                pe.wait_ge(env.con_in, 16)

            def project(c):
                raw = raw_evicted if rms else qk_evicted
                for j in range(3):
                    for m in range(2):
                        if j == 0 and c == 1:
                            pe.wait_ge(s_taken if quantum else v_spread, m + 1)
                        if j == 0 and c >= 2:
                            pe.wait_ge(added, 2 * (c - 2) + m + 1)
                        if j >= 1:
                            pe.wait_ge(raw, NT * c + 2 * (j - 1) + m + 1)
                        for a in range(2):
                            last = nc.tensor.matmul(ps[2 + m][0:HD, 0:CW], wqkv[:, a, j * D + m * HD:j * D + (m + 1) * HD],
                                                    chunk(x, c)[:, a], start=a == 0, stop=a == 1)
                        last.then_inc(proj[j], 1)
                        if rms and j >= 1:
                            head_mean_square(NT * c + 2 * (j - 1) + m)

            def states(c):
                for m in range(2):
                    pe.wait_ge(v_spread, 2 * c + m + 1)
                    for a in range(2):
                        last = nc.tensor.matmul(ps[2 + m][0:2 * QB, 0:CW], wsp[:, a, m * 2 * QB:(m + 1) * 2 * QB],
                                                chunk(x, c)[:, a], start=a == 0, stop=a == 1)
                    last.then_inc(s_proj, 1)

            def state_norms(c):
                pe.wait_ge(s_squared, c + 1)
                if c >= 1:
                    pe.wait_ge(s_factor, 4 * c - 3)
                if c >= 3:
                    pe.wait_ge(ln.log_var, c - 2)
                if c >= 1:
                    pe.wait_ge(qt_moved, GPC * c)
                nc.tensor.matmul(ps[0][0:2 * QB, 0:CW], env.ones[0:2 * QB, 0:2 * QB], ssq[:], start=True, stop=True).then_inc(s_norm, 1)

            def head_mean_square(t):
                pe.wait_ge(head_sq, t + 1)
                if t % NT == 0 and t >= 3 * NT:
                    pe.wait_ge(ln.log_var, t // NT - 2)
                if t > 0:
                    pe.wait_ge(head_log, t)
                nc.tensor.matmul(ps[0][0:HD, 0:CW], env.head_mean, rsq[:, t % 2], start=True, stop=True).then_inc(head_ms, 1)

            def scores(g):
                c = g // GPC
                pe.wait_ge(head_scaled if rms else qk_evicted, NT * c + NT)
                pe.wait_ge(k_spread, 2 * c + 2)
                if quantum:
                    pe.wait_ge(s_scaled, 2 * c + 2)
                if g >= 1:
                    pe.wait_ge(shifted, g)
                for i in range(GI):
                    i16 = (g % GPC) * GI + i
                    for a in range(2):
                        o = (i // 4) * HN * N + a * HH * N
                        last = nc.tensor.matmul(ps[4][SLOT * (i % 4):SLOT * (i % 4 + 1), o:o + HH * N],
                                                q[:, c % 2, a, i16 * N:i16 * N + SLOT], kx[:, c % 2, a, i16, :],
                                                start=True, stop=True)
                    if quantum:
                        o = 2 * HN * N + (i // 4) * 2 * N
                        last = nc.tensor.matmul(ps[4][SLOT * (i % 4):SLOT * (i % 4 + 1), o:o + 2 * N],
                                                st[:, c % 2, 0, i16 * N:i16 * N + SLOT], st[:, c % 2, :, i16 * N:(i16 + 1) * N],
                                                start=True, stop=True)
                last.then_inc(scored, 1)

            def turn_values(g):
                c = g // GPC
                pe.wait_ge(v_spread, 2 * c + 2)
                for f in range(GI // 2):
                    n = g * FV + f
                    if n >= 2:
                        pe.wait_ge(vt_evicted, n - 1)
                    for i in range(2):
                        for a in range(2):
                            o = (2 * i + a) * HD
                            last = nc.tensor.transpose(ps[5 + n % 2][0:HH * N, o:o + HD],
                                                       vx[:, c % 2, a, (g % GPC) * GI + 2 * f + i, :], env.ident[0:HD, 0:HD])
                    last.then_inc(vt_ready, 1)
                if quantum:
                    n = g * FV + FV - 1
                    pe.wait_ge(vt_evicted, n - 1)
                    for f in range(2):
                        for a in range(2):
                            o = (g * GI + 4 * f) * N
                            last = nc.tensor.transpose(ps[5 + n % 2][0:4 * N, (2 * f + a) * HD:(2 * f + a + 1) * HD],
                                                       x[:, a, o:o + 4 * N], env.ident[0:HD, 0:HD])
                    last.then_inc(vt_ready, 1)

            def weigh(g):
                c = g // GPC
                pe.wait_ge(normed, g + 1)
                if g >= 1:
                    pe.wait_ge(pt_evicted, g)
                for f in range(2):
                    for a in range(2):
                        j = 2 * f + a
                        last = nc.tensor.transpose(ps[7][0:HH * N, j * 128:(j + 1) * 128],
                                                   p[:, g % 2, f, a * HH * N:(a + 1) * HH * N], env.ident)
                last.then_inc(pt_ready, 1)
                if quantum:
                    pe.wait_ge(spread, g + 1)
                    pe.wait_ge(s_factor, 4 * c + 1)
                    if c >= 2:
                        pe.wait_ge(ln.log_var, c - 1)
                    if g >= 1:
                        pe.wait_ge(qt_moved, g)
                    for f in range(2):
                        last = nc.tensor.transpose(ps[0][0:4 * N, f * 128:f * 128 + QR],
                                                   px[0:QR, g % 2, f].rearrange("p i k -> p (i k)"), env.ident[0:QR, 0:QR])
                    last.then_inc(qt_ready, 1)
                pe.wait_ge(pt_evicted, g + 1)
                pe.wait_ge(vt_evicted, (g + 1) * FV)
                if g >= 1:
                    pe.wait_ge(ctx_evicted, 2 * g)
                for i in range(GI):
                    for a in range(2):
                        o = a * GW + i * N
                        last = nc.tensor.matmul(ps[1][0:HD, o:o + N], vt[:, g % 2, i, a, :],
                                                pt[:, g % 2, 2 * (i // 4) + a, SLOT * (i % 4):SLOT * (i % 4) + N],
                                                start=True, stop=True)
                last.then_inc(ctx_ready, 1)

            def project_out(c):
                pe.wait_ge(wo_in, 32 if quantum else 16)
                pe.wait_ge(ctx_evicted, 2 * GPC * (c + 1))
                for m in range(2):
                    pe.wait_ge(s_taken if quantum else v_spread, 2 * min(c + 1, NC - 1) + m + 1)
                    if quantum:
                        pe.wait_ge(qt_moved, GPC * (c + 1))
                    if c == NC - 1:
                        pe.wait_ge(added, 2 * (c - 1) + m + 1)
                    for a in range(2):
                        last = nc.tensor.matmul(ps[2 + m][0:HD, 0:CW], wo[:, a, m * HD:(m + 1) * HD], cx[:, c % 2, a],
                                                start=a == 0, stop=a == 1 and not quantum)
                    for f in range(2 * GPC if quantum else 0):
                        last = nc.tensor.matmul(ps[2 + m][0:HD, f * 4 * N:(f + 1) * 4 * N], xt[:, f // 2, f % 2, m],
                                                qt[:, f // 2, f % 2].rearrange("p (i n) -> p i n", n=SLOT)[:, :, 0:N],
                                                start=False, stop=f == 2 * GPC - 1)
                    last.then_inc(proj[3], 1)

            def norm_mean(c, taken):
                if rms:
                    pe.wait_ge(head_log, NT * min(NC, taken + 1))
                if quantum:
                    pe.wait_ge(s_factor, 4 * min(NC, taken + 1) - 3)
                    pe.wait_ge(qt_moved, GPC * taken)
                ln.mean(pe, c)

            pe.wait_ge(w_in, 16)
            if quantum:
                pe.wait_ge(wo_in, 32)
            project(0)
            if quantum:
                states(0)
                state_norms(0)
            for c in range(NC):
                if c >= 2:
                    norm_mean(c - 2, c)
                for g in (2 * c, 2 * c + 1):
                    scores(g)
                    turn_values(g)
                if c >= 2:
                    ln.var(pe, c - 2)
                if c + 1 < NC:
                    project(c + 1)
                weigh(2 * c)
                if quantum and c + 1 < NC:
                    states(c + 1)
                weigh(2 * c + 1)
                if quantum and c + 1 < NC:
                    state_norms(c + 1)
                if c == NC - 1:
                    norm_mean(NC - 2, NC)
                project_out(c)
            ln.overlapped(lambda e, c: norm_mean(c, NC), ln.var, pe, NC - 2, begun=True)

        @block.scalar
        def _(act):
            pre = name

            def take_qk(c):
                for j in range(2):
                    for m in range(2):
                        t = NT * c + 2 * j + m
                        act.wait_ge(proj[j], 2 * c + m + 1)
                        if c >= 2 and j == 0:
                            act.wait_ge(scored, GPC * (c - 1))
                        if c >= 2 and j == 1:
                            act.wait_ge(k_spread, 2 * (c - 1))
                        dst = (q if j == 0 else k)[:, c % 2, m, 0:CW]
                        bias = cols(env, pre + ("_qb" if j == 0 else "_kb"))[0:HD, m:m + 1]
                        nc.scalar.activation(dst, ps[2 + m][0:HD, 0:CW], ACT.Identity, bias=bias)\
                            .then_inc(raw_evicted if rms else qk_evicted, 1)
                        if rms:
                            act.wait_ge(raw_evicted, t + 1)
                            if t >= 2:
                                act.wait_ge(head_ms, t - 1)
                            nc.scalar.activation(rsq[:, t % 2], dst, ACT.Square).then_inc(head_sq, 1)
                            if t % NT:
                                head_rms(t - 1)
                if rms:
                    head_rms(NT * c + NT - 1)

            def take_states(c):
                for m in range(2):
                    act.wait_ge(s_proj, 2 * c + m + 1)
                    if c >= 2:
                        act.wait_ge(scored, GPC * (c - 1))
                    nc.scalar.activation(st[:, c % 2, m, 0:CW], ps[2 + m][0:2 * QB, 0:CW], ACT.Identity,
                                         bias=cols(env, name + ("_spb", "_spbx")[m])[0:2 * QB, :]).then_inc(s_taken, 1)
                act.wait_ge(s_taken, 2 * c + 1)
                if c >= 1:
                    act.wait_ge(s_norm, c)
                nc.scalar.activation(ssq[:], st[:, c % 2, 0, 0:CW], ACT.Square).then_inc(s_squared, 1)

            def take_norms(c):
                act.wait_ge(s_norm, c + 1)
                if c >= 1:
                    act.wait_ge(s_scaled, 2 * c)
                nc.scalar.activation(srs[:], ps[0][0:2 * QB, 0:CW], ACT.Ln, bias=tiny[0:2 * QB, 0:1]).then_inc(s_factor, 1)
                act.wait_ge(s_factor, 4 * c + 1)
                nc.scalar.activation(srs[:], srs[:], ACT.Exp, scale=0.5).then_inc(s_factor, 1)
                act.wait_ge(s_factor, 4 * c + 2)
                nc.scalar.activation(srs[:], srs[:], ACT.Ln, bias=tiny[0:2 * QB, 1:2]).then_inc(s_factor, 1)
                act.wait_ge(s_factor, 4 * c + 3)
                nc.scalar.activation(srs[:], srs[:], ACT.Exp, scale=-1.0).then_inc(s_factor, 1)

            def square_overlaps(g):
                act.wait_ge(scored, g + 1)
                if g >= 2:
                    act.wait_ge(fid_ready, g - 1)
                nc.scalar.activation(osq[:, g % 2].rearrange("p f e k -> p (f e k)"), ps[4][:, 2 * HN * N:2 * HN * N + 4 * N],
                                     ACT.Square, scale=HW ** 0.25).then_inc(ov_squared, 1)

            def head_rms(t):
                act.wait_ge(head_ms, t + 1)
                if t >= 2:
                    act.wait_ge(head_scaled, t - 1)
                nc.scalar.activation(rrs[:, t % 2], ps[0][0:HD, 0:CW], ACT.Ln, bias=env.rms_eps[0:HD, :]).then_inc(head_log, 1)
                act.wait_ge(head_log, t + 1)
                nc.scalar.activation(rrs[:, t % 2], rrs[:, t % 2], ACT.Exp, scale=-0.5).then_inc(head_rstd, 1)

            def take_values(g):
                for f in range(GI // 2):
                    n = g * FV + f
                    act.wait_ge(vt_ready, n + 1)
                    if g >= 2 and f == 0:
                        act.wait_ge(ctx_ready, g - 1)
                    nc.scalar.activation(vt[:, g % 2, 2 * f:2 * f + 2].rearrange("p i a f -> p (i a f)"),
                                         ps[5 + n % 2][0:HH * N, 0:4 * HD], ACT.Copy).then_inc(vt_evicted, 1)
                if quantum:
                    n = g * FV + FV - 1
                    act.wait_ge(vt_ready, n + 1)
                    if g >= 2:
                        act.wait_ge(proj[3], 2 * (g // GPC))
                    nc.scalar.activation(xt[:, g % 2].rearrange("p f a d -> p (f a d)"), ps[5 + n % 2][0:4 * N, 0:4 * HD],
                                         ACT.Copy).then_inc(vt_evicted, 1)

            def exponent(g):
                act.wait_ge(shifted, g + 1)
                nc.scalar.activation(p[:, g % 2], p[:, g % 2], ACT.Exp, scale=HW ** -0.5).then_inc(expd, 1)

            def take_context(g):
                c = g // GPC
                act.wait_ge(pt_ready, g + 1)
                if g >= 2:
                    act.wait_ge(ctx_ready, g - 1)
                nc.scalar.activation(pt[:, g % 2].rearrange("p a b -> p (a b)"), ps[7][0:HH * N, 0:512], ACT.Copy).then_inc(pt_evicted, 1)
                if quantum:
                    act.wait_ge(qt_ready, g + 1)
                    if g >= 2:
                        act.wait_ge(proj[3], 2 * c)
                    nc.scalar.activation(qt[:, g % 2, :, 0:QR], ps[0][0:4 * N, 0:256].rearrange("p (f q) -> p f q", f=2)[:, :, 0:QR],
                                         ACT.Copy).then_inc(qt_moved, 1)
                act.wait_ge(ctx_ready, g + 1)
                if c >= 2:
                    act.wait_ge(proj[3], 2 * (c - 1))
                for a in range(2):
                    o = (g % GPC) * GW
                    bias, scale = (gated_b[:, 0, a:a + 1], gate[0:HD, 1:2]) if quantum else (cols(env, pre + "_vb")[0:HD, a:a + 1], 1.0)
                    nc.scalar.activation(cx[:, c % 2, a, o:o + GW], ps[1][0:HD, a * GW:(a + 1) * GW], ACT.Identity,
                                         bias=bias, scale=scale).then_inc(ctx_evicted, 1)

            act.preload_act_table_set("natural_log_exp_and_others")
            if quantum:
                act.wait_ge(gate_in, 16)
                nc.scalar.activation(gate[:, 0:1], gate[:, 0:1], ACT.Exp, scale=-1.0).then_inc(gate_step, 1)
            act.wait_ge(pad_zero, 3 if quantum else 1)
            if quantum:
                act.wait_ge(gate_step, 5)
            take_qk(0)
            if quantum:
                take_states(0)
                take_norms(0)
            for c in range(NC):
                if c >= 2:
                    ln.square(act, c - 2)
                for g in (2 * c, 2 * c + 1):
                    if quantum:
                        square_overlaps(g)
                    take_values(g)
                    exponent(g)
                if c >= 2:
                    ln.rstd(act, c - 2)
                if c + 1 < NC:
                    take_qk(c + 1)
                take_context(2 * c)
                if quantum and c + 1 < NC:
                    take_states(c + 1)
                take_context(2 * c + 1)
                if quantum and c + 1 < NC:
                    take_norms(c + 1)
            ln.overlapped(ln.square, ln.rstd, act, NC - 2)

        @block.gpsimd
        def _(pool):
            pool.memset(q[:, :, :, CW:], 0.0).then_inc(pad_zero, 1)
            if quantum:
                pool.memset(st[:, :, :, CW:], 0.0).then_inc(pad_zero, 1)
                pool.memset(tiny[:, 0:1], 1e-19)
                pool.memset(tiny[:, 1:2], 1e-8).then_inc(pad_zero, 1)

            def spread_fidelities(g):
                pool.wait_ge(normed, g + 1)
                if g >= 2:
                    pool.wait_ge(qt_ready, g - 1)
                nc.gpsimd.tensor_tensor(px[:, g % 2], p[:, g % 2, :, None, HN * N:HP * N].broadcast_to([128, 2, 4, N]),
                                        env.image_mask[:, None, :, None].broadcast_to([128, 2, 4, N]), ALU.mult).then_inc(spread, 1)

            for c in range(NC):
                if quantum and c >= 1:
                    spread_fidelities(2 * c - 2)
                    spread_fidelities(2 * c - 1)
                for a in range(2 if c else 1):
                    pool.wait_ge(head_scaled if rms else qk_evicted, NT * c + 2 + a + 1)
                    if c >= 2:
                        pool.wait_ge(scored, GPC * (c - 1))
                    nc.gpsimd.tensor_tensor(kx[:, c % 2, a].rearrange("p i (h k) -> p i h k", h=HH),
                                            k[:, c % 2, a].rearrange("p (i k) -> p i k", k=N)[:, :, None, :].broadcast_to([HD, IC, HH, N]),
                                            env.head_mask[:, None, :, None].broadcast_to([HD, IC, HH, N]), ALU.mult).then_inc(k_spread, 1)
                if response is not None:
                    for part in ((0,), (1, 2), (3,), ())[c]:
                        response.on_pool(pool, part)
            if quantum:
                spread_fidelities(NG - 2)
                spread_fidelities(NG - 1)
                pool.wait_ge(spread, NG)

        @block.vector
        def _(dve):
            def head_scale(c):
                for t in range(NT * c, NT * c + NT):
                    j, m = (t % NT) // 2, t % 2
                    dst = (q if j == 0 else k)[:, c % 2, m, 0:CW]
                    dve.wait_ge(head_rstd, t + 1)
                    wcol = cols(env, name + ("_qn" if j == 0 else "_kn"))[0:HD, 0:1]
                    nc.vector.scalar_tensor_tensor(dst, dst, wcol, rrs[:, t % 2], ALU.mult, ALU.mult).then_inc(head_scaled, 1)

            def spread_first_keys():
                dve.wait_ge(head_scaled if rms else qk_evicted, NT)
                nc.vector.tensor_tensor(kx[:, 0, 1].rearrange("p i (h k) -> p i h k", h=HH),
                                        k[:, 0, 1, :].rearrange("p (i k) -> p i k", k=N)[:, :, None, :].broadcast_to([HD, IC, HH, N]),
                                        env.head_mask[:, None, :, None].broadcast_to([HD, IC, HH, N]), ALU.mult).then_inc(k_spread, 1)

            def spread_values(c):
                for a in range(2):
                    dve.wait_ge(proj[2], 2 * c + a + 1)
                    if c >= 2:
                        dve.wait_ge(vt_ready, FV * GPC * (c - 1))
                    nc.vector.tensor_tensor(vx[:, c % 2, a].rearrange("p i (h k) -> p i h k", h=HH),
                                            ps[2 + a][0:HD, 0:CW].rearrange("p (i k) -> p i k", k=N)[:, :, None, :].broadcast_to([HD, IC, HH, N]),
                                            env.head_mask[:, None, :, None].broadcast_to([HD, IC, HH, N]), ALU.mult).then_inc(v_spread, 1)

            def softmax(g):
                s = ps[4][:, 0:2 * HN * N].rearrange("p (f h k) -> p f h k", f=2, k=N)
                pg = p[:, g % 2].rearrange("p f (h k) -> p f h k", k=N)
                dve.wait_ge(scored, g + 1)
                if g >= 2:
                    dve.wait_ge(pt_ready, g - 1)
                if quantum:
                    dve.wait_ge(ov_squared, g + 1)
                    if g >= 2:
                        dve.wait_ge(spread, g - 1)
                    nc.vector.tensor_tensor(pg[:, :, HN], osq[:, g % 2, :, 0], osq[:, g % 2, :, 1], ALU.add).then_inc(fid_ready, 1)
                nc.vector.reduce_max(mx[:, g % 2, :, 0:HN], s, AX_X).then_inc(maxed, 1)
                if quantum:
                    dve.wait_ge(fid_ready, g + 1)
                    nc.vector.reduce_max(mx[:, g % 2, :, HN], pg[:, :, HN], AX_X).then_inc(maxed, 1)
                    dve.wait_ge(maxed, 2 * g + 2)
                    nc.vector.tensor_tensor(pg[:, :, HN], pg[:, :, HN], mx[:, g % 2, :, HN, None].broadcast_to([128, 2, N]), ALU.subtract)
                else:
                    dve.wait_ge(maxed, g + 1)
                nc.vector.tensor_tensor(pg[:, :, 0:HN], s, mx[:, g % 2, :, 0:HN, None].broadcast_to([128, 2, HN, N]), ALU.subtract)\
                    .then_inc(shifted, 1)
                dve.wait_ge(expd, g + 1)
                nc.vector.reduce_sum(sm[:, g % 2], pg, AX_X).then_inc(summed, 1)
                dve.wait_ge(summed, g + 1)
                nc.vector.reciprocal(sm[:, g % 2], sm[:, g % 2]).then_inc(inverted, 1)
                dve.wait_ge(inverted, g + 1)
                if quantum:
                    nc.vector.tensor_scalar(sm[:, g % 2, :, HN], sm[:, g % 2, :, HN], gate[:, 0:1], None, ALU.mult).then_inc(weighted, 1)
                    dve.wait_ge(weighted, g + 1)
                nc.vector.tensor_tensor(pg, pg, sm[:, g % 2, :, :, None].broadcast_to([128, 2, HP, N]), ALU.mult).then_inc(normed, 1)

            def scale_states(c):
                dve.wait_ge(s_factor, 4 * c + 4)
                nc.vector.tensor_tensor(st[:, c % 2, 0, 0:CW], st[:, c % 2, 0, 0:CW], srs[:], ALU.mult).then_inc(s_scaled, 1)
                dve.wait_ge(s_taken, 2 * c + 2)
                nc.vector.scalar_tensor_tensor(st[:, c % 2, 1, 0:CW], st[:, c % 2, 1, 0:CW], env.conj[:, 0:1], srs[:], ALU.mult, ALU.mult)\
                    .then_inc(s_scaled, 1)

            if quantum:
                dve.wait_ge(gate_step, 1)
                nc.vector.tensor_scalar(gate[:, 0:1], gate[:, 0:1], 1.0, None, ALU.add).then_inc(gate_step, 1)
                dve.wait_ge(gate_step, 2)
                nc.vector.reciprocal(gate[:, 0:1], gate[:, 0:1]).then_inc(gate_step, 1)
                dve.wait_ge(gate_step, 3)
                nc.vector.tensor_scalar(gate[:, 1:2], gate[:, 0:1], -1.0, 1.0, ALU.mult, ALU.add).then_inc(gate_step, 1)
                dve.wait_ge(gate_step, 4)
                nc.vector.tensor_scalar(gated_b[:, 1], cols(env, name + "_ob")[0:HD, :], gate[0:HD, 1:2], None, ALU.mult)
                nc.vector.tensor_scalar(gated_b[:, 0], cols(env, name + "_vb")[0:HD, :], gate[0:HD, 1:2], None, ALU.mult).then_inc(gate_step, 1)
                dve.wait_ge(gate_step, 5)
            if rms:
                head_scale(0)
            if rms:
                spread_values(0)
                spread_first_keys()
            else:
                spread_first_keys()
                spread_values(0)
            if quantum:
                scale_states(0)
            for c in range(NC):
                if response is not None and c == NC - 1:
                    response.sum_up(dve)
                if c >= 2:
                    ln.centre(dve, c - 2)
                softmax(2 * c)
                softmax(2 * c + 1)
                if c >= 2:
                    ln.scale(dve, c - 2)
                if c + 1 < NC:
                    if rms:
                        head_scale(c + 1)
                    spread_values(c + 1)
                    if quantum:
                        scale_states(c + 1)
                if c == NC - 1:
                    ln.centre(dve, NC - 2)
                ob = gated_b[:, 1] if quantum else cols(env, name + "_ob")[0:HD, :]
                for m in range(2):
                    dve.wait_ge(proj[3], 2 * c + m + 1)
                    hc = chunk(env.h, c)[:, m]
                    nc.vector.scalar_tensor_tensor(hc, ps[2 + m][0:HD, 0:CW], ob[:, m:m + 1], hc,
                                                   ALU.add, ALU.add).then_inc(added, 1)
            ln.overlapped(ln.centre, ln.scale, dve, NC - 2, begun=True)


class Rms:

    def __init__(self, env, name, src, dst, w, bank, ready_src=None, per_chunk=1):
        self.bank = env.ps[bank]
        self.env, self.src, self.dst, self.w, self.ready_src, self.per_chunk = env, src, dst, w, ready_src, per_chunk
        self.squared = env.sem(name + "_squared")
        self.mean_ready = env.sem(name + "_mean_ready")
        self.log_mean = env.sem(name + "_log_mean")
        self.factor_ready = env.sem(name + "_factor_ready")
        self.ready = env.sem(name + "_ready")

    def square(self, act, c):
        nc, env = self.env.nc, self.env
        if self.ready_src is not None:
            act.wait_ge(self.ready_src, self.per_chunk * (c + 1))
        if c >= 2:
            act.wait_ge(self.mean_ready, c - 1)
        nc.scalar.activation(self.sq[:, c % 2], chunk(self.src, c), ACT.Square).then_inc(self.squared, 1)

    def mean(self, pe, c):
        nc, env = self.env.nc, self.env
        pe.wait_ge(self.squared, c + 1)
        if c > 0:
            pe.wait_ge(self.log_mean, c)
        for a in range(2):
            last = nc.tensor.matmul(self.bank[0:HD, 0:CW], env.mean_w, self.sq[:, c % 2, a], start=a == 0, stop=a == 1)
        last.then_inc(self.mean_ready, 1)

    def factor(self, act, c):
        nc, env = self.env.nc, self.env
        act.wait_ge(self.mean_ready, c + 1)
        if c >= 2:
            act.wait_ge(self.ready, 2 * (c - 1))
        nc.scalar.activation(self.rs[:, c % 2], self.bank[0:HD, 0:CW], ACT.Ln, bias=env.rms_eps[0:HD, :]).then_inc(self.log_mean, 1)
        act.wait_ge(self.log_mean, c + 1)
        nc.scalar.activation(self.rs[:, c % 2], self.rs[:, c % 2], ACT.Exp, scale=-0.5).then_inc(self.factor_ready, 1)

    def scale(self, dve, c):
        nc = self.env.nc
        dve.wait_ge(self.factor_ready, c + 1)
        for a in range(2):
            nc.vector.scalar_tensor_tensor(chunk(self.dst, c)[:, a], chunk(self.src, c)[:, a], self.w[0:HD, a:a + 1],
                                           self.rs[:, c % 2], ALU.mult, ALU.mult).then_inc(self.ready, 1)


def stage_wide_attention(env, name, weights, ahead=()):
    nc = env.nc
    x, x2, ps = env.x, env.x2, env.ps
    JQ = QH // 2
    R = JQ * N
    KC = KVH * N
    KS = KVH * SLOT
    TQK, TV = JQ + KVH, KVH
    NT = TQK + TV
    with ExitStack() as ctx:
        def sb(n, shape, dt=F32):
            return ctx.enter_context(nc.sbuf_tensor(name + "_" + n, shape, dt))

        def sem(n):
            return env.sem(name + "_" + n)

        wq, wk, wv, wo, w_in = weights.wq, weights.wk, weights.wv, weights.wo, weights.w_in
        raw = sb("raw", [128, 2, CW])
        swp = sb("swapped", [128, 2, CW])
        q = sb("q", [128, 2, IC, R])
        k = sb("k", [128, 2, KVH, CW])
        vs = sb("vs", [WD, 2, IC, KVH, SLOT])
        vt = sb("vt", [KS, 2, GI, WD])
        s = sb("s", [R, 2, GI, KC])
        mx = sb("mx", [R, 2, GI])
        sm = sb("sm", [R, 2, GI])
        p = sb("p", [R, 2, 2, GI, KVH, SLOT])
        pt = sb("pt", [KS, 2, 2, GI, R])
        cx = sb("cx", [128, 2, JQ, CW])
        rsq1, rrs1, rsq2, rrs2 = sb("rsq1", [HD, 2, 2, CW]), sb("rrs1", [HD, 2, CW]), sb("rsq2", [HD, 2, 2, CW]), sb("rrs2", [HD, 2, CW])
        added = sem("added")
        n1 = Rms(env, name + "_n1", x, x2, cols(env, "n1w"), 0)
        n2 = Rms(env, name + "_n2", x, x2, cols(env, "n2w"), 1, added, 2)
        n1.sq, n1.rs, n2.sq, n2.rs = rsq1, rrs1, rsq2, rrs2
        zeroed, projected, taken, swapped, sin_done, cos_done, turned = (
            sem(n) for n in ("zeroed", "projected", "taken", "swapped", "sin_done", "cos_done", "turned"))
        scored, masked, maxed, shifted, expd, summed, inverted, normed = (
            sem(n) for n in ("scored", "masked", "maxed", "shifted", "expd", "summed", "inverted", "normed"))
        filled, moved, out_ready, h_added = (sem(n) for n in ("filled", "moved", "out_ready", "h_added"))
        FG = 1 + 6
        FC = GPC * FG

        def fill_of(g, j):
            base = FC * (g // GPC)
            return base + g % GPC if j == 0 else base + GPC + (FG - 1) * (g % GPC) + j - 1

        block = ctx.enter_context(nc.Block())

        @block.sync
        def _(sp):
            for w in ahead:
                w.load(sp)

        @block.tensor
        def _(pe):
            def project(c):
                pe.wait_ge(n1.ready, 2 * (c + 1))
                for t in range(NT):
                    if t >= 2:
                        pe.wait_ge(taken, NT * c + t - 1)
                    elif c == 1:
                        pe.wait_ge(taken, NT - 1 + t)
                    elif c >= 2:
                        pe.wait_ge(added, 2 * (c - 2) + t + 1)
                    w, rows = (wq, 128) if t < JQ else (wk, 128) if t < TQK else (wv, WD)
                    j = t if t < JQ else t - JQ if t < TQK else t - TQK
                    for a in range(2):
                        last = nc.tensor.matmul(ps[2 + t % 2][0:rows, 0:CW], w[:, a, j * rows:(j + 1) * rows],
                                                chunk(x2, c)[:, a], start=a == 0, stop=a == 1)
                    last.then_inc(projected, 1)

            def scores(g):
                c = g // GPC
                pe.wait_ge(turned, TQK * (c + 1))
                if g >= 1:
                    pe.wait_ge(masked, g)
                for i in range(GI):
                    i16 = (g % GPC) * GI + i
                    for e in range(2):
                        last = nc.tensor.matmul(ps[4 + e][0:R, i * KC:(i + 1) * KC], q[e * WD:(e + 1) * WD, c % 2, i16, :],
                                                k[e * WD:(e + 1) * WD, c % 2, :, i16 * N:(i16 + 1) * N], start=True, stop=True)
                last.then_inc(scored, 1)

            def bank(g, j):
                n = fill_of(g, j)
                if n >= 2:
                    pe.wait_ge(moved, n - 1)
                return ps[6 + n % 2]

            def turn_values(g):
                c = g // GPC
                pe.wait_ge(taken, NT * (c + 1))
                to = bank(g, 0)
                for i in range(GI):
                    last = nc.tensor.transpose(to[0:KS, i * WD:(i + 1) * WD],
                                               vs[:, c % 2, (g % GPC) * GI + i].rearrange("p g k -> p (g k)"), env.ident[0:WD, 0:WD])
                last.then_inc(filled, 1)

            def weigh(g):
                pe.wait_ge(normed, g + 1)
                for j in range(4):
                    to, e = bank(g, 1 + j), j % 2
                    for i in range(4):
                        last = nc.tensor.transpose(to[0:KS, i * R:(i + 1) * R],
                                                   p[:, g % 2, e, 4 * (j // 2) + i].rearrange("p g k -> p (g k)"), env.ident[0:R, 0:R])
                    last.then_inc(filled, 1)
                for j in range(2):
                    pe.wait_ge(moved, fill_of(g, 2 + 2 * j) + 1)
                    to = bank(g, 5 + j)
                    for i in range(4):
                        for e in range(2):
                            last = nc.tensor.matmul(to[e * WD:(e + 1) * WD, i * R:(i + 1) * R], vt[:, g % 2, 4 * j + i, :],
                                                    pt[:, g % 2, e, 4 * j + i, :], start=True, stop=True)
                    last.then_inc(filled, 1)

            def project_out(c):
                pe.wait_ge(moved, fill_of(GPC * c + GPC - 1, 6) + 1)
                for m in range(2):
                    pe.wait_ge(taken, NT * min(c + 1, NC - 1) + NT - 1 + m)
                    if c == NC - 1:
                        pe.wait_ge(added, 2 * (c - 1) + m + 1)
                    for j in range(JQ):
                        last = nc.tensor.matmul(ps[2 + m][0:HD, 0:CW], wo[:, j, m * HD:(m + 1) * HD], cx[:, c % 2, j],
                                                start=j == 0, stop=j == JQ - 1)
                    last.then_inc(out_ready, 1)

            for c in range(2):
                n1.mean(pe, c)
            pe.wait_ge(w_in, 64)
            project(0)
            for c in range(NC):
                for g in (2 * c, 2 * c + 1):
                    scores(g)
                    turn_values(g)
                if c >= 1:
                    n2.mean(pe, c - 1)
                if c + 2 < NC:
                    n1.mean(pe, c + 2)
                if c + 1 < NC:
                    project(c + 1)
                for g in (2 * c, 2 * c + 1):
                    weigh(g)
                project_out(c)
            n2.mean(pe, NC - 1)

        @block.scalar
        def _(act):
            def take(c):
                for t in range(NT):
                    n = NT * c + t
                    act.wait_ge(projected, n + 1)
                    if t < TQK:
                        r = TQK * c + t
                        if r >= 2:
                            act.wait_ge(turned, r - 1)
                        nc.scalar.activation(raw[:, r % 2], ps[2 + t % 2][:, 0:CW], ACT.Copy).then_inc(taken, 1)
                    else:
                        if c >= 2 and t == TQK:
                            act.wait_ge(filled, fill_of(GPC * (c - 2) + GPC - 1, 0) + 1)
                        nc.scalar.activation(vs[:, c % 2, :, t - TQK, 0:N],
                                             ps[2 + t % 2][0:WD, 0:CW].rearrange("p (i k) -> p i k", k=N), ACT.Copy).then_inc(taken, 1)

            def take_values(g):
                n = fill_of(g, 0)
                act.wait_ge(filled, n + 1)
                if g >= 2:
                    act.wait_ge(filled, fill_of(g - 2, 6) + 1)
                nc.scalar.activation(vt[:, g % 2].rearrange("p i d -> p (i d)"), ps[6 + n % 2][0:KS, 0:GI * WD], ACT.Copy).then_inc(moved, 1)

            def exponent(g):
                act.wait_ge(shifted, g + 1)
                nc.scalar.activation(s[:], s[:], ACT.Exp, scale=WD ** -0.5).then_inc(expd, 1)

            def move_weighed(g):
                c = g // GPC
                for j in range(4):
                    n = fill_of(g, 1 + j)
                    act.wait_ge(filled, n + 1)
                    nc.scalar.activation(pt[:, g % 2, j % 2, 4 * (j // 2):4 * (j // 2) + 4].rearrange("p i r -> p (i r)"),
                                         ps[6 + n % 2][0:KS, 0:4 * R], ACT.Copy).then_inc(moved, 1)
                for j in range(2):
                    n = fill_of(g, 5 + j)
                    act.wait_ge(filled, n + 1)
                    if c >= 2:
                        act.wait_ge(out_ready, 2 * (c - 1))
                    o = ((g % GPC) * GI + 4 * j) * N
                    nc.scalar.activation(cx[:, c % 2, :, o:o + 4 * N].rearrange("p j (i n) -> p i j n", n=N),
                                         ps[6 + n % 2][:, 0:4 * R].rearrange("p (i j n) -> p i j n", i=4, j=JQ), ACT.Copy).then_inc(moved, 1)

            act.preload_act_table_set("natural_log_exp_and_others")
            for c in range(2):
                n1.square(act, c)
                n1.factor(act, c)
            act.wait_ge(zeroed, 2)
            take(0)
            for c in range(NC):
                if c >= 1:
                    n2.square(act, c - 1)
                for g in (2 * c, 2 * c + 1):
                    take_values(g)
                    exponent(g)
                if c >= 1:
                    n2.factor(act, c - 1)
                if c + 2 < NC:
                    n1.square(act, c + 2)
                    n1.factor(act, c + 2)
                if c + 1 < NC:
                    take(c + 1)
                for g in (2 * c, 2 * c + 1):
                    move_weighed(g)
            n2.square(act, NC - 1)
            n2.factor(act, NC - 1)

        @block.gpsimd
        def _(pool):
            pool.memset(vs[:, :, :, :, N:], 0.0).then_inc(zeroed, 1)
            pool.memset(p[:], 0.0).then_inc(zeroed, 1)

            def table(tab):
                return tab[:, None, :].broadcast_to([128, IC, N])

            def by_token(ap):
                return ap.rearrange("p (i n) -> p i n", n=N)

            def turn(c):
                for t in range(TQK):
                    r = TQK * c + t
                    pool.wait_ge(swapped, r + 1)
                    nc.gpsimd.tensor_tensor(by_token(raw[:, r % 2]), by_token(raw[:, r % 2]), table(env.cos), ALU.mult).then_inc(cos_done, 1)
                    nc.gpsimd.tensor_tensor(by_token(swp[:, r % 2]), by_token(swp[:, r % 2]), table(env.sin), ALU.mult).then_inc(sin_done, 1)

            turn(0)
            for c in range(NC):
                if c + 1 < NC:
                    turn(c + 1)
                pool.wait_ge(added, 2 * c + 2)
                nc.gpsimd.tensor_tensor(chunk(env.h, c), chunk(env.h, c), chunk(x, c), ALU.add).then_inc(h_added, 1)
            pool.wait_ge(h_added, NC)

        @block.vector
        def _(dve):
            def swap(r):
                dve.wait_ge(taken, NT * (r // TQK) + r % TQK + 1)
                nc.vector.stream_shuffle(swp[:, r % 2], raw[:, r % 2], [i ^ 1 for i in range(32)]).then_inc(swapped, 1)

            def turn(c):
                for t in range(TQK + 1):
                    r = TQK * c + t
                    if t < TQK:
                        swap(r)
                    if t == 0:
                        continue
                    r, u = r - 1, t - 1
                    dve.wait_ge(cos_done, r + 1)
                    dve.wait_ge(sin_done, r + 1)
                    if c >= 2 and u == 0:
                        dve.wait_ge(scored, GPC * (c - 1))
                    if u < JQ:
                        nc.vector.tensor_tensor(q[:, c % 2, :, u * N:(u + 1) * N], raw[:, r % 2].rearrange("p (i n) -> p i n", n=N),
                                                swp[:, r % 2].rearrange("p (i n) -> p i n", n=N), ALU.add).then_inc(turned, 1)
                    else:
                        nc.vector.tensor_tensor(k[:, c % 2, u - JQ], raw[:, r % 2], swp[:, r % 2], ALU.add).then_inc(turned, 1)

            def softmax(g):
                sc = env.psall[0:R, 4:6, 0:GI * KC].rearrange("p e (i k) -> p e i k", k=KC)
                if g >= 1:
                    dve.wait_ge(normed, g)
                dve.wait_ge(scored, g + 1)
                nc.vector.tensor_tensor(s[:], sc, env.causal[:, None, None, :].broadcast_to([R, 2, GI, KC]), ALU.add).then_inc(masked, 1)
                dve.wait_ge(masked, g + 1)
                nc.vector.reduce_max(mx[:], s[:], AX_X).then_inc(maxed, 1)
                dve.wait_ge(maxed, g + 1)
                nc.vector.tensor_tensor(s[:], s[:], mx[:, :, :, None].broadcast_to([R, 2, GI, KC]), ALU.subtract).then_inc(shifted, 1)
                dve.wait_ge(expd, g + 1)
                nc.vector.reduce_sum(sm[:], s[:], AX_X).then_inc(summed, 1)
                dve.wait_ge(summed, g + 1)
                nc.vector.reciprocal(sm[:], sm[:]).then_inc(inverted, 1)
                dve.wait_ge(inverted, g + 1)
                if g >= 2:
                    dve.wait_ge(filled, fill_of(g - 2, 4) + 1)
                for e in range(2):
                    last = nc.vector.tensor_tensor(p[:, g % 2, e, :, :, 0:N], s[:, e].rearrange("p i (g k) -> p i g k", k=N),
                                                   sm[:, e, :, None, None].broadcast_to([R, GI, KVH, N]), ALU.mult)
                last.then_inc(normed, 1)

            for c in range(2):
                n1.scale(dve, c)
            turn(0)
            dve.wait_ge(zeroed, 2)
            for c in range(NC):
                softmax(2 * c)
                softmax(2 * c + 1)
                if c >= 1:
                    n2.scale(dve, c - 1)
                if c + 2 < NC:
                    n1.scale(dve, c + 2)
                if c + 1 < NC:
                    turn(c + 1)
                for m in range(2):
                    dve.wait_ge(out_ready, 2 * c + m + 1)
                    xc = chunk(x, c)[:, m]
                    nc.vector.tensor_tensor(xc, ps[2 + m][0:HD, 0:CW], xc, ALU.add).then_inc(added, 1)
            n2.scale(dve, NC - 1)
            dve.wait_ge(n2.ready, 2 * NC)


def stage_routed_ffn(env, name, router, experts, src, E, K, TL, norm_out, load_experts=False):
    nc = env.nc
    ps = env.ps
    top2 = K == 2
    RT = 128
    NR = -(-T // RT)
    LAST = T - (NR - 1) * RT
    FN = EF if top2 else FF
    NH = FN // 128
    BW = 384
    HF = FN // BW
    KU = [HD if top2 else HD + 1, HD]
    assert TL * RT >= T * K + E * (RT - 1) - RT + 1 and TL % 2 == 0
    with ExitStack() as ctx:
        def sb(n, shape, dt=F32):
            return ctx.enter_context(nc.sbuf_tensor(name + "_" + n, shape, dt))

        def sem(n):
            return env.sem(name + "_" + n)

        wr, wu, wd = router.wr, experts.wu, experts.wd
        chosen = sb("chosen", [RT, NR, E])
        lg, pr, t0, t1, t2, t3 = (sb(n, [RT, NR, E]) for n in ("lg", "pr", "t0", "t1", "t2", "t3"))
        before = sb("before", [RT, NR + 1, E])
        r0, r1 = sb("r0", [RT, NR]), sb("r1", [RT, NR])
        cnt = sb("cnt", [RT, 4, E])
        tile_cmp, tile_sum, tile_expert = sb("tile_cmp", [1, TL, E]), sb("tile_sum", [1, TL]), sb("tile_expert", [1, TL], I32)
        slot = sb("slot", [RT, K, NR], U32)
        share = sb("share", [RT, 2, NR])
        xtok = sb("xtok", [RT, NR, D])
        xs = sb("xs", [RT, 2, D])
        xf = sb("xf", [KU[0], 2, 2, RT])
        hid = sb("hid", [RT, 2, FN])
        hidt = sb("hidt", [128, 2, NH, RT])
        ys = sb("ys", [RT, 2, D])
        yb = [xtok] + [sb("yb", [RT, NR, D]) for _ in range(K - 1)]
        if top2:
            top8 = sb("top8", [RT, NR, 8])
            gs = sb("gs", [RT, 2, BW])
        else:
            bg, b2 = router.bg, router.b2
        x_slots, y_slots = env.x_slots, env.y_slots
        small_in, w_in = router.small_in, experts.w_in
        routed, exp_in, exp_out, chain = (sem(n) for n in ("routed", "logits_shifted", "logits_exp", "router_steps"))
        zeroed, prefix_ready, rank_ready, slots_ready, tiles_ready = (
            sem(n) for n in ("zeroed", "prefix_ready", "rank_ready", "slots_ready", "tiles_ready"))
        xt_ready, xt_moved, scattered = sem("xt_ready"), sem("xt_moved"), sem("scattered")
        w_ready = sem("w_ready")
        x_in, y_out = [sem("x0_in"), sem("x1_in")], [sem("y0_out"), sem("y1_out")]
        x_turned, x_moved, up_ready, acted, hid_ready, h_turned, h_moved, down_ready, y_moved = (
            sem(n) for n in ("x_turned", "x_moved", "up_ready", "acted", "hid_ready", "hid_turned", "hid_moved", "down_ready", "y_moved"))
        y_back = [sem(f"y{t}_back") for t in range(NR)]
        summed, weighed, out_turned, added = sem("share_summed"), sem("weighed"), sem("out_turned"), sem("added")
        ones_ready = sem("ones_ready")
        ln = Norm(env, name + "_ln", env.x, added, [-(-(c + 1) * CW // RT) for c in range(NC)])
        norm_at = {}
        for c in range(NC if norm_out else 0):
            norm_at.setdefault(ln.counts[c], []).append((0, c))
            norm_at.setdefault(ln.counts[c] + (1 if c == NC - 1 else 2), []).append((1, c))
        assert ln.counts[-1] == NR
        block = ctx.enter_context(nc.Block())

        def rows(t):
            return LAST if t == NR - 1 else RT

        def wait(eng, s, value):
            if not isinstance(value, int) or value > 0:
                eng.wait_ge(s, value)

        def tiles_loop(eng, body):
            for i in range(2):
                body(i, i, 2)
            with eng.Fori(1, TL // 2 - 2) as it:
                for u in range(2):
                    body(it * 2 + u, u, 2)
            for i in range(TL - 4, TL):
                body(i, i % 2, min(2, TL - 1 - i))

        def i_half(i, p):
            return i // 2 if isinstance(i, int) else (i - p) // 2

        @block.sync
        def _(sp):
            if load_experts:
                experts.load(sp)
            for e in range(E):
                sp.wait_ge(w_in[e], 32)
                sp.sem_inc(w_ready, 1)

        @block.tensor
        def _(pe):
            pe.wait_ge(small_in, 16 if top2 else 48)
            for t in range(NR):
                for a in range(2):
                    last = nc.tensor.matmul(ps[7][0:rows(t), t * E:(t + 1) * E], src[:, a, t * RT:t * RT + rows(t)], wr[:, a], start=a == 0, stop=a == 1)
            last.then_inc(routed, 1)
            for t in range(NR):
                for a in range(2):
                    o = (t % 2) * D + a * HD
                    last = nc.tensor.transpose(ps[1 + t // 2][0:rows(t), o:o + HD], src[:, a, t * RT:t * RT + rows(t)], env.ident[0:HD, 0:HD])
                if t % 2 or t == NR - 1:
                    last.then_inc(xt_ready, 1)
            pe.wait_ge(prefix_ready, 1)
            nc.tensor.matmul(ps[6][:, 0:NR * E], env.earlier, chosen[:].rearrange("p t e -> p (t e)"), start=True, stop=False)
            nc.tensor.matmul(ps[6][:, 0:NR * E], env.ones, before[:, 0:NR].rearrange("p t e -> p (t e)"), start=False, stop=True)
            nc.tensor.matmul(ps[6][:, NR * E:(NR + 1) * E], env.ones, before[:, NR], start=True, stop=True).then_inc(rank_ready, 1)

            def turn_x(i, p):
                pe.wait_ge(x_in[p], i_half(i, p) * 16 + 16)
                wait(pe, x_moved, i)
                for a in range(2):
                    last = nc.tensor.transpose(ps[0][0:HD, a * RT:(a + 1) * RT], xs[:, p, a * HD:(a + 1) * HD], env.ident)
                last.then_inc(x_turned, 1)

            def expert(i):
                return pe.value_load(tile_expert[0:1, bass.ds(i, 1)], min_val=0, max_val=E - 1)

            def up(i, p):
                e = expert(i)
                pe.wait_ge(w_ready, e + 1)
                pe.wait_ge(x_moved, i + 1)
                for u in range(2):
                    if top2:
                        wait(pe, hid_ready if u else acted, i - 1)
                    else:
                        wait(pe, acted, i * 2 + (u - 3))
                    for a in range(2):
                        last = nc.tensor.matmul(ps[2 + 2 * p + u][:, 0:BW], xf[0:KU[a], p, a],
                                                wu[0:KU[a], bass.ds(e, 1), a, u * BW:(u + 1) * BW].rearrange("p e f -> p (e f)"),
                                                start=a == 0, stop=a == 1)
                    last.then_inc(up_ready, 1)

            def turn_hidden(i, p):
                for f in range(HF):
                    n = i * HF + f
                    if top2:
                        pe.wait_ge(hid_ready, i + 1)
                    else:
                        pe.wait_ge(acted, n + 1)
                    wait(pe, h_moved, n - 1)
                    for j in range(3):
                        last = nc.tensor.transpose(ps[(1, 6)[(p * HF + f) % 2]][:, j * RT:(j + 1) * RT],
                                                   hid[:, p, f * BW + j * 128:f * BW + (j + 1) * 128], env.ident)
                    last.then_inc(h_turned, 1)

            def down(i, p):
                e = expert(i)
                pe.wait_ge(h_moved, i * HF + HF)
                wait(pe, y_moved, i)
                for j in range(NH):
                    last = nc.tensor.matmul(ps[7][:, 0:D], hidt[:, p, j], wd[:, bass.ds(e, 1), j, :].rearrange("p e f -> p (e f)"),
                                            start=j == 0, stop=j == NH - 1)
                last.then_inc(down_ready, 1)

            def norm_steps(t):
                for part, c in sorted(norm_at.get(t, [])):
                    (ln.mean, ln.var)[part](pe, c)

            pe.wait_ge(tiles_ready, 1)
            pe.wait_ge(xt_moved, -(-NR // 2))
            pe.wait_ge(slots_ready, 1)
            if not top2:
                pe.wait_ge(ones_ready, 1)
            turn_x(0, 0)
            turn_x(1, 1)
            up(0, 0)

            def body(i, p, ahead):
                if ahead >= 1:
                    up(i + 1, 1 - p)
                turn_hidden(i, p)
                if ahead >= 2:
                    turn_x(i + 2, p)
                if not isinstance(i, int) or i >= 1:
                    down(i - 1, 1 - p)

            tiles_loop(pe, body)
            down(TL - 1, 1)
            for t in range(NR):
                if top2:
                    pe.wait_ge(weighed, t + 1)
                else:
                    pe.wait_ge(y_back[t], 16)
                if t >= 4:
                    pe.wait_ge(added, t - 3)
                for a in range(2):
                    last = nc.tensor.transpose(ps[2 + t % 4][0:HD, a * RT:a * RT + rows(t)], yb[0][0:rows(t), t, a * HD:(a + 1) * HD],
                                               env.ident[0:rows(t), 0:rows(t)])
                last.then_inc(out_turned, 1)
                norm_steps(t)
            norm_steps(NR)
            norm_steps(NR + 1)

        @block.scalar
        def _(act):
            for b in range(-(-NR // 2)):
                act.wait_ge(xt_ready, b + 1)
                n = rows(2 * b)
                w = min(2, NR - 2 * b)
                nc.scalar.activation(xtok[0:n, 2 * b:2 * b + w].rearrange("p t d -> p (t d)"), ps[1 + b][0:n, 0:w * D], ACT.Copy).then_inc(xt_moved, 1)
            if top2:
                act.wait_ge(exp_in, 1)
                nc.scalar.activation(pr[:], pr[:], ACT.Exp).then_inc(exp_out, 1)

            def load_x(i, p):
                act.dma_start(xs[:, p], x_slots[bass.ds(i * RT, RT), :]).then_inc(x_in[p], 16)

            def move_x(i, p, more):
                act.wait_ge(x_turned, i + 1)
                wait(act, up_ready, i * 2 - 2)
                nc.scalar.activation(xf[0:HD, p].rearrange("p a r -> p (a r)"), ps[0][0:HD, 0:2 * RT], ACT.Copy).then_inc(x_moved, 1)
                if more:
                    load_x(i + 2, p)

            def nonlinear(i, p):
                for u in range(1 if top2 else 2):
                    act.wait_ge(up_ready, i * 2 + (u + 1))
                    if top2:
                        wait(act, hid_ready, i - 1)
                        nc.scalar.activation(gs[:, p], ps[2 + 2 * p][:, 0:BW], ACT.Silu).then_inc(acted, 1)
                    else:
                        wait(act, h_turned, i * HF - HF)
                        nc.scalar.activation(hid[:, p, u * BW:(u + 1) * BW], ps[2 + 2 * p + u][:, 0:BW], ACT.Gelu).then_inc(acted, 1)

            def move_hidden(i, p):
                for f in range(HF):
                    act.wait_ge(h_turned, i * HF + (f + 1))
                    wait(act, down_ready, i - 1)
                    nc.scalar.activation(hidt[:, p, 3 * f:3 * f + 3].rearrange("p j r -> p (j r)"),
                                         ps[(1, 6)[(p * HF + f) % 2]][:, 0:BW], ACT.Copy).then_inc(h_moved, 1)

            act.wait_ge(scattered, 16 * K * NR)
            load_x(0, 0)
            load_x(1, 1)
            move_x(0, 0, True)
            move_x(1, 1, True)
            nonlinear(0, 0)

            def body(i, p, ahead):
                if ahead >= 1:
                    nonlinear(i + 1, 1 - p)
                move_hidden(i, p)
                if ahead >= 2:
                    move_x(i + 2, p, not isinstance(i, int) or i + 4 < TL)

            tiles_loop(act, body)
            if norm_out:
                act.preload_act_table_set("natural_log_exp_and_others")
                ln.overlapped(ln.square, ln.rstd, act, 0)

        @block.gpsimd
        def _(pool):
            pool.memset(lg[:], 0.0).then_inc(zeroed, 1)
            if not top2:
                pool.wait_ge(zeroed, 1)
                pool.memset(xf[HD:HD + 1], 1.0).then_inc(ones_ready, 1)
                pool.wait_ge(ones_ready, 1)
            pool.memset(before[:, 0], 0.0).then_inc(zeroed, 1)
            pool.wait_ge(env.slots_zero, 16)
            pool.wait_ge(slots_ready, 1)
            pool.wait_ge(xt_moved, -(-NR // 2))
            for t in range(NR):
                for k in range(K):
                    nc.gpsimd.indirect_dma_start(x_slots, bass.IndirectOffsetOnAxis(ap=slot[0:rows(t), k, t:t + 1], axis=0),
                                                 xtok[0:rows(t), t], None).then_inc(scattered, 16)

            def body(i, p, ahead):
                pool.wait_ge(y_moved, i + 1)
                pool.dma_start(y_slots[bass.ds(i * RT, RT), :], ys[:, p]).then_inc(y_out[p], 16)

            tiles_loop(pool, body)
            for p in range(2):
                pool.wait_ge(y_out[p], 16 * (TL // 2))
            for t in range(NR):
                for k in range(K):
                    nc.gpsimd.indirect_dma_start(yb[k][0:rows(t), t], None, y_slots,
                                                 bass.IndirectOffsetOnAxis(ap=slot[0:rows(t), k, t:t + 1], axis=0)).then_inc(y_back[t], 16)

        @block.vector
        def _(dve):
            V = nc.vector
            steps = [0]

            def link(ins):
                steps[0] += 1
                ins.then_inc(chain, 1)
                dve.wait_ge(chain, steps[0])

            def over(v):
                return v[:, :, None].broadcast_to([RT, NR, E])

            def running(a, free, width):
                sh = 1
                while sh < width:
                    b = free[0]
                    V.tensor_copy(b[..., 0:sh], a[..., 0:sh])
                    link(V.tensor_tensor(b[..., sh:], a[..., sh:], a[..., 0:width - sh], ALU.add))
                    a, free = b, free[1:] + free[:1]
                    sh *= 2
                return a

            dve.wait_ge(zeroed, 2)
            dve.wait_ge(routed, 1)
            for lo, hi, n in ((0, NR - 1, RT), (NR - 1, NR, LAST)):
                logits = ps[7][0:n, lo * E:hi * E].rearrange("p (t e) -> p t e", e=E)
                if top2:
                    last = V.tensor_copy(lg[0:n, lo:hi], logits)
                else:
                    last = V.tensor_tensor(lg[0:n, lo:hi], logits, bg[0:n, None, :].broadcast_to([n, hi - lo, E]), ALU.add)
            link(last)
            link(V.reduce_max(r0[:], lg[:], AX_X))
            valid = env.valid[:, :, None].broadcast_to([RT, NR, E])
            if top2:
                V.tensor_tensor(pr[:], lg[:], over(r0), ALU.subtract).then_inc(exp_in, 1)
                dve.wait_ge(exp_out, 1)
                link(V.reduce_sum(r0[:], pr[:], AX_X))
                link(V.reciprocal(r0[:], r0[:]))
                link(V.tensor_tensor(pr[:], pr[:], over(r0), ALU.mult))
                for t in range(NR):
                    last = V.max(top8[:, t], pr[:, t])
                link(last)
                second = top8[:, :, 1:2].broadcast_to([RT, NR, E])
                V.tensor_tensor(t0[:], pr[:], second, ALU.is_gt)
                link(V.tensor_tensor(t1[:], pr[:], second, ALU.is_equal))
                link(V.reduce_sum(r1[:], t0[:], AX_X))
                link(V.tensor_scalar(r1[:], r1[:], -1.0, 2.0, ALU.mult, ALU.add))
                a = running(t1, [t2, t3], E)
                link(V.tensor_tensor(a[:], a[:], over(r1), ALU.is_le))
                link(V.tensor_tensor(a[:], a[:], t1[:], ALU.mult))
                link(V.tensor_tensor(a[:], a[:], t0[:], ALU.add))
            else:
                link(V.tensor_tensor(t1[:], lg[:], over(r0), ALU.is_equal))
                a = running(t1, [t2, t3], E)
                link(V.tensor_scalar(a[:], a[:], 1.0, None, ALU.is_le))
                link(V.tensor_tensor(a[:], a[:], t1[:], ALU.mult))
            link(V.tensor_tensor(chosen[:], a[:], valid, ALU.mult))
            for t in range(NR):
                link(V.tensor_tensor(before[:, t + 1], before[:, t], chosen[:, t], ALU.add))
            dve.sem_inc(prefix_ready, 1)
            if top2:
                a = running(chosen, [t1, t2], E)
                free = t1 if a is t2 else t2
                link(V.tensor_scalar(a[:], a[:], 1.0, None, ALU.is_equal))
                link(V.tensor_tensor(free[:], a[:], chosen[:], ALU.mult))
                link(V.tensor_tensor(a[:], chosen[:], free[:], ALU.subtract))
                choice = [free, a]
                for k in range(2):
                    link(V.tensor_tensor(t3[:], pr[:], choice[k][:], ALU.mult))
                    link(V.reduce_sum(share[:, k], t3[:], AX_X))
            else:
                choice = [chosen]
            dve.wait_ge(rank_ready, 1)
            link(V.tensor_scalar(cnt[:, 0], ps[6][:, NR * E:(NR + 1) * E], 1.0 / RT, (RT - 1.0) / RT - 0.5 + 0.5 / RT, ALU.mult, ALU.add))
            link(V.tensor_scalar(cnt[:, 0], cnt[:, 0], ROUND, ROUND, ALU.add, ALU.subtract))
            upto = running(cnt[:, 0], [cnt[:, 1], cnt[:, 2]], E)
            link(V.tensor_tensor(cnt[:, 3], upto, cnt[:, 0], ALU.subtract))
            link(V.tensor_scalar(cnt[:, 3], cnt[:, 3], float(RT), None, ALU.mult))
            link(V.tensor_tensor(lg[:], ps[6][:, 0:NR * E].rearrange("p (t e) -> p t e", e=E), cnt[:, 3:4].broadcast_to([RT, NR, E]), ALU.add))
            for k in range(K):
                link(V.tensor_tensor(t3[:], lg[:], choice[k][:], ALU.mult))
                link(V.reduce_sum(r0[:], t3[:], AX_X))
                link(V.tensor_copy(slot[:, k], r0[:]))
            dve.sem_inc(slots_ready, 1)
            link(V.tensor_tensor(tile_cmp[:], upto[0:1, None, :].broadcast_to([1, TL, E]),
                                 env.tile_no[:, 0:TL, None].broadcast_to([1, TL, E]), ALU.is_le))
            link(V.reduce_sum(tile_sum[:], tile_cmp[:], AX_X))
            link(V.tensor_scalar(tile_expert[:], tile_sum[:], E - 1.0, None, ALU.min))
            dve.sem_inc(tiles_ready, 1)
            if top2:
                V.tensor_tensor(r0[:], share[:, 0], share[:, 1], ALU.add).then_inc(summed, 1)
                dve.wait_ge(summed, 1)
                link(V.tensor_scalar(r0[:], r0[:], 1e-30, None, ALU.max))
                V.reciprocal(r0[:], r0[:]).then_inc(summed, 1)
                dve.wait_ge(summed, 2)
                V.tensor_tensor(share[:], share[:], r0[:, None, :].broadcast_to([RT, 2, NR]), ALU.mult).then_inc(summed, 1)
                dve.wait_ge(summed, 3)

            def gate(i, p):
                dve.wait_ge(acted, i + 1)
                dve.wait_ge(up_ready, i * 2 + 2)
                wait(dve, h_turned, i - 1)
                V.tensor_tensor(hid[:, p], ps[3 + 2 * p][:, 0:BW], gs[:, p], ALU.mult).then_inc(hid_ready, 1)

            def move_y(i, p):
                dve.wait_ge(down_ready, i + 1)
                wait(dve, y_out[p], i_half(i, p) * 16)
                if top2:
                    V.tensor_copy(ys[:, p], ps[7][:, 0:D]).then_inc(y_moved, 1)
                else:
                    e = dve.value_load(tile_expert[0:1, bass.ds(i, 1)], min_val=0, max_val=E - 1)
                    V.tensor_tensor(ys[:, p], ps[7][:, 0:D], b2[:, bass.ds(e, 1), :].rearrange("p e f -> p (e f)"), ALU.add).then_inc(y_moved, 1)

            if top2:
                gate(0, 0)

            def body(i, p, ahead):
                if top2 and ahead >= 1:
                    gate(i + 1, 1 - p)
                if not isinstance(i, int) or i >= 1:
                    move_y(i - 1, 1 - p)

            tiles_loop(dve, body)
            move_y(TL - 1, 1)

            def add(t):
                dve.wait_ge(out_turned, t + 1)
                hc = env.h[:, :, t * RT:t * RT + rows(t)]
                V.tensor_tensor(hc, hc, ps[2 + t % 4][0:HD, 0:2 * RT].rearrange("p (a r) -> p a r", a=2)[:, :, 0:rows(t)], ALU.add)\
                    .then_inc(added, 1)

            def norm_steps(t):
                for part, c in sorted(norm_at.get(t, [])):
                    (ln.centre, ln.scale)[part](dve, c)

            for t in range(NR):
                if top2:
                    n = rows(t)
                    dve.wait_ge(y_back[t], 32)
                    V.tensor_scalar(yb[0][0:n, t], yb[0][0:n, t], share[0:n, 0, t:t + 1], None, ALU.mult).then_inc(summed, 1)
                    dve.wait_ge(summed, 4 + t)
                    V.scalar_tensor_tensor(yb[0][0:n, t], yb[1][0:n, t], share[0:n, 1, t:t + 1], yb[0][0:n, t], ALU.mult, ALU.add).then_inc(weighed, 1)
                if t >= 1:
                    add(t - 1)
                norm_steps(t - 1)
            add(NR - 1)
            norm_steps(NR - 1)
            norm_steps(NR)
            norm_steps(NR + 1)
            dve.wait_ge(added, NR)


def stage_convolution(env, name, quant, ahead=()):
    nc = env.nc
    x, ps = env.x, env.ps
    x4 = x[:, :, :].rearrange("p a (b n) -> p a b n", n=N)
    J1 = 13
    LATE = (N - J1) * IC
    NF = FF // 128
    with ExitStack() as ctx:
        def sb(n, shape, dt=F32):
            return ctx.enter_context(nc.sbuf_tensor(name + "_" + n, shape, dt))

        def sem(n):
            return env.sem(name + "_" + n)

        work = [(0, j) for j in range(N)] + [(1, j) for j in range(J1, N)]
        diag = sb("diag", [HD, len(work), HD])
        w1, w2, q1, q2, a1r, a2r = quant.w1, quant.w2, quant.q1, quant.q2, quant.a1r, quant.a2r
        mean1, mean2, inv1, inv2, s1, s2 = quant.mean1, quant.mean2, quant.inv1, quant.inv2, quant.s1, quant.s2
        diag_ready, conv_ready, tapped, final = sem("diag_ready"), sem("conv_ready"), sem("tapped"), sem("final")
        divided = sem("divided")
        inverted, inverse_out, mean_step, quant_step = sem("steps_inverted"), sem("inverse_out"), sem("mean_step"), sem("quant_step")
        ln = Norm(env, name + "_ln", x, final, [2 * (c + 1) for c in range(NC)])
        block = ctx.enter_context(nc.Block())

        @block.sync
        def _(sp):
            quant.load(sp)
            sp.wait_ge(inverted, 1)
            sp.dma_start(quant.inverse_dram.rearrange("(p f) -> p f", f=HD), quant.rows[:]).then_inc(inverse_out, 16)
            sp.wait_ge(inverse_out, 16)
            sp.dma_start(a1r[:], quant.inverse_dram[None, 0:FF].broadcast_to([HD, FF])).then_inc(quant.inverse_in, 16)
            sp.dma_start(a2r[:], quant.inverse_dram[None, FF:FF + D].broadcast_to([128, D])).then_inc(quant.inverse_in, 16)
            for w in ahead:
                w.load(sp)

        @block.tensor
        def _(pe):
            def convolve(c):
                for n, (a, j) in enumerate(work):
                    pe.wait_ge(diag_ready, n + 1)
                    to = ps[4 + c][0:HD, 0:CW] if a == 0 else ps[4 + c][0:HD, CW:CW + LATE]
                    to = to.rearrange("p (b n) -> p b n", b=IC)[:, :, j - (0 if a == 0 else J1):]
                    last = nc.tensor.matmul(to, diag[:, n], x4[:, a, c * IC:(c + 1) * IC, 0:N - j], start=j == (0 if a == 0 else J1), stop=j == N - 1)
                last.then_inc(conv_ready, 1)

            convolve(0)
            convolve(1)
            convolve(2)
            ln.mean(pe, 0)
            convolve(3)
            ln.mean(pe, 1)
            ln.var(pe, 0)
            ln.overlapped(ln.mean, ln.var, pe, 1, begun=True)

        @block.scalar
        def _(act):
            for n, (a, j) in enumerate(work):
                nc.scalar.activation(diag[:, n], env.ident[0:HD, 0:HD], ACT.Copy, scale=env.taps[:, a, j:j + 1]).then_inc(diag_ready, 1)
            ln.overlapped(ln.square, ln.rstd, act, 0)

        @block.gpsimd
        def _(pool):
            pool.wait_ge(quant.w_in, 32)
            pool.wait_ge(quant.inverse_in, 32)
            for w, r, shape in ((w1, a1r, [HD, 2, FF]), (w2, a2r, [128, NF, D])):
                nc.gpsimd.tensor_tensor(w[:], w[:], r[:, None, :].broadcast_to(shape), ALU.mult).then_inc(divided, 1)
            pool.wait_ge(divided, 2)

        @block.vector
        def _(dve):
            V = nc.vector
            dve.wait_ge(quant.rows_in, 32)
            V.reciprocal(quant.rows[:], quant.rows[:]).then_inc(inverted, 1)
            n = 0
            for j in range(J1):
                for b in range(2):
                    im = slice(b * B // 2, (b + 1) * B // 2)
                    if n >= 2:
                        dve.wait_ge(tapped, n - 1)
                    V.scalar_tensor_tensor(env.h4[:, 1, im, j:N], x4[:, 1, im, 0:N - j], env.taps[:, 1, j:j + 1], env.h4[:, 1, im, j:N],
                                           ALU.mult, ALU.add).then_inc(tapped, 1)
                    n += 1
            dve.wait_ge(tapped, n)
            def add(c):
                dve.wait_ge(conv_ready, c + 1)
                hc = chunk(env.h, c)[:, 0]
                V.tensor_tensor(hc, hc, ps[4 + c][0:HD, 0:CW], ALU.add).then_inc(final, 1)
                hl = env.h4[:, 1, c * IC:(c + 1) * IC, J1:]
                V.tensor_tensor(hl, hl, ps[4 + c][0:HD, CW:CW + LATE].rearrange("p (b n) -> p b n", b=IC), ALU.add).then_inc(final, 1)

            add(0)
            add(1)
            steps = [0]

            def link(ins):
                steps[0] += 1
                ins.then_inc(mean_step, 1)
                dve.wait_ge(mean_step, steps[0])

            dve.wait_ge(quant.m_in, 32)
            V.reduce_sum(mean2[:], quant.m2r[:], AX_X)
            link(V.reduce_sum(mean1[:], quant.m1r[:], AX_X))
            V.tensor_scalar(mean2[:], mean2[:], 1.0 / FF, None, ALU.mult)
            link(V.tensor_scalar(mean1[:], mean1[:], 1.0 / D, None, ALU.mult))
            V.reciprocal(inv1[:], mean1[:])
            V.reciprocal(inv2[:], mean2[:])
            V.tensor_scalar(s1[:], cols(env, "f1_aw1"), mean1[:, 0:1], None, ALU.mult)
            link(V.tensor_scalar(s2[:], cols(env, "f1_aw2")[0:HD, :], mean2[0:HD, 0:1], None, ALU.mult))

            ln.centre(dve, 0)
            add(2)
            for i, (w, q) in enumerate(((w1, q1), (w2, q2))):
                dve.wait_ge(divided, i + 1)
                V.tensor_scalar(w[:], w[:], QHI, QLO, ALU.min, ALU.max).then_inc(quant_step, 1)
                dve.wait_ge(quant_step, 2 * i + 1)
                V.tensor_scalar(w[:], w[:], ROUND, None, ALU.add).then_inc(quant_step, 1)
                dve.wait_ge(quant_step, 2 * i + 2)
                V.tensor_scalar(q[:], w[:], ROUND, None, ALU.subtract)

            ln.centre(dve, 1)
            ln.scale(dve, 0)
            add(3)
            ln.overlapped(ln.centre, ln.scale, dve, 1, begun=True)


def stage_quantised_ffn(env, name, weights):
    nc = env.nc
    x, ps = env.x, env.ps
    NF = FF // 128
    with ExitStack() as ctx:
        def sb(n, shape, dt=F32):
            return ctx.enter_context(nc.sbuf_tensor(name + "_" + n, shape, dt))

        def sem(n):
            return env.sem(name + "_" + n)

        q1, q2, inv1, inv2, s1, s2 = weights.q1, weights.q2, weights.inv1, weights.inv2, weights.s1, weights.s2
        xt = sb("xt", [HD, 2, CW])
        xq = sb("xq", [HD, 2, 2, CW], BF16)
        g = sb("g", [128, 2, NF, CW])
        gq = sb("gq", [128, 2, NF, CW], BF16)
        y = sb("y", [HD, 2, 2, CW])
        qstep, gstep = sem("x_quant_step"), sem("g_quant_step")
        up_ready, gelu_ready, down_ready, y_ready, added = (sem(n) for n in ("up_ready", "gelu_ready", "down_ready", "y_ready", "added"))
        ln = Norm(env, name + "_ln", x, added, [c + 1 for c in range(NC)], var_banks=(0, 0, 1, 1))
        block = ctx.enter_context(nc.Block())

        @block.tensor
        def _(pe):

            def up(c):
                pe.wait_ge(qstep, 3 * (c + 1))
                for f in range(NF):
                    n = c * NF + f
                    if n >= 3:
                        pe.wait_ge(gelu_ready, n - 2)
                    for a in range(2):
                        last = nc.tensor.matmul(ps[1 + n % 3][:, 0:CW], q1[:, a, f * 128:(f + 1) * 128], xq[:, c % 2, a], start=a == 0, stop=a == 1)
                    last.then_inc(up_ready, 1)

            def down(c):
                pe.wait_ge(gstep, 4 * (c + 1))
                if c >= 2:
                    pe.wait_ge(y_ready, 2 * (c - 1))
                for m in range(2):
                    for f in range(NF):
                        last = nc.tensor.matmul(ps[4 + 2 * (c % 2) + m][0:HD, 0:CW], q2[:, f, m * HD:(m + 1) * HD], gq[:, c % 2, f],
                                                start=f == 0, stop=f == NF - 1)
                    last.then_inc(down_ready, 1)

            up(0)
            for c in range(NC):
                if c + 1 < NC:
                    up(c + 1)
                if c >= 2:
                    ln.mean(pe, c - 2)
                down(c)
                if c >= 2:
                    ln.var(pe, c - 2)
            ln.overlapped(ln.mean, ln.var, pe, NC - 2)

        @block.scalar
        def _(act):
            def gelu(c):
                for f in range(NF):
                    n = c * NF + f
                    act.wait_ge(up_ready, n + 1)
                    if c >= 2 and f == 0:
                        act.wait_ge(gstep, 4 * (c - 1))
                    nc.scalar.activation(g[:, c % 2, f], ps[1 + n % 3][:, 0:CW], ACT.Gelu, bias=cols(env, name + "_b1")[:, f:f + 1],
                                         scale=s1[:, f:f + 1]).then_inc(gelu_ready, 1)

            def out(c):
                for m in range(2):
                    act.wait_ge(down_ready, 2 * c + m + 1)
                    if c >= 2:
                        act.wait_ge(added, c - 1)
                    nc.scalar.activation(y[:, c % 2, m], ps[4 + 2 * (c % 2) + m][0:HD, 0:CW], ACT.Identity,
                                         bias=cols(env, name + "_b2")[0:HD, m:m + 1], scale=s2[:, m:m + 1]).then_inc(y_ready, 1)

            gelu(0)
            for c in range(NC):
                if c + 1 < NC:
                    gelu(c + 1)
                if c == 2:
                    act.preload_act_table_set("natural_log_exp_and_others")
                out(c)
                if c >= 2:
                    ln.square(act, c - 2)
                    ln.rstd(act, c - 2)
            ln.overlapped(ln.square, ln.rstd, act, NC - 2)

        @block.gpsimd
        def _(pool):
            for c in range(NC):
                pool.wait_ge(y_ready, 2 * (c + 1))
                nc.gpsimd.tensor_tensor(chunk(env.h, c), chunk(env.h, c), y[:, c % 2], ALU.add).then_inc(added, 1)
            pool.wait_ge(added, NC)

        @block.vector
        def _(dve):
            V = nc.vector
            def quant_x(c):
                if c >= 1:
                    dve.wait_ge(qstep, 3 * c)
                V.tensor_scalar(xt[:], chunk(x, c), inv1[0:HD, 0:1], QHI, ALU.mult, ALU.min).then_inc(qstep, 1)
                dve.wait_ge(qstep, 3 * c + 1)
                V.tensor_scalar(xt[:], xt[:], QLO, ROUND, ALU.max, ALU.add).then_inc(qstep, 1)
                dve.wait_ge(qstep, 3 * c + 2)
                if c >= 2:
                    dve.wait_ge(up_ready, NF * (c - 1))
                V.tensor_scalar(xq[:, c % 2], xt[:], ROUND, None, ALU.subtract).then_inc(qstep, 1)

            def quant_g(c):
                gc = g[:, c % 2]
                dve.wait_ge(gelu_ready, NF * (c + 1))
                V.tensor_scalar(gc, gc, 10.0, -10.0, ALU.min, ALU.max).then_inc(gstep, 1)
                dve.wait_ge(gstep, 4 * c + 1)
                V.tensor_scalar(gc, gc, inv2[:, 0:1], QHI, ALU.mult, ALU.min).then_inc(gstep, 1)
                dve.wait_ge(gstep, 4 * c + 2)
                V.tensor_scalar(gc, gc, QLO, ROUND, ALU.max, ALU.add).then_inc(gstep, 1)
                dve.wait_ge(gstep, 4 * c + 3)
                if c >= 2:
                    dve.wait_ge(down_ready, 2 * (c - 1))
                V.tensor_scalar(gq[:, c % 2], gc, ROUND, None, ALU.subtract).then_inc(gstep, 1)

            quant_x(0)
            quant_x(1)
            for c in range(NC):
                quant_g(c)
                if c + 2 < NC:
                    quant_x(c + 2)
                if c >= 2:
                    ln.centre(dve, c - 2)
                    ln.scale(dve, c - 2)
            ln.overlapped(ln.centre, ln.scale, dve, NC - 2)


def stage_class_ffn(env, name, weights, ahead=()):
    nc = env.nc
    x, ps = env.x, env.ps
    x4 = x[:, :, :].rearrange("p a (b n) -> p a b n", n=N)
    NF = FF // 128
    NPT = N - NCLS
    PI = 32
    NPS = B // PI
    PW = PI * NPT
    XW = NCLS * B
    with ExitStack() as ctx:
        def sb(n, shape, dt=F32):
            return ctx.enter_context(nc.sbuf_tensor(name + "_" + n, shape, dt))

        def sem(n):
            return env.sem(name + "_" + n)

        w1, w2, gw, gw_in, w_in = weights.w1, weights.w2, weights.gw, weights.gw_in, weights.w_in
        gwx = sb("gwx", [HD, 2, NCLS, 2, HD])
        z1 = sb("z1", [HD, NCLS, B])
        gate = sb("gate", [HD, 2, NCLS, B])
        hp = sb("hp", [128, 2, NF, PW])
        hx = sb("hx", [128, 2, NF, NCLS, B])
        wy = sb("wy", [HD, 2, 2, NCLS, B])
        gw_spread, z_ready, z1_moved, gates_ready = (sem(n) for n in ("gw_spread", "z_ready", "z1_moved", "gates_ready"))
        up_ready, gelu_ready, down_ready, patch_added = (sem(n) for n in ("up_ready", "gelu_ready", "down_ready", "patch_added"))
        pair_ready, gated, pair_added = sem("pair_ready"), sem("gated"), sem("pair_added")
        ln = Norm(env, name + "_ln", x, pair_added, [4] * NC)
        block = ctx.enter_context(nc.Block())
        ups = [(0, slice(2 * a, 2 * a + 2)) for a in range(3)] + [(1, slice(a, NCLS, 2)) for a in range(2)]
        downs = [(1, slice(2 * e, 2 * e + 2)) for e in range(3)] + [(0, slice(e, NCLS, 2)) for e in range(2)]
        NU = NPS * NF

        @block.sync
        def _(sp):
            for w in ahead:
                w.load(sp)

        @block.tensor
        def _(pe):
            def up(s):
                for f in range(NF):
                    n = s * NF + f
                    if n >= 2:
                        pe.wait_ge(gelu_ready, n - 1)
                    for a in range(2):
                        last = nc.tensor.matmul(ps[2 + n % 2][:, 0:PW], w1[:, 0, a, f * 128:(f + 1) * 128],
                                                x4[:, a, s * PI:(s + 1) * PI, NCLS:N], start=a == 0, stop=a == 1)
                    last.then_inc(up_ready, 1)

            def down(s):
                pe.wait_ge(gelu_ready, NF * (s + 1))
                for m in range(2):
                    for f in range(NF):
                        last = nc.tensor.matmul(ps[4 + 2 * s + m][0:HD, 0:PW], w2[:, 0, f, m * HD:(m + 1) * HD], hp[:, s, f],
                                                start=f == 0, stop=f == NF - 1)
                    last.then_inc(down_ready, 1)

            pe.wait_ge(w_in[0], 32)
            up(0)
            up(1)
            down(0)
            pe.wait_ge(gw_spread, 1)
            for j in range(2):
                for i in range(NCLS):
                    for a in range(2):
                        last = nc.tensor.matmul(ps[j][0:HD, i * B:(i + 1) * B], gwx[:, a, i, j], x4[:, a, :, i], start=a == 0, stop=a == 1)
            last.then_inc(z_ready, 1)
            down(1)
            n = NU
            for e, (member, pos) in enumerate(ups):
                pe.wait_ge(w_in[1 + e], 32)
                w = B * len(range(NCLS)[pos])
                for f in range(NF):
                    pe.wait_ge(gelu_ready, n - 1)
                    for a in range(2):
                        last = nc.tensor.matmul(ps[2 + n % 2][:, 0:w], w1[:, 1 + e, a, f * 128:(f + 1) * 128],
                                                x4[:, a, :, pos].rearrange("p b n -> p n b"), start=a == 0, stop=a == 1)
                    last.then_inc(up_ready, 1)
                    n += 1
            pe.wait_ge(gelu_ready, n)
            pe.wait_ge(patch_added, 2 * NPS)
            for member in (1, 0):
                for m in range(2):
                    for e, (mem, pos) in enumerate(downs):
                        if mem != member:
                            continue
                        to = ps[4 + 2 * member + m][0:HD, 0:XW].rearrange("p (n b) -> p n b", b=B)[:, pos]
                        for f in range(NF):
                            last = nc.tensor.matmul(to, w2[:, 1 + e, f, m * HD:(m + 1) * HD], hx[:, member, f, pos],
                                                    start=f == 0, stop=f == NF - 1)
                    last.then_inc(pair_ready, 1)
            ln.overlapped(ln.mean, ln.var, pe, 0)

        @block.scalar
        def _(act):
            act.wait_ge(gw_in, 16)
            nc.scalar.activation(gwx[:].rearrange("p a n g d -> p (a n g) d"),
                                 gw[:].rearrange("p a n g -> p (a n g)")[:, :, None].broadcast_to([HD, 4 * NCLS, HD]), ACT.Copy).then_inc(gw_spread, 1)
            for n in range(NU):
                act.wait_ge(up_ready, n + 1)
                s, f = n // NF, n % NF
                nc.scalar.activation(hp[:, s, f], ps[2 + n % 2][:, 0:PW], ACT.Gelu, bias=cols(env, name + "_pb1")[:, f:f + 1]).then_inc(gelu_ready, 1)
            act.wait_ge(z_ready, 1)
            nc.scalar.activation(z1[:].rearrange("p n b -> p (n b)"), ps[1][0:HD, 0:XW], ACT.Copy).then_inc(z1_moved, 1)
            n = NU
            for e, (member, pos) in enumerate(ups):
                w = B * len(range(NCLS)[pos])
                for f in range(NF):
                    act.wait_ge(up_ready, n + 1)
                    nc.scalar.activation(hx[:, member, f, pos], ps[2 + n % 2][:, 0:w].rearrange("p (n b) -> p n b", b=B), ACT.Gelu,
                                         bias=cols(env, f"{name}_eb1{e}")[:, f:f + 1]).then_inc(gelu_ready, 1)
                    n += 1
            act.preload_act_table_set("natural_log_exp_and_others")
            ln.overlapped(ln.square, ln.rstd, act, 0)

        @block.vector
        def _(dve):
            V = nc.vector
            for s in range(NPS):
                for m in range(2):
                    dve.wait_ge(down_ready, 2 * s + m + 1)
                    hc = env.h4[:, m, s * PI:(s + 1) * PI, NCLS:N]
                    V.scalar_tensor_tensor(hc, ps[4 + 2 * s + m][0:HD, 0:PW].rearrange("p (b n) -> p b n", n=NPT),
                                           cols(env, name + "_pb2")[0:HD, m:m + 1], hc, ALU.add, ALU.add).then_inc(patch_added, 1)
                if s == 0:
                    dve.wait_ge(z1_moved, 1)
                    z0 = ps[0][0:HD, 0:XW].rearrange("p (n b) -> p n b", b=B)
                    V.tensor_tensor(gate[:, 0], z0, z1[:], ALU.is_gt).then_inc(gates_ready, 1)
                    V.tensor_tensor(gate[:, 1], z0, z1[:], ALU.is_lt).then_inc(gates_ready, 1)
            dve.wait_ge(gates_ready, 2)
            ng = 0
            for k, member in enumerate((1, 0)):
                for m in range(2):
                    dve.wait_ge(pair_ready, 2 * k + m + 1)
                    for e, (mem, pos) in enumerate(downs):
                        if mem == member:
                            src = ps[4 + 2 * member + m][0:HD, 0:XW].rearrange("p (n b) -> p n b", b=B)[:, pos]
                            V.scalar_tensor_tensor(wy[:, member, m, pos], src, cols(env, f"{name}_eb2{e}")[0:HD, m:m + 1],
                                                   gate[:, member, pos], ALU.add, ALU.mult).then_inc(gated, 1)
                            ng += 1
                    hc = env.h4[:, m, :, 0:NCLS].rearrange("p b n -> p n b")
                    dve.wait_ge(gated, ng)
                    if k == 1:
                        dve.wait_ge(pair_added, m + 1)
                    V.tensor_tensor(hc, hc, wy[:, member, m], ALU.add).then_inc(pair_added, 1)
            dve.wait_ge(pair_added, 4)
            ln.overlapped(ln.centre, ln.scale, dve, 0)


ROUND = 1.5 * 2.0 ** 23
QLO, QHI = -8.0, 7.0
PI_DOWN = 3.1415925
SN = 64
NCLS = 6


def halves(v):
    return np.ascontiguousarray(np.moveaxis(np.asarray(v).reshape(2, HD, *np.shape(v)[1:]), 0, 1))


def tiles(v):
    return np.ascontiguousarray(np.asarray(v).reshape(-1, 128).T)


COLS = {}


def pack_columns(parts):
    out, at = [], 0
    for name, v in parts:
        v = np.asarray(v)
        n = v.shape[1]
        col = np.zeros((128, n), np.float32)
        col[:v.shape[0]] = v
        COLS[name] = (at, n)
        at += n
        out.append(col)
    return np.concatenate(out, 1)


def constants():
    f = np.arange(HD)
    mean_w = np.zeros((128, HD), np.float32)
    mean_w[:HD] = 1.0 / D
    head_mask = np.zeros((128, HH), np.float32)
    head_mask[:HD] = (f[:, None] // HW == np.arange(HH)[None])
    head_mean = np.zeros((128, HD), np.float32)
    head_mean[:HD] = (f[:, None] // HW == f[None] // HW) / HW
    ident = np.eye(128, dtype=np.float32)
    d = np.arange(WD)
    inv = (1.0 / np.float32(THETA) ** (np.arange(0, WD, 2, dtype=np.float32) / np.float32(WD))).astype(np.float32)
    angle = (inv[d // 2][:, None] * np.arange(N, dtype=np.float32)[None]).astype(np.float32)
    cos = np.tile(np.cos(angle), (2, 1)).astype(np.float32)
    sin = np.tile(np.sin(angle) * np.where(d % 2, 1, -1)[:, None], (2, 1)).astype(np.float32)
    causal = np.full((128, KVH * N), MASKED, np.float32)
    r = np.arange(QH // 2 * N)
    kc = np.arange(KVH * N)
    seen = ((r[:, None] // N) // (QH // KVH // 2) == kc[None] // N) & (kc[None] % N <= r[:, None] % N)
    causal[:len(r)][seen] = 0.0
    ones = np.ones((128, 128), np.float32)
    earlier = np.triu(np.ones((128, 128), np.float32), 1)
    valid = np.ones((128, -(-T // 128)), np.float32)
    valid[T % 128 or 128:, -1] = 0
    tile_no = np.tile(np.arange(MOE_TILES, dtype=np.float32), (128, 1))
    image_mask = (np.arange(128)[:, None] // SLOT == np.arange(4)[None]).astype(np.float32)
    conj = np.where(np.arange(128) < QB, 1, -1).astype(np.float32)[:, None]
    return [("earlier", earlier), ("valid", valid), ("tile_no", tile_no), ("ones", ones), ("image_mask", image_mask), ("conj", conj), ("cos", cos), ("sin", sin), ("causal", causal),
            ("mean_w", mean_w), ("head_mask", head_mask), ("head_mean", head_mean), ("ident", ident)]


def build(nc, d, out, con_at, con_n):
    ctx = ExitStack()
    with ctx:
        env = Env(nc, ctx)
        env.h = env.sb("h", [HD, 2, T])
        env.h4 = env.h[:, :, :].rearrange("p a (b n) -> p a b n", n=N)
        env.x = env.sb("x", [HD, 2, T])
        env.x2 = env.sb("x2", [HD, 2, T])
        env.taps = env.sb("taps", [HD, 2, N])
        env.sq = env.sb("ln_sq", [HD, 2, 2, CW])
        env.rs = env.sb("ln_rs", [HD, 2, CW])
        env.ln_eps = env.sb("ln_eps", [128, 1])
        env.rms_eps = env.sb("rms_eps", [128, 1])
        env.vec = env.sb("vec", [128, d["vec"].shape[1]])
        env.vec_dram = d["vec"]
        env.vec_in = env.keep_sem("vec_in")
        env.con = env.sb("con", [128, con_n])
        env.con_dram = d["con"]
        env.con_in = env.keep_sem("con_in")

        def con(name, rows):
            a, n = con_at[name]
            return env.con[0:rows, a:a + n]
        env.mean_w, env.head_mask, env.head_mean, env.ident = con("mean_w", HD), con("head_mask", HD), con("head_mean", HD), con("ident", 128)
        env.ones, env.image_mask, env.conj = con("ones", 128), con("image_mask", 128), con("conj", 2 * QB)
        env.earlier, env.valid, env.tile_no = con("earlier", 128), con("valid", 128), con("tile_no", 1)
        env.x_slots = nc.dram_tensor("x_slots", (MOE_TILES * 128, D), F32).ap()
        env.y_slots = nc.dram_tensor("y_slots", (MOE_TILES * 128, D), F32).ap()
        env.slots_zero = env.keep_sem("slots_zero")
        env.cos, env.sin, env.causal = con("cos", 128), con("sin", 128), con("causal", QH // 2 * N)
        env.psall = ctx.enter_context(nc.psum_tensor("banks", [128, 8, 512], F32))
        env.ps = [env.psall[:, i, :] for i in range(8)]

        def of(name):
            return {n[len(name) + 1:]: ap for n, ap in d.items() if n.startswith(name + "_")}

        moe_router = RouterWeights(env, ctx, "moe_router", of("moe"))
        with ExitStack() as region:
            a0, g0 = NarrowWeights(env, region, "a0", of("a0")), WideWeights(env, region, "g0", of("g0"))
            response = Response(env, region, of("s1"))
            stage_tokens(env, d["patches"], d["tok_w"], d["tok_pos"], response, ahead=[a0, g0, moe_router])
            env.end_stage()
            stage_narrow_attention(env, "a0", a0, rms=True, response=response)
            env.end_stage()
            stage_wide_attention(env, "g0", g0)
            env.end_stage()
        with ExitStack() as region:
            experts = ExpertWeights(env, region, "moe", of("moe"))
            stage_routed_ffn(env, "moe", moe_router, experts, env.x2, NE, 2, MOE_TILES, norm_out=True, load_experts=True)
            env.end_stage()
        with ExitStack() as region:
            a2, a3 = NarrowWeights(env, region, "a2", of("a2")), NarrowWeights(env, region, "a3", of("a3"))
            with ExitStack() as inner:
                f1 = QuantisedWeights(env, inner, "f1", of("f1"))
                stage_convolution(env, "s1", f1, ahead=[a2])
                env.end_stage()
                stage_quantised_ffn(env, "f1", f1)
                env.end_stage()
            with ExitStack() as inner:
                f2 = ClassWeights(env, inner, "f2", of("f2"))
                stage_narrow_attention(env, "a2", a2, ahead=[f2])
                env.end_stage()
                stage_class_ffn(env, "f2", f2, ahead=[a3])
                env.end_stage()
            with ExitStack() as inner:
                f3_router = RouterWeights(env, inner, "f3_router", of("f3"))
                f3 = ExpertWeights(env, inner, "f3", of("f3"))
                stage_narrow_attention(env, "a3", a3, quantum=True, ahead=[f3_router, f3])
                env.end_stage()
                stage_routed_ffn(env, "f3", f3_router, f3, env.x, NX, 1, TOP1_TILES, norm_out=False)
                env.end_stage()

        stored = env.sem("out_stored")
        with nc.Block() as block:
            @block.sync
            def _(sp):
                sp.dma_start(out, env.h[:]).then_inc(stored, 16)
                sp.wait_ge(stored, 16)


def prepare(inp):
    g = {k: np.asarray(v) for k, v in inp.items()}
    x = g["x"].reshape(NC, IC, 4, 16, 4, 16, 3)
    px = x.transpose(3, 5, 6, 0, 1, 2, 4).reshape(KP, 128, NC, IC * NP)
    a = {"patches": np.ascontiguousarray(px.transpose(2, 1, 0, 3)),
         "tok_w": np.ascontiguousarray(g["L0_tok_W"].reshape(KP, 128, D).transpose(1, 0, 2)),
         "tok_pos": halves(g["L0_tok_pos_emb"].T)}
    a["a0_wqkv"] = halves(g["L0_attn_qkv_w"].T)
    a["a0_wo"] = halves(g["L0_attn_proj_w"].T)
    w = g["L0_ffn_w_qkv"]
    a["g0_wq"] = halves(w[:, 0:QH * WD])
    wk = w[:, QH * WD:(QH + KVH) * WD].reshape(D, KVH, 1, WD)
    a["g0_wk"] = halves(np.broadcast_to(wk, (D, KVH, 2, WD)).reshape(D, KVH * 2 * WD))
    a["g0_wv"] = halves(w[:, (QH + KVH) * WD:])
    a["g0_wo"] = np.ascontiguousarray(g["L0_ffn_w_out"].reshape(QH // 2, 128, D).transpose(1, 0, 2))
    a["moe_wr"] = halves(g["L0_ffn_w_router"])
    a["moe_up"] = np.ascontiguousarray(g["L0_ffn_w_gate_up"].reshape(NE, 2, HD, 2 * EF).transpose(0, 2, 1, 3))
    a["moe_down"] = g["L0_ffn_w_down"]
    b = g["L0_attn_qkv_b"]
    a["s1_prm"] = np.ascontiguousarray(np.stack([halves(g["L1_attn_" + n]) for n in ("A_real", "A_imag", "B_mat", "C_mat")], 1))
    a["f1_w1"] = halves(g["L1_ffn_w1"].T)
    a["f1_w2"] = np.ascontiguousarray(g["L1_ffn_w2"].T.reshape(FF // 128, 128, D).transpose(1, 0, 2))
    for n, src in (("aw1", "alpha_w1"), ("aw2", "alpha_w2"), ("aa1", "alpha_a1"), ("aa2", "alpha_a2")):
        a["f1_" + n] = g["L1_ffn_" + src][None]
    a["a2_wqkv"], a["a2_wo"] = halves(g["L2_attn_qkv_w"].T), halves(g["L2_attn_proj_w"].T)
    a["f2_p1"], a["f2_p2"], a["f2_e1"], a["f2_e2"] = (g["L2_ffn_" + n] for n in ("moe0_W1", "moe0_W2", "A1_W", "A2_W"))
    a["f2_gw"] = halves(g["L2_ffn_G_W"].transpose(1, 0, 2))
    a["a3_wqkv"], a["a3_wo"] = halves(g["L3_attn_in_w"].T), halves(g["L3_attn_out_w"].T)
    swap = np.r_[8:16, 0:8]
    a["a3_wsp"] = halves(np.concatenate([g["L3_attn_sp_w"].T, g["L3_attn_sp_w"].T[:, swap]], 1))
    a["a3_qw"] = g["L3_attn_qw"].reshape(1, 1)
    a["f3_wr"], a["f3_bg"], a["f3_b2"], a["f3_down"] = halves(g["L3_ffn_Wg"]), g["L3_ffn_bg"][None], g["L3_ffn_b2"][None], g["L3_ffn_W2"]
    w1 = g["L3_ffn_W1"].reshape(NX, 2, HD, FF).transpose(0, 2, 1, 3)
    b1 = np.broadcast_to(g["L3_ffn_b1"][:, None, None], (NX, 1, 2, FF))
    a["f3_up"] = np.ascontiguousarray(np.concatenate([w1, b1], 1))
    more = [("s1_ld", halves(g["L1_attn_log_delta"])), ("f1_b1", tiles(g["L1_ffn_b1"])), ("f1_aw1", tiles(g["L1_ffn_alpha_w1"])),
            ("f1_b2", halves(g["L1_ffn_b2"])), ("f1_aw2", halves(g["L1_ffn_alpha_w2"])),
            ("f2_pb1", tiles(g["L2_ffn_moe0_b1"])), ("f2_pb2", halves(g["L2_ffn_moe0_b2"])),
            ("a3_spb", g["L3_attn_sp_b"][:, None]), ("a3_spbx", g["L3_attn_sp_b"][swap][:, None])]
    for e in range(5):
        more += [(f"f2_eb1{e}", tiles(g["L2_ffn_A1_b"][e])), (f"f2_eb2{e}", halves(g["L2_ffn_A2_b"][e]))]
    for n, bias, out in (("a2", g["L2_attn_qkv_b"], g["L2_attn_proj_b"]), ("a3", g["L3_attn_in_b"], g["L3_attn_out_b"])):
        more += [(f"{n}_{v}b", halves(bias[i * D:(i + 1) * D])) for i, v in enumerate("qkv")] + [(n + "_ob", halves(out))]
    parts = more + [("tok_b", halves(g["L0_tok_b"])), ("cls", halves(g["cls_tok"].reshape(D))),
             ("a0_qb", halves(b[0:D])), ("a0_kb", halves(b[D:2 * D])), ("a0_vb", halves(b[2 * D:])),
             ("n1w", halves(g["L0_ffn_norm1_w"])), ("n2w", halves(g["L0_ffn_norm2_w"])),
             ("a0_ob", halves(g["L0_attn_proj_b"])),
             ("a0_qn", np.tile(g["L0_attn_q_norm_w"], HH)[:, None]), ("a0_kn", np.tile(g["L0_attn_k_norm_w"], HH)[:, None])]
    a["vec"] = pack_columns(parts)
    cons = constants()
    at, con_at = 0, {}
    for n, v in cons:
        con_at[n] = (at, v.shape[1])
        at += v.shape[1]
    a["con"] = np.concatenate([v for _, v in cons], 1)
    return a, con_at, at


def kernel(**inputs):
    import concourse.bacc as _bacc
    from concourse.bass_utils import run_bass_kernel_spmd as _run

    nc = _bacc.Bacc("TRN2", target_bir_lowering=False, num_devices=1)
    arrays, con_at, con_n = prepare(inputs)
    arrays = {"in_" + n: a for n, a in arrays.items()}
    d = {n[3:]: nc.dram_tensor(n, a.shape, mybir.dt.from_np(a.dtype), kind="ExternalInput").ap() for n, a in arrays.items()}
    out = nc.dram_tensor("out", (HD, 2, T), F32, kind="ExternalOutput").ap()
    build(nc, d, out, con_at, con_n)
    r = _run(nc, [arrays], core_ids=[0])
    got = np.asarray(r.results[0]["out"])
    return np.ascontiguousarray(got.transpose(2, 1, 0)).reshape(B, N, D)
```
